# Optimizing a Trainium2 kernel written in Bass

```python
import numpy as np
import jax
import jax.numpy as jnp

def _softmax(x, axis=-1):
    return jax.nn.softmax(x, axis=axis)
def _gelu(x):
    return jax.nn.gelu(x, approximate=True)
def _silu(x):
    return jax.nn.silu(x)
def _sigmoid(x):
    return jax.nn.sigmoid(x)
def _layernorm(x, axis=-1, eps=1e-5):
    m = jnp.mean(x, axis=axis, keepdims=True)
    v = jnp.var(x, axis=axis, keepdims=True)
    return (x - m) / jnp.sqrt(v + eps)
def _scatter_add(tgt, idx, src, axis=0):
    return tgt.at[idx].add(src)
def _segment_sum(src, seg, n):
    return jax.ops.segment_sum(src, seg, n)

kernel_name = 'mk_conv_attn_hybrid_d2_conv_nchw128_1196d4'

def setup_inputs(seed: int = 0):
    np.random.seed(seed)
    _w = jnp.asarray
    def _rec_inputs():
        import jax
        import jax.numpy as jnp
        _gk = jax.random.key(seed)
        x = -0.0005207 + 1.001 * jax.random.normal(jax.random.fold_in(_gk, 1), (4, 128, 64, 64), jnp.float32)
        return x
    x = _rec_inputs()
    def _L0_conv_setup():
        import jax, jax.numpy as jnp
        import numpy as np
        K = 7
        DIL = 2
        PAD = 6
        G = 8
        key = jax.random.key(seed)
        ks = jax.random.split(key, 5)
        B, C, H, W = (4, 128, 64, 64)
        Cr = C // 4
        KKG = K * K * G
        return {'x': jax.random.normal(ks[0], (B, C, H, W), jnp.float32), 'w_reduce': jax.random.normal(ks[1], (Cr, C), jnp.float32) * 0.05, 'b_reduce': jax.random.normal(ks[2], (Cr,), jnp.float32) * 0.05, 'w_span': jax.random.normal(ks[3], (KKG, Cr), jnp.float32) * 0.05, 'b_span': jax.random.normal(ks[4], (KKG,), jnp.float32) * 0.05}
    _L0_conv_all = _L0_conv_setup()
    _L0_conv_in = {k: v for k, v in _L0_conv_all.items() if k in ('w_reduce', 'b_reduce', 'w_span', 'b_span', )}
    del _L0_conv_all

    def _L1_attn_setup():
        import jax, jax.numpy as jnp
        import numpy as np
        HEADS = 4
        WINDOW = 64
        NEG = -10000.0
        key = jax.random.key(seed)
        k1, k2, k3 = jax.random.split(key, 3)
        B, T, C = (8, 8192, 128)
        x = jax.random.normal(k1, (B, T, C), dtype=jnp.float32)
        w_qkv = jax.random.normal(k2, (3 * C, C), dtype=jnp.float32) * 0.02
        w_proj = jax.random.normal(k3, (C, C), dtype=jnp.float32) * 0.02
        b_proj = jnp.zeros((C,), dtype=jnp.float32)
        return {'x': x, 'w_qkv': w_qkv, 'w_proj': w_proj, 'b_proj': b_proj}
    _L1_attn_all = _L1_attn_setup()
    _L1_attn_in = {k: v for k, v in _L1_attn_all.items() if k in ('w_qkv', 'w_proj', 'b_proj', )}
    del _L1_attn_all

    def _L1_ffn_setup():
        import jax, jax.numpy as jnp
        import numpy as np
        PADDED_SL = 8192
        TEMPERATURE = 1.0
        SIGMA_POW = 0.25

        def _stu_conv(phi, u, n):
            b, sl, d = u.shape
            sgn = jnp.where(jnp.arange(sl) % 2 == 0, 1.0, -1.0).astype(u.dtype)
            sgn3 = sgn[None, :, None]
            Vf = jnp.fft.rfft(phi, n=n, axis=0)
            Uf_p = jnp.fft.rfft(u, n=n, axis=1)
            Uf_m = jnp.fft.rfft(u * sgn3, n=n, axis=1)
            U_plus = jnp.fft.irfft(Vf[None, :, :, None] * Uf_p[:, :, None, :], n=n, axis=1)[:, :sl]
            U_minus = jnp.fft.irfft(Vf[None, :, :, None] * Uf_m[:, :, None, :], n=n, axis=1)[:, :sl]
            U_minus = U_minus * sgn[None, :, None, None]
            return (U_plus, U_minus)

        def _compute_spectral(u, sigma, phi, Mpp, Mpm):
            U_plus, U_minus = _stu_conv(phi, u, PADDED_SL)
            s = sigma ** SIGMA_POW
            out = jnp.einsum('btkd,k,kde->bte', U_plus, s, Mpp)
            out = out + jnp.einsum('btkd,k,kde->bte', U_minus, s, Mpm)
            return out

        def _compute_ar_u(Mu, u):
            sl = u.shape[1]
            out = jnp.zeros(u.shape[:2] + (Mu.shape[-1],), dtype=u.dtype)
            for i in range(Mu.shape[0]):
                ui = jnp.pad(u, ((0, 0), (i, 0), (0, 0)))[:, :sl]
                out = out + jnp.einsum('btd,de->bte', ui, Mu[i])
            return out

        def _stu(u, sigma, phi, Mu, Mpp, Mpm):
            return _compute_spectral(u, sigma, phi, Mpp, Mpm) + _compute_ar_u(Mu, u)
        key = jax.random.key(seed)
        ks = jax.random.split(key, 8)
        b, sl, d, K, k_u = (2, 4096, 128, 16, 3)
        x = jax.random.normal(ks[0], (b, sl, d), dtype=jnp.float32)
        sigma = jax.random.uniform(ks[1], (K,), dtype=jnp.float32, minval=0.001, maxval=1.0)
        phi = jax.random.normal(ks[2], (sl, K), dtype=jnp.float32) / np.sqrt(sl)
        M_u = jax.random.normal(ks[3], (4, k_u, d, d), dtype=jnp.float32) * 0.02
        M_phi_plus = jax.random.normal(ks[4], (4, K, d, d), dtype=jnp.float32) * 0.02
        M_phi_minus = jax.random.normal(ks[5], (4, K, d, d), dtype=jnp.float32) * 0.02
        log_weights = jnp.ones((4,), dtype=jnp.float32)
        u01 = jax.random.uniform(ks[6], (4,), dtype=jnp.float32, minval=1e-06, maxval=1.0 - 1e-06)
        gumbel = -jnp.log(-jnp.log(u01))
        return {'x': x, 'sigma': sigma, 'phi': phi, 'M_u': M_u, 'M_phi_plus': M_phi_plus, 'M_phi_minus': M_phi_minus, 'log_weights': log_weights, 'gumbel': gumbel}
    _L1_ffn_all = _L1_ffn_setup()
    _L1_ffn_in = {k: v for k, v in _L1_ffn_all.items() if k in ('sigma', 'phi', 'M_u', 'M_phi_plus', 'M_phi_minus', 'log_weights', 'gumbel', )}
    del _L1_ffn_all

    return {
        "x": x,
        "L0_conv_w_reduce": _L0_conv_in["w_reduce"],
        "L0_conv_b_reduce": _L0_conv_in["b_reduce"],
        "L0_conv_w_span": _L0_conv_in["w_span"],
        "L0_conv_b_span": _L0_conv_in["b_span"],
        "L1_attn_w_qkv": _L1_attn_in["w_qkv"],
        "L1_attn_w_proj": _L1_attn_in["w_proj"],
        "L1_attn_b_proj": _L1_attn_in["b_proj"],
        "L1_ffn_sigma": _L1_ffn_in["sigma"],
        "L1_ffn_phi": _L1_ffn_in["phi"],
        "L1_ffn_M_u": _L1_ffn_in["M_u"],
        "L1_ffn_M_phi_plus": _L1_ffn_in["M_phi_plus"],
        "L1_ffn_M_phi_minus": _L1_ffn_in["M_phi_minus"],
        "L1_ffn_log_weights": _L1_ffn_in["log_weights"],
        "L1_ffn_gumbel": _L1_ffn_in["gumbel"],
    }

def reference(x, L0_conv_w_reduce, L0_conv_b_reduce, L0_conv_w_span, L0_conv_b_span, L1_attn_w_qkv, L1_attn_w_proj, L1_attn_b_proj, L1_ffn_sigma, L1_ffn_phi, L1_ffn_M_u, L1_ffn_M_phi_plus, L1_ffn_M_phi_minus, L1_ffn_log_weights, L1_ffn_gumbel):
    import jax
    import jax.numpy as jnp
    def _L0_conv_ref(x, w_reduce, b_reduce, w_span, b_span):
        import jax, jax.numpy as jnp
        import numpy as np
        K = 7
        DIL = 2
        PAD = 6
        G = 8
        B, C, H, W = x.shape
        Cg = C // G
        red = jnp.einsum('bchw,oc->bohw', x, w_reduce) + b_reduce[None, :, None, None]
        ker = jnp.einsum('bohw,ko->bkhw', red, w_span) + b_span[None, :, None, None]
        ker = ker.reshape(B, G, K * K, H, W)
        xp = jnp.pad(x, ((0, 0), (0, 0), (PAD, PAD), (PAD, PAD)))
        patches = jnp.stack([xp[:, :, i * DIL:i * DIL + H, j * DIL:j * DIL + W] for i in range(K) for j in range(K)], axis=2)
        patches = patches.reshape(B, G, Cg, K * K, H, W)
        out = jnp.einsum('bgckhw,bgkhw->bgchw', patches, ker)
        return out.reshape(B, C, H, W)

    def _L1_attn_ref(x, w_qkv, w_proj, b_proj):
        import jax, jax.numpy as jnp
        import numpy as np
        HEADS = 4
        WINDOW = 64
        NEG = -10000.0
        B, T, C = x.shape
        H, W = (HEADS, WINDOW)
        hd = C // H
        scale = hd ** (-0.5)
        nw = T // W
        xw = x.reshape(B * nw, W, C)
        qkv = xw @ w_qkv.T
        qkv = qkv.reshape(B * nw, W, 3, H, hd)
        q = qkv[:, :, 0].transpose(0, 2, 1, 3)
        k = qkv[:, :, 1].transpose(0, 2, 1, 3)
        v = qkv[:, :, 2].transpose(0, 2, 1, 3)
        attn = jnp.einsum('bhqd,bhkd->bhqk', q, k) * scale
        causal = jnp.tril(jnp.ones((W, W), dtype=bool))
        attn = jnp.where(causal, attn, NEG)
        attn = jax.nn.softmax(attn, axis=-1)
        out = jnp.einsum('bhqk,bhkd->bhqd', attn, v)
        out = out.transpose(0, 2, 1, 3).reshape(B * nw, W, C)
        out = out @ w_proj.T + b_proj
        return out.reshape(B, T, C)

    def _L1_ffn_ref(x, sigma, phi, M_u, M_phi_plus, M_phi_minus, log_weights, gumbel):
        import jax, jax.numpy as jnp
        import numpy as np
        PADDED_SL = 8192
        TEMPERATURE = 1.0
        SIGMA_POW = 0.25

        def _stu_conv(phi, u, n):
            b, sl, d = u.shape
            sgn = jnp.where(jnp.arange(sl) % 2 == 0, 1.0, -1.0).astype(u.dtype)
            sgn3 = sgn[None, :, None]
            Vf = jnp.fft.rfft(phi, n=n, axis=0)
            Uf_p = jnp.fft.rfft(u, n=n, axis=1)
            Uf_m = jnp.fft.rfft(u * sgn3, n=n, axis=1)
            U_plus = jnp.fft.irfft(Vf[None, :, :, None] * Uf_p[:, :, None, :], n=n, axis=1)[:, :sl]
            U_minus = jnp.fft.irfft(Vf[None, :, :, None] * Uf_m[:, :, None, :], n=n, axis=1)[:, :sl]
            U_minus = U_minus * sgn[None, :, None, None]
            return (U_plus, U_minus)

        def _compute_spectral(u, sigma, phi, Mpp, Mpm):
            U_plus, U_minus = _stu_conv(phi, u, PADDED_SL)
            s = sigma ** SIGMA_POW
            out = jnp.einsum('btkd,k,kde->bte', U_plus, s, Mpp)
            out = out + jnp.einsum('btkd,k,kde->bte', U_minus, s, Mpm)
            return out

        def _compute_ar_u(Mu, u):
            sl = u.shape[1]
            out = jnp.zeros(u.shape[:2] + (Mu.shape[-1],), dtype=u.dtype)
            for i in range(Mu.shape[0]):
                ui = jnp.pad(u, ((0, 0), (i, 0), (0, 0)))[:, :sl]
                out = out + jnp.einsum('btd,de->bte', ui, Mu[i])
            return out

        def _stu(u, sigma, phi, Mu, Mpp, Mpm):
            return _compute_spectral(u, sigma, phi, Mpp, Mpm) + _compute_ar_u(Mu, u)
        T = x.shape[1]
        outs = []
        for i, frac in enumerate((1, 2, 4, 8)):
            xi = x[:, :T // frac]
            si = _stu(xi, sigma, phi, M_u[i], M_phi_plus[i], M_phi_minus[i])
            si = jnp.pad(si, ((0, 0), (0, T - si.shape[1]), (0, 0)))
            outs.append(si)
        y_soft = jax.nn.softmax((log_weights + gumbel) / TEMPERATURE)
        y_hard = jax.nn.one_hot(jnp.argmax(y_soft), 4, dtype=y_soft.dtype)
        weights = y_hard - jax.lax.stop_gradient(y_soft) + y_soft
        stacked = jnp.stack(outs, axis=-1)
        return jnp.sum(stacked * weights, axis=-1)

    def _gn(v, G=32, eps=1e-5):
        B_, C_, H_, W_ = v.shape
        g = v.reshape(B_, G, C_ // G, H_, W_)
        m = jnp.mean(g, axis=(2, 3, 4), keepdims=True)
        s = jnp.var(g, axis=(2, 3, 4), keepdims=True)
        return ((g - m) / jnp.sqrt(s + eps)).reshape(v.shape)

    def _ln_c(v, eps=1e-6):
        m = jnp.mean(v, axis=1, keepdims=True)
        s = jnp.var(v, axis=1, keepdims=True)
        return (v - m) / jnp.sqrt(s + eps)

    def _ln_t(v, eps=1e-5):
        m = jnp.mean(v, axis=-1, keepdims=True)
        s = jnp.var(v, axis=-1, keepdims=True)
        return (v - m) / jnp.sqrt(s + eps)

    def _to_tokens(v):
        B_, C_, H_, W_ = v.shape
        return v.reshape(B_, C_, H_ * W_).transpose(0, 2, 1)
    def _from_tokens(t, like):
        B_, C_, H_, W_ = like.shape
        return t.transpose(0, 2, 1).reshape(B_, C_, H_, W_)

    x = x + _L0_conv_ref(_gn(x), L0_conv_w_reduce, L0_conv_b_reduce, L0_conv_w_span, L0_conv_b_span)
    t = _to_tokens(x)
    t = t + _L1_attn_ref(_ln_t(t), L1_attn_w_qkv, L1_attn_w_proj, L1_attn_b_proj)
    t = t + _L1_ffn_ref(_ln_t(t), L1_ffn_sigma, L1_ffn_phi, L1_ffn_M_u, L1_ffn_M_phi_plus, L1_ffn_M_phi_minus, L1_ffn_log_weights, L1_ffn_gumbel)
    x = _from_tokens(t, x)
    return x


_drawn_inputs = setup_inputs


def setup_inputs(seed=0):
    import zlib

    import numpy as np

    out = dict(_drawn_inputs(seed))
    spreads = {'L1_attn_b_proj': (0.0, 0.1), 'L1_ffn_log_weights': (1.0, 0.2)}
    factors = {'L1_attn_w_qkv': 6.061, 'L1_attn_w_proj': 6.053}
    for name, (base, spread) in spreads.items():
        noise = np.random.default_rng([zlib.crc32(name.encode()), seed]).standard_normal(out[name].shape)
        drawn = base * np.exp(spread * noise) if base else spread * noise
        out[name] = jnp.asarray(drawn.astype(out[name].dtype))
    for name, factor in factors.items():
        out[name] = (out[name] * factor).astype(out[name].dtype)
    return out
```

```python
from contextlib import ExitStack

import concourse.bass as bass
from concourse import mybir

F32 = mybir.dt.float32
F16 = mybir.dt.float16
ALU = mybir.AluOpType
ACT = mybir.ActivationFunctionType
AX = mybir.AxisListType

P = 128
B = 4
IMG = 64
T = IMG * IMG
CH = 512
NCH = T // CH
ROWS = CH // IMG

KS = 7
DIL = 2
PAD = 6
GC = 8
CG = P // GC
CR = 32
TAPS = KS * KS
PW = IMG + 2 * PAD
POOL_TAPS = 5
PARTS = POOL_TAPS + KS * (KS - POOL_TAPS)
GN_CH = 4
GN_EPS = 1e-5
LN_EPS = 1e-5

HEADS = 4
HD = P // HEADS
WIN = 64
NW = CH // WIN
NPAIR = NW // 2
NEG = -10000.0

NK = 16
NE = 4
AR = 3
HALF = T // 2
NBLK = HALF // P
NGRP = HALF // CH
PH_SCALE = 4096.0
U_SCALE = 256.0
LINE = P + HALF
SW = HALF + 1


def program(nc, x, w_reduce, b_reduce, w_span, b_span, w_qkv, w_proj, b_proj,
            sigma, phi, m_u, m_plus, m_minus, log_weights, gumbel, out):
    x_v = x.rearrange("b c h w -> c b (h w)")
    out_v = out.rearrange("b c h w -> c b (h w)")
    lines = nc.dram_tensor("filter_lines", [NK, 4, LINE], F16, kind="Internal").ap()

    top = ExitStack()
    with top:
        def sb(name, shape, dt=F32, on=top):
            return on.enter_context(nc.sbuf_tensor(name, shape, dt))

        def ps(name, shape, on):
            return on.enter_context(nc.psum_tensor(name, shape, F32))

        def sem(name):
            return top.enter_context(nc.semaphore(name))

        X = sb("X", [P, B, T])
        ident = sb("ident", [P, P])
        flip = sb("flip", [P, P])
        averager = sb("averager", [P, P])
        gn_avg = sb("gn_avg", [P, P])
        mean_col = sb("mean_col", [P, NCH, NCH])
        spread = sb("spread", [NCH, NCH, P])
        eps_col = sb("eps_col", [P, 1])
        one_row = sb("one_row", [1, P])
        wqkvT = sb("wqkvT", [P, 3, P])
        wprojT = sb("wprojT", [P, P])
        bproj = sb("bproj", [P, 1])
        mix = sb("mix", [P, NE, NK])
        gate = sb("gate", [P, NE])

        st0 = ExitStack()
        with st0:
            wq_raw = sb("wq_raw", [P, 3, P], on=st0)
            wp_raw = sb("wp_raw", [P, P], on=st0)
            gate_in = sb("gate_in", [P, 2, NE], on=st0)
            gate_t = sb("gate_t", [P, 8, NE], on=st0)
            gate_s = sb("gate_s", [P, 8], on=st0)
            sig_in = sb("sig_in", [P, 3, NK], on=st0)
            phi_in = sb("phi_in", [P, 32, NK], on=st0)
            phi_n = sb("phi_n", [P, 32, NK], on=st0)
            phi_m = sb("phi_m", [P, 6], on=st0)
            line_sb = sb("line_sb", [NK, 4, LINE], F16, on=st0)
            psA = ps("psA", [P, 4, P], st0)
            psB = ps("psB", [P, P], st0)
            psP = ps("psP", [P, 4, CH], st0)

            weights_in = sem("weights_in")
            gate_ld = sem("gate_ld")
            phi_ld = sem("phi_ld")
            consts = sem("consts")
            ident0 = sem("ident0")
            wT_ready = sem("wT_ready")
            phi_rowmax = sem("phi_rowmax")
            phi_maxT = sem("phi_maxT")
            phi_max = sem("phi_max")
            phi_bc = sem("phi_bc")
            phi_scaled = sem("phi_scaled")
            phi_T = sem("phi_T")
            phi_hi = sem("phi_hi")
            phi_lo = sem("phi_lo")
            line_zero = sem("line_zero")
            lines_out = sem("lines_out")
            v0 = sem("v0")
            expd = sem("expd")
            sigd = sem("sigd")

            with nc.Block() as block:
                @block.sync
                def _(sp):
                    sp.dma_start(phi_in[:], phi.rearrange("(a l) k -> a l k", a=P)).then_inc(phi_ld, 16)
                    sp.dma_start(wq_raw[:], w_qkv.rearrange("(t p) c -> p t c", p=P)).then_inc(weights_in, 16)
                    sp.dma_start(wp_raw[:], w_proj).then_inc(weights_in, 16)
                    sp.dma_start(gate_in[:, 0], bass.AP(log_weights.tensor, 0, [[0, P], [1, NE]])).then_inc(gate_ld, 16)
                    sp.dma_start(gate_in[:, 1], bass.AP(gumbel.tensor, 0, [[0, P], [1, NE]])).then_inc(gate_ld, 16)
                    sp.dma_start(sig_in[:, 0], bass.AP(sigma.tensor, 0, [[0, P], [1, NK]])).then_inc(gate_ld, 16)
                    sp.dma_start(bproj[:], b_proj.rearrange("(c a) -> c a", a=1)).then_inc(weights_in, 16)
                    sp.wait_ge(phi_hi, 8)
                    sp.wait_ge(phi_lo, 8)
                    sp.dma_start(lines, line_sb[:]).then_inc(lines_out, 16)
                    sp.wait_ge(lines_out, 16)
                    sp.wait_ge(weights_in, 48)
                    sp.wait_ge(gate_ld, 48)

                @block.gpsimd
                def _(pool):
                    nc.gpsimd.memset(ident[:], 0.0).then_inc(ident0, 1)
                    nc.gpsimd.memset(gn_avg[:], 1.0 / GN_CH).then_inc(ident0, 1)
                    nc.gpsimd.memset(mean_col[:], 0.0).then_inc(ident0, 1)
                    nc.gpsimd.memset(spread[:], 0.0).then_inc(ident0, 1)
                    nc.gpsimd.memset(flip[:], 0.0).then_inc(ident0, 1)
                    pool.wait_ge(ident0, 5)
                    nc.gpsimd.affine_select(out=ident[:], in_=ident[:], compare_op=ALU.not_equal, fill=1.0,
                                            base=0, pattern=[[-1, P]], channel_multiplier=1).then_inc(consts, 1)
                    nc.gpsimd.affine_select(out=flip[:], in_=flip[:], compare_op=ALU.not_equal, fill=1.0,
                                            base=1 - P, pattern=[[1, P]], channel_multiplier=1).then_inc(consts, 1)
                    gv = gn_avg[:].rearrange("p (g r) -> p g r", r=GN_CH)
                    nc.gpsimd.affine_select(out=gv, in_=gv, compare_op=ALU.is_ge, fill=0.0, base=0,
                                            pattern=[[-GN_CH, P // GN_CH], [0, GN_CH]],
                                            channel_multiplier=1).then_inc(ident0, 1)
                    pool.wait_ge(ident0, 6)
                    nc.gpsimd.affine_select(out=gv, in_=gv, compare_op=ALU.is_ge, fill=0.0, base=GN_CH - 1,
                                            pattern=[[GN_CH, P // GN_CH], [0, GN_CH]],
                                            channel_multiplier=-1).then_inc(consts, 1)
                    nc.gpsimd.affine_select(out=mean_col[:], in_=mean_col[:], compare_op=ALU.not_equal,
                                            fill=1.0 / P, base=0, pattern=[[1, NCH], [-1, NCH]],
                                            channel_multiplier=0).then_inc(consts, 1)
                    nc.gpsimd.affine_select(out=spread[:], in_=spread[:], compare_op=ALU.not_equal, fill=1.0,
                                            base=0, pattern=[[-1, NCH], [0, P]], channel_multiplier=1).then_inc(consts, 1)
                    nc.gpsimd.memset(averager[:], 1.0 / P).then_inc(consts, 1)
                    nc.gpsimd.memset(one_row[:], 1.0).then_inc(consts, 1)
                    nc.gpsimd.memset(eps_col[:], LN_EPS).then_inc(consts, 1)
                    nc.gpsimd.memset(line_sb[:, :, HALF:], 0.0).then_inc(consts, 1)

                @block.tensor
                def _(pe):
                    pe.wait_ge(consts, 9)
                    pe.wait_ge(weights_in, 48)
                    for t in range(3):
                        nc.tensor.transpose(psA[:, t], wq_raw[:, t], ident[:])
                    nc.tensor.transpose(psA[:, 3], wp_raw[:], ident[:]).then_inc(wT_ready, 1)
                    pe.wait_ge(phi_rowmax, 1)
                    nc.tensor.transpose(psB[0:1, :], phi_m[:, 0:1], ident[:]).then_inc(phi_maxT, 1)
                    pe.wait_ge(phi_max, 1)
                    nc.tensor.matmul(psB[:, 0:1], one_row[:], phi_m[0:1, 1:2], start=True, stop=True).then_inc(phi_bc, 1)
                    pe.wait_ge(phi_scaled, 1)
                    for r in range(8):
                        if r >= 4:
                            pe.wait_ge(phi_lo, r - 3)
                        for j in range(4):
                            slot = (1 - j // 2) * 2 + j % 2
                            last = nc.tensor.matmul(psP[0:NK, r % 4, slot * P:(slot + 1) * P], phi_n[:, 4 * r + j],
                                                    flip[:], start=True, stop=True)
                        last.then_inc(phi_T, 1)

                @block.scalar
                def _(act):
                    act.wait_ge(v0, 4)
                    nc.scalar.activation(gate_t[:, 2], gate_t[:, 1], ACT.Exp).then_inc(expd, 1)
                    act.wait_ge(gate_ld, 48)
                    nc.scalar.activation(sig_in[:, 1], sig_in[:, 0], ACT.Sqrt).then_inc(sigd, 1)
                    act.wait_ge(sigd, 1)
                    nc.scalar.activation(sig_in[:, 2], sig_in[:, 1], ACT.Sqrt).then_inc(sigd, 1)
                    act.wait_ge(consts, 9)
                    for r in range(8):
                        act.wait_ge(phi_T, r + 1)
                        for q in range(2):
                            src = psP[0:NK, r % 4, :].rearrange("p (j q a) -> p q j a", q=2, j=2)[:, q]
                            dst = line_sb[:, 2 * q, 0:HALF].rearrange("p (a l) -> p l a", l=16)[:, 14 - 2 * r:16 - 2 * r]
                            last = nc.scalar.activation(dst, src, ACT.Copy)
                        last.then_inc(phi_hi, 1)

                @block.vector
                def _(dve):
                    n = [0]

                    def link(ins):
                        n[0] += 1
                        ins.then_inc(v0, 1)
                        dve.wait_ge(v0, n[0])

                    dve.wait_ge(gate_ld, 48)
                    link(nc.vector.tensor_tensor(gate_t[:, 0], gate_in[:, 0], gate_in[:, 1], ALU.add))
                    link(nc.vector.tensor_reduce(gate_s[:, 0:1], gate_t[:, 0], AX.X, ALU.max))
                    link(nc.vector.tensor_scalar(gate_t[:, 1], gate_t[:, 0], gate_s[:, 0:1], None, ALU.subtract))
                    link(nc.vector.memset(gate_s[:, 4:5], 1.0))
                    dve.wait_ge(expd, 1)
                    link(nc.vector.tensor_reduce(gate_s[:, 1:2], gate_t[:, 2], AX.X, ALU.add))
                    link(nc.vector.reciprocal(gate_s[:, 2:3], gate_s[:, 1:2]))
                    link(nc.vector.tensor_scalar(gate_t[:, 3], gate_t[:, 2], gate_s[:, 2:3], None, ALU.mult))
                    link(nc.vector.tensor_reduce(gate_s[:, 3:4], gate_t[:, 3], AX.X, ALU.max))
                    link(nc.vector.tensor_scalar(gate_t[:, 4], gate_t[:, 3], gate_s[:, 3:4], None, ALU.is_equal))
                    for i in range(NE):
                        link(nc.vector.tensor_tensor(gate_t[:, 5, i:i + 1], gate_t[:, 4, i:i + 1], gate_s[:, 4:5], ALU.mult))
                        link(nc.vector.tensor_tensor(gate_s[:, 4:5], gate_s[:, 4:5], gate_t[:, 5, i:i + 1], ALU.subtract))
                    link(nc.vector.tensor_tensor(gate_t[:, 6], gate_t[:, 5], gate_t[:, 3], ALU.subtract))
                    link(nc.vector.tensor_tensor(gate[:], gate_t[:, 6], gate_t[:, 3], ALU.add))
                    dve.wait_ge(phi_ld, 16)
                    nc.vector.tensor_reduce(phi_m[:, 0:1], phi_in[:], AX.XY, ALU.max,
                                            apply_absolute_value=True).then_inc(phi_rowmax, 1)
                    dve.wait_ge(phi_maxT, 1)
                    nc.vector.tensor_reduce(phi_m[0:1, 1:2], psB[0:1, :], AX.X, ALU.max).then_inc(phi_max, 1)
                    dve.wait_ge(phi_bc, 1)
                    link(nc.vector.tensor_scalar(phi_m[:, 2:3], psB[:, 0:1], 1e-30, None, ALU.max))
                    link(nc.vector.reciprocal(phi_m[:, 3:4], phi_m[:, 2:3]))
                    nc.vector.tensor_scalar(phi_n[:], phi_in[:], phi_m[:, 3:4], PH_SCALE, ALU.mult,
                                            ALU.mult).then_inc(phi_scaled, 1)
                    link(nc.vector.tensor_scalar(phi_m[:, 4:5], phi_m[:, 2:3], 1.0 / (PH_SCALE * U_SCALE), None, ALU.mult))
                    dve.wait_ge(sigd, 2)
                    for i in range(NE):
                        link(nc.vector.tensor_scalar(mix[:, i], sig_in[:, 2], gate[:, i:i + 1], phi_m[:, 4:5],
                                                     ALU.mult, ALU.mult))
                    for r in range(8):
                        dve.wait_ge(phi_hi, r + 1)
                        for q in range(2):
                            src = psP[0:NK, r % 4, :].rearrange("p (j q a) -> p q j a", q=2, j=2)[:, q]
                            hi = line_sb[:, 2 * q, 0:HALF].rearrange("p (a l) -> p l a", l=16)[:, 14 - 2 * r:16 - 2 * r]
                            lo = line_sb[:, 2 * q + 1, 0:HALF].rearrange("p (a l) -> p l a", l=16)[:, 14 - 2 * r:16 - 2 * r]
                            last = nc.vector.tensor_tensor(lo, src, hi, ALU.subtract)
                        last.then_inc(phi_lo, 1)
                    dve.wait_ge(wT_ready, 1)
                    nc.vector.tensor_copy(wqkvT[:], psA[:, 0:3])
                    link(nc.vector.tensor_copy(wprojT[:], psA[:, 3]))

        st1 = ExitStack()
        with st1:
            xpad = sb("xpad", [P, PW, PW], on=st1)
            red = sb("red", [P, T], on=st1)
            tapw = sb("tapw", [P, TAPS, P], on=st1)
            wsT = sb("wsT", [CR + 1, GC * TAPS], on=st1)
            ws_raw = sb("ws_raw", [98, 4, CR], on=st1)
            wrT = sb("wrT", [P, CR], on=st1)
            wr_raw = sb("wr_raw", [CR, P], on=st1)
            bred = sb("bred", [CR, 1], on=st1)
            prod = sb("prod", [P, 2, POOL_TAPS, ROWS, IMG], on=st1)
            parts = sb("parts", [P, PARTS, ROWS, IMG], on=st1)
            conv = sb("conv", [P, CH], on=st1)
            bn = sb("bn", [P, B, NCH, 6], on=st1)
            cstat = sb("cstat", [P, B, 2], on=st1)
            dstat = sb("dstat", [P, 6, B], on=st1)
            taps_ps = ps("taps_ps", [P, KS, CH], st1)
            psR = ps("psR", [P, CH], st1)

            x_in = sem("x_in")
            cw_in = sem("cw_in")
            wr_T = sem("wr_T")
            ws_T = sem("ws_T")
            wr_ready = sem("wr_ready")
            tap_ready = sem("tap_ready")
            tap_zero = sem("tap_zero")
            gn_a = sem("gn_a")
            gn_b = sem("gn_b")
            v1 = sem("v1")
            frame = sem("frame")
            gmean = sem("gmean")
            gvar = sem("gvar")
            gstd = sem("gstd")
            gnorm = sem("gnorm")
            xpad_ready = sem("xpad_ready")
            red_mm = sem("red_mm")
            red_ready = sem("red_ready")
            kern = sem("kern")
            mul = sem("mul")
            pool_added = sem("pool_added")
            vsum = sem("vsum")

            with nc.Block() as block:
                @block.sync
                def _(sp):
                    for b in range(B):
                        sp.dma_start(X[:, b], x_v[:, b]).then_inc(x_in, 16)
                    sp.dma_start(ws_raw[:], w_span.rearrange("(t r) o -> r t o", r=98)).then_inc(cw_in, 16)
                    sp.dma_start(wr_raw[:], w_reduce).then_inc(cw_in, 16)
                    sp.dma_start(bred[:], b_reduce.rearrange("(c a) -> c a", a=1)).then_inc(cw_in, 16)
                    sp.dma_start(wsT[CR:CR + 1, :], b_span.rearrange("(a k) -> a k", a=1)).then_inc(cw_in, 16)

                @block.gpsimd
                def _(pool):
                    nc.gpsimd.memset(xpad[:], 0.0).then_inc(frame, 1)
                    nc.gpsimd.memset(red[:], 0.0).then_inc(frame, 1)
                    nc.gpsimd.memset(tapw[:], 0.0).then_inc(tap_zero, 1)
                    pool.wait_ge(frame, 2)
                    pool.wait_ge(tap_zero, 1)
                    nc.gpsimd.memset(red[CR:CR + 1, :], 1.0).then_inc(frame, 1)
                    for b in range(B):
                        with pool.Fori(0, NCH, 1) as c:
                            for i in range(1, KS):
                                pool.wait_ge(mul, KS + ((b * NCH + c) * KS + i) * KS + POOL_TAPS)
                                if i == 1:
                                    pool.wait_ge(vsum, 1 + (b * NCH + c) * 2)
                                else:
                                    pool.wait_ge(pool_added, (b * NCH + c) * (KS - 1) + i - 1)
                                sums = parts[:, 0:POOL_TAPS]
                                nc.gpsimd.tensor_tensor(sums, prod[:, 0] if i == 1 else sums, prod[:, i % 2],
                                                        ALU.add).then_inc(pool_added, 1)

                @block.tensor
                def _(pe):
                    pe.wait_ge(cw_in, 64)
                    nc.tensor.transpose(psR[:, 0:CR], wr_raw[:], ident[0:CR, 0:CR]).then_inc(wr_T, 1)
                    for t in range(4):
                        last = nc.tensor.transpose(taps_ps[0:CR, 0, t * 98:(t + 1) * 98], ws_raw[:, t], ident[0:98, 0:98])
                    last.then_inc(ws_T, 1)
                    pe.wait_ge(gn_a, 1)
                    nc.tensor.matmul(taps_ps[:, 1, 0:B], gn_avg[:], dstat[:, 0], start=True, stop=True).then_inc(gmean, 1)
                    pe.wait_ge(gn_b, 1)
                    nc.tensor.matmul(taps_ps[:, 2, 0:B], gn_avg[:], dstat[:, 2], start=True, stop=True).then_inc(gvar, 1)
                    pe.wait_ge(wr_ready, 1)
                    pe.wait_ge(tap_ready, 1)
                    pe.wait_ge(gnorm, 1)
                    for b in range(B):
                        pe.wait_ge(xpad_ready, b + 1)
                        for c in range(NCH):
                            if b or c:
                                pe.wait_ge(red_ready, b * NCH + c)
                            nc.tensor.matmul(psR[0:CR, :], wrT[:],
                                             xpad[:, PAD + c * ROWS:PAD + (c + 1) * ROWS, PAD:PAD + IMG],
                                             start=True, stop=True).then_inc(red_mm, 1)
                        pe.wait_ge(red_ready, (b + 1) * NCH)
                        with pe.Fori(0, NCH, 1) as c:
                            for i in range(KS):
                                for j in range(KS):
                                    pe.wait_ge(mul, ((b * NCH + c) * KS + i) * KS + j + 1)
                                    nc.tensor.matmul(taps_ps[:, j], tapw[:, i * KS + j], red[:, bass.ts(c, CH)],
                                                     start=True, stop=True).then_inc(kern, 1)

                @block.scalar
                def _(act):
                    act.wait_ge(gn_b, 2)
                    nc.scalar.activation(dstat[:, 3], dstat[:, 5], ACT.Sqrt, bias=eps_col[:]).then_inc(gstd, 1)
                    act.wait_ge(frame, 3)
                    act.wait_ge(gnorm, 1)
                    act.wait_ge(x_in, 16 * B)
                    for b in range(B):
                        if b:
                            act.wait_ge(mul, KS + b * NCH * TAPS)
                        nc.scalar.activation(xpad[:, PAD:PAD + IMG, PAD:PAD + IMG],
                                             X[:, b].rearrange("p (h w) -> p h w", w=IMG), ACT.Identity,
                                             bias=dstat[:, 4, b:b + 1], scale=dstat[:, 2, b:b + 1]).then_inc(xpad_ready, 1)
                        if b:
                            act.wait_ge(kern, b * NCH * TAPS)
                        for c in range(NCH):
                            act.wait_ge(red_mm, b * NCH + c + 1)
                            nc.scalar.activation(red[0:CR, c * CH:(c + 1) * CH], psR[0:CR, :], ACT.Identity,
                                                 bias=bred[:]).then_inc(red_ready, 1)

                @block.vector
                def _(dve):
                    dve.sem_inc(mul, KS)
                    dve.sem_inc(vsum, 1)
                    n = [0]

                    def link(ins):
                        n[0] += 1
                        ins.then_inc(v1, 1)
                        dve.wait_ge(v1, n[0])

                    dve.wait_ge(x_in, 16 * B)
                    for b in range(B):
                        for c in range(NCH):
                            last = nc.vector.bn_stats(bn[:, b, c], X[:, b, c * CH:(c + 1) * CH])
                    link(last)
                    for b in range(B):
                        last = nc.vector.bn_aggr(cstat[:, b], bn[:, b])
                    link(last)
                    nc.vector.tensor_copy(dstat[:, 0], cstat[:, :, 0]).then_inc(gn_a, 1)
                    dve.wait_ge(gmean, 1)
                    link(nc.vector.tensor_copy(dstat[:, 1], taps_ps[:, 1, 0:B]))
                    link(nc.vector.tensor_tensor(dstat[:, 3], dstat[:, 0], dstat[:, 1], ALU.subtract))
                    link(nc.vector.tensor_tensor(dstat[:, 4], dstat[:, 3], dstat[:, 3], ALU.mult))
                    nc.vector.tensor_tensor(dstat[:, 2], dstat[:, 4], cstat[:, :, 1], ALU.add).then_inc(gn_b, 1)
                    dve.wait_ge(gvar, 1)
                    nc.vector.tensor_copy(dstat[:, 5], taps_ps[:, 2, 0:B]).then_inc(gn_b, 1)
                    dve.wait_ge(gstd, 1)
                    link(nc.vector.reciprocal(dstat[:, 2], dstat[:, 3]))
                    nc.vector.scalar_tensor_tensor(out=dstat[:, 4], in0=dstat[:, 1], scalar=-1.0, in1=dstat[:, 2],
                                                   op0=ALU.mult, op1=ALU.mult).then_inc(gnorm, 1)
                    dve.wait_ge(wr_T, 1)
                    nc.vector.tensor_copy(wrT[:], psR[:, 0:CR]).then_inc(wr_ready, 1)
                    dve.wait_ge(ws_T, 1)
                    link(nc.vector.tensor_copy(wsT[0:CR, :], taps_ps[0:CR, 0, 0:GC * TAPS]))
                    dve.wait_ge(tap_zero, 1)
                    for k in range(TAPS):
                        src = wsT[:].rearrange("p (g k) -> p g k", k=TAPS)[:, :, k:k + 1]
                        last = nc.vector.tensor_copy(tapw[0:CR + 1, k].rearrange("p (g c) -> p g c", c=CG),
                                                     src.to_broadcast([CR + 1, GC, CG]))
                    last.then_inc(tap_ready, 1)

                    def multiply(b, c, i, j):
                        dve.wait_ge(kern, ((b * NCH + c) * KS + i) * KS + j + 1)
                        if j < POOL_TAPS:
                            dst = prod[:, i % 2, j]
                        else:
                            dst = parts[:, POOL_TAPS + i * (KS - POOL_TAPS) + j - POOL_TAPS]
                        at = (c * ROWS + i * DIL) * PW + j * DIL
                        shifted = bass.AP(xpad, at, [[PW * PW, P], [PW, ROWS], [1, IMG]])
                        nc.vector.tensor_tensor(dst, taps_ps[:, j].rearrange("p (r w) -> p r w", w=IMG), shifted,
                                                ALU.mult).then_inc(mul, 1)

                    def row(b, c, i, cols):
                        if i >= 2 and 0 in cols:
                            dve.wait_ge(pool_added, (b * NCH + c) * (KS - 1) + max(i - 2, 1))
                        for j in cols:
                            multiply(b, c, i, j)

                    def finish(b, c):
                        dve.wait_ge(pool_added, (b * NCH + c + 1) * (KS - 1))
                        dve.wait_ge(mul, KS + (b * NCH + c + 1) * TAPS)
                        nc.vector.tensor_reduce(conv[:].rearrange("p (r w) -> p r w", w=IMG),
                                                parts[:].rearrange("p j r w -> p r w j"), AX.X, ALU.add).then_inc(vsum, 1)
                        dve.wait_ge(vsum, 1 + (b * NCH + c) * 2 + 1)
                        nc.vector.tensor_tensor(X[:, b, bass.ts(c, CH)], X[:, b, bass.ts(c, CH)], conv[:],
                                                ALU.add).then_inc(vsum, 1)

                    for b in range(B):
                        dve.wait_ge(xpad_ready, b + 1)
                        with dve.Fori(0, NCH, 1) as c:
                            dve.wait_ge(vsum, 1 + (b * NCH + c) * 2)
                            for i in range(KS):
                                row(b, c, i, range(KS))
                            finish(b, c)

        SHARED = B * T
        shared = sb("shared", [P, SHARED])
        stN = ExitStack()
        XN = sb("XN", [P, B, 2 + T], on=stN)

        def layer_norm(name):
            st = ExitStack()
            with st:
                sq = shared[:, 0:2 * CH].rearrange("p (s c) -> p s c", s=2)
                var_sb = shared[0:NCH, 2 * CH:3 * CH]
                rstd = shared[0:NCH, 3 * CH:4 * CH]
                psM = ps(f"{name}_psM", [P, 3, CH], st)
                psV = ps(f"{name}_psV", [NCH, CH], st)
                psS = ps(f"{name}_psS", [P, 3, CH], st)
                mean_ready, centred, squared, summed = (sem(f"{name}_{s}") for s in ("mean", "centred", "squared", "summed"))
                rooted, inverted, spread_out, normed, pads = (sem(f"{name}_{s}") for s in ("rooted", "inverted", "spread", "normed", "pads"))

                with nc.Block() as block:
                    @block.gpsimd
                    def _(pool):
                        nc.gpsimd.memset(XN[:, :, 0:2], 0.0).then_inc(pads, 1)
                        pool.wait_ge(pads, 1)

                    @block.tensor
                    def _(pe):
                        pe.sem_inc(summed, 1)
                        pe.sem_inc(spread_out, 1)
                        with pe.Fori(0, B, 1) as b:
                            def mean(c):
                                if c >= 3:
                                    pe.wait_ge(centred, 1 + b * NCH + c - 2)
                                else:
                                    pe.wait_ge(centred, 1 + b * NCH)
                                nc.tensor.matmul(psM[:, c % 3], averager[:], X[:, b, c * CH:(c + 1) * CH],
                                                 start=True, stop=True).then_inc(mean_ready, 1)

                            def var(c):
                                pe.wait_ge(squared, b * NCH + c + 1)
                                if c == 0:
                                    pe.wait_ge(rooted, 1 + b)
                                nc.tensor.matmul(psV[:], mean_col[:, c], sq[:, c % 2], start=(c == 0),
                                                 stop=(c == NCH - 1)).then_inc(summed, 1)

                            mean(0)
                            mean(1)
                            for c in range(NCH):
                                if c + 2 < NCH:
                                    mean(c + 2)
                                var(c)
                            pe.wait_ge(inverted, 1 + b + 1)
                            for c in range(NCH):
                                if c >= 3:
                                    pe.wait_ge(normed, 1 + b * NCH + c - 2)
                                else:
                                    pe.wait_ge(normed, 1 + b * NCH)
                                nc.tensor.matmul(psS[:, c % 3], spread[:, c], rstd, start=True,
                                                 stop=True).then_inc(spread_out, 1)

                    @block.scalar
                    def _(act):
                        act.sem_inc(rooted, 1)
                        with act.Fori(0, B, 1) as b:
                            for c in range(NCH):
                                act.wait_ge(centred, 1 + b * NCH + c + 1)
                                act.wait_ge(summed, 1 + b * NCH + max(c - 1, 0))
                                nc.scalar.activation(sq[:, c % 2], XN[:, b, 2 + c * CH:2 + (c + 1) * CH],
                                                     ACT.Square).then_inc(squared, 1)
                            act.wait_ge(summed, 1 + b * NCH + NCH)
                            act.wait_ge(inverted, 1 + b)
                            nc.scalar.activation(var_sb, psV[:], ACT.Sqrt, bias=eps_col[0:NCH]).then_inc(rooted, 1)

                    @block.vector
                    def _(dve):
                        dve.sem_inc(centred, 1)
                        dve.sem_inc(inverted, 1)
                        dve.sem_inc(normed, 1)
                        with dve.Fori(0, B, 1) as b:
                            for c in range(NCH):
                                dve.wait_ge(mean_ready, b * NCH + c + 1)
                                nc.vector.scalar_tensor_tensor(
                                    out=XN[:, b, 2 + c * CH:2 + (c + 1) * CH], in0=psM[:, c % 3], scalar=-1.0,
                                    in1=X[:, b, c * CH:(c + 1) * CH], op0=ALU.mult, op1=ALU.add).then_inc(centred, 1)
                            dve.wait_ge(rooted, 1 + b + 1)
                            dve.wait_ge(spread_out, 1 + b * NCH)
                            nc.vector.reciprocal(rstd, var_sb).then_inc(inverted, 1)
                            for c in range(NCH):
                                dve.wait_ge(spread_out, 1 + b * NCH + c + 1)
                                if c == 0:
                                    dve.wait_ge(squared, b * NCH + NCH)
                                v = XN[:, b, 2 + c * CH:2 + (c + 1) * CH]
                                nc.vector.tensor_tensor(v, psS[:, c % 3], v, ALU.mult).then_inc(normed, 1)

        layer_norm("ln1")

        st2 = ExitStack()
        with st2:
            used = [0]

            def carve(*dims):
                size = 1
                for d in dims:
                    size *= d
                a = used[0]
                used[0] += size
                assert used[0] <= SHARED
                names = "abcdef"[:len(dims)]
                spec = f"p ({' '.join(names)}) -> p {' '.join(names)}"
                return shared[:, a:a + size].rearrange(spec, **dict(zip(names, dims)))

            xs = carve(2, NW, 2, WIN)
            qs = carve(2, CH)
            ks = carve(2, CH)
            vs = carve(2, NW, P)
            pr = carve(2, NPAIR, HEADS, WIN)
            pT = carve(2, 2, NPAIR, P)
            at = carve(2, CH)
            keep_mask = carve(1, WIN)
            neg_mask = carve(1, WIN)
            red1 = sb("red1", [P, 2, 3, HEADS * NPAIR], on=st2)
            psS = ps("psS", [P, HEADS, CH], st2)
            psV = ps("psV", [P, 2, CH], st2)
            psO = ps("psO", [P, 2, CH], st2)

            chunk_in = sem("chunk_in")
            qk_mm = sem("qk_mm")
            q_out = sem("q_out")
            k_out = sem("k_out")
            v_mm = sem("v_mm")
            v_out = sem("v_out")
            v_zero = sem("v_zero")
            mask_fill = sem("mask_fill")
            s_mm = sem("s_mm")
            s_out = sem("s_out")
            masked = sem("masked")
            maxed = sem("maxed")
            shifted_ = sem("shifted_")
            exped = sem("exped")
            sumd = sem("sumd")
            recd = sem("recd")
            probs = sem("probs")
            pt_mm = sem("pt_mm")
            pt_out = sem("pt_out")
            o_mm = sem("o_mm")
            o_out = sem("o_out")
            y_mm = sem("y_mm")
            y_out = sem("y_out")

            NG2 = B * NCH // 2

            with nc.Block() as block:
                def where(i, s):
                    return (i * 2 + s) // NCH, (i * 2 + s) % NCH

                @block.gpsimd
                def _(pool):
                    nc.gpsimd.memset(keep_mask[:], 1.0).then_inc(mask_fill, 1)
                    nc.gpsimd.memset(neg_mask[:], 0.0).then_inc(mask_fill, 1)
                    pool.wait_ge(mask_fill, 2)
                    for w in range(2):
                        half = slice(w * WIN, (w + 1) * WIN)
                        for m, v in ((keep_mask, 0.0), (neg_mask, NEG)):
                            nc.gpsimd.affine_select(out=m[half], in_=m[half], compare_op=ALU.is_ge, fill=v, base=0,
                                                    pattern=[[0, 1], [-1, WIN]], channel_multiplier=1).then_inc(mask_fill, 1)
                    pool.wait_ge(mask_fill, 6)
                    nc.gpsimd.memset(vs[:], 0.0).then_inc(v_zero, 1)
                    for b in range(B):
                        with pool.Fori(0, NCH // 2, 1) as i:
                            g = (b * NCH // 2 + i) * 2
                            for s in range(2):
                                pool.wait_ge(v_mm, 1 + g)
                                src = XN[:, b, bass.ds(2 + (i * 2 + s) * CH, CH)].rearrange("p (n a t) -> p n a t", a=1, t=WIN)
                                nc.gpsimd.tensor_copy(xs[:, s], src.to_broadcast([P, NW, 2, WIN])).then_inc(chunk_in, 1)
                            for s in range(2):
                                pool.wait_ge(s_out, 1 + g + s + 1)
                                sc = pr[:, s].rearrange("p n h k -> p (n h) k")
                                nc.gpsimd.tensor_tensor(sc, sc, neg_mask.to_broadcast([P, NPAIR * HEADS, WIN]),
                                                        ALU.add).then_inc(masked, 1)

                @block.tensor
                def _(pe):
                    pe.sem_inc(v_mm, 1)
                    with pe.Fori(0, NG2, 1) as i:
                        g = i * 2

                        def scores(s):
                            pe.wait_ge(chunk_in, g + s + 1)
                            pe.wait_ge(y_out, 1 + g)
                            if s:
                                pe.wait_ge(q_out, g + 1)
                                pe.wait_ge(k_out, g + 1)
                            nc.tensor.matmul(psO[:, 0], wqkvT[:, 0], xs[:, s, :, 0], start=True, stop=True)
                            nc.tensor.matmul(psO[:, 1], wqkvT[:, 1], xs[:, s, :, 0], start=True, stop=True).then_inc(qk_mm, 1)
                            pe.wait_ge(pt_out, 1 + g)
                            if s:
                                pe.wait_ge(v_out, g + 1)
                            for w in range(NW):
                                both = xs[:, s, w].rearrange("p a t -> p (a t)")
                                last = nc.tensor.matmul(psV[:, w // 4, (w % 4) * P:(w % 4 + 1) * P], both,
                                                        wqkvT[:, 2], start=True, stop=True)
                            last.then_inc(v_mm, 1)
                            pe.wait_ge(q_out, g + s + 1)
                            pe.wait_ge(k_out, g + s + 1)
                            pe.wait_ge(s_out, 1 + g)
                            for n in range(NPAIR):
                                for w in range(2):
                                    for h in range(HEADS):
                                        tok = slice((2 * n + w) * WIN, (2 * n + w + 1) * WIN)
                                        hp = slice(h * HD, (h + 1) * HD)
                                        col = (s * NPAIR + n) * WIN
                                        last = nc.tensor.matmul(psS[w * WIN:(w + 1) * WIN, h, col:col + WIN],
                                                                qs[hp, s, tok], ks[hp, s, tok], start=True, stop=True)
                            last.then_inc(s_mm, 1)

                        def heads(s):
                            pe.wait_ge(probs, g + s + 1)
                            pe.wait_ge(v_out, g + 2)
                            pe.wait_ge(pt_out, 1 + g + s)
                            for a in range(2):
                                for n in range(NPAIR):
                                    last = nc.tensor.transpose(psV[:, a, n * P:(n + 1) * P],
                                                               pr[:, s, n, 2 * a:2 * a + 2].rearrange("p h k -> p (h k)"), ident[:])
                            last.then_inc(pt_mm, 1)
                            pe.wait_ge(pt_out, 1 + g + s + 1)
                            for n in range(NPAIR):
                                for w in range(2):
                                    for a in range(2):
                                        hp = slice(a * 2 * HD, (a + 1) * 2 * HD)
                                        tok = slice((2 * n + w) * WIN, (2 * n + w + 1) * WIN)
                                        last = nc.tensor.matmul(psO[hp, 1, tok], vs[:, s, 2 * n + w, hp],
                                                                pT[:, s, a, n, w * WIN:(w + 1) * WIN],
                                                                start=True, stop=True)
                            last.then_inc(o_mm, 1)

                        def project(s):
                            pe.wait_ge(o_out, g + s + 1)
                            pe.wait_ge(y_out, 1 + g + s)
                            nc.tensor.matmul(psO[:, 0], wprojT[:], at[:, s], start=True, stop=True).then_inc(y_mm, 1)

                        scores(0)
                        scores(1)
                        heads(0)
                        project(0)
                        heads(1)
                        project(1)

                @block.scalar
                def _(act):
                    act.sem_inc(pt_out, 1)
                    act.wait_ge(v_zero, 1)
                    with act.Fori(0, NG2, 1) as i:
                        g = i * 2
                        for s in range(2):
                            act.wait_ge(qk_mm, g + s + 1)
                            nc.scalar.activation(qs[:, s], psO[:, 0], ACT.Copy, scale=HD ** -0.5).then_inc(q_out, 1)
                            act.wait_ge(v_mm, 1 + g + s + 1)
                            for j in range(2):
                                half = slice(j * WIN, (j + 1) * WIN)
                                dst = vs[half, s].rearrange("p w (a j c) -> p (w a) j c", a=2, j=2)[:, :, j]
                                src = psV[half].rearrange("p b (w a j c) -> p (b w a) j c", a=2, j=2, c=HD)[:, :, j]
                                last = nc.scalar.activation(dst, src, ACT.Copy)
                            last.then_inc(v_out, 1)
                        for s in range(2):
                            act.wait_ge(shifted_, g + s + 1)
                            nc.scalar.activation(pr[:, s], pr[:, s], ACT.Exp).then_inc(exped, 1)
                        for s in range(2):
                            act.wait_ge(pt_mm, g + s + 1)
                            nc.scalar.activation(pT[:, s].rearrange("p a n q -> p a (n q)"), psV[:], ACT.Copy).then_inc(pt_out, 1)
                            act.wait_ge(o_mm, g + s + 1)
                            nc.scalar.activation(at[:, s], psO[:, 1], ACT.Copy).then_inc(o_out, 1)

                @block.vector
                def _(dve):
                    dve.sem_inc(y_out, 1)
                    dve.sem_inc(s_out, 1)
                    dve.wait_ge(mask_fill, 6)
                    for b in range(B):
                        with dve.Fori(0, NCH // 2, 1) as i:
                            g = (b * NCH // 2 + i) * 2
                            rows = [pr[:, s].rearrange("p n h k -> p (n h) k") for s in range(2)]

                            def spread_row(v):
                                return v.rearrange("p (m a) -> p m a", a=1).to_broadcast([P, HEADS * NPAIR, WIN])

                            def keys_out(s):
                                dve.wait_ge(qk_mm, g + s + 1)
                                nc.vector.tensor_copy(ks[:, s], psO[:, 1]).then_inc(k_out, 1)

                            def mask(s):
                                dve.wait_ge(s_mm, g + s + 1)
                                src = psS[:, :, s * NPAIR * WIN:(s + 1) * NPAIR * WIN].rearrange("p h (n k) -> p h n k", k=WIN)
                                keep = keep_mask.rearrange("p (a b) k -> p a b k", a=1).to_broadcast([P, HEADS, NPAIR, WIN])
                                nc.vector.tensor_tensor(pr[:, s].rearrange("p n h k -> p h n k"), src, keep,
                                                        ALU.mult).then_inc(s_out, 1)

                            def shift(s):
                                dve.wait_ge(masked, g + s + 1)
                                nc.vector.tensor_reduce(red1[:, s, 0], rows[s], AX.X, ALU.max).then_inc(maxed, 1)
                                dve.wait_ge(maxed, g + s + 1)
                                nc.vector.tensor_tensor(rows[s], rows[s], spread_row(red1[:, s, 0]),
                                                        ALU.subtract).then_inc(shifted_, 1)

                            def normalise(s):
                                dve.wait_ge(exped, g + s + 1)
                                nc.vector.tensor_reduce(red1[:, s, 1], rows[s], AX.X, ALU.add).then_inc(sumd, 1)
                                dve.wait_ge(sumd, g + s + 1)
                                nc.vector.reciprocal(red1[:, s, 2], red1[:, s, 1]).then_inc(recd, 1)
                                dve.wait_ge(recd, g + s + 1)
                                nc.vector.tensor_tensor(rows[s], rows[s], spread_row(red1[:, s, 2]),
                                                        ALU.mult).then_inc(probs, 1)

                            keys_out(0)
                            mask(0)
                            keys_out(1)
                            shift(0)
                            mask(1)
                            normalise(0)
                            shift(1)
                            normalise(1)
                            for s in range(2):
                                dve.wait_ge(y_mm, g + s + 1)
                                xv = X[:, b, bass.ts(i * 2 + s, CH)]
                                nc.vector.scalar_tensor_tensor(out=xv, in0=psO[:, 0], scalar=bproj[:], in1=xv,
                                                               op0=ALU.add, op1=ALU.add).then_inc(y_out, 1)

        layer_norm("ln2")

        U = shared[:].bitcast(F16).rearrange("p (b q n h c) -> p b q n h c", b=B, q=2, n=NBLK, h=2)
        SEGS = []
        for A in range(NGRP):
            cuts = sorted({0, CH} | {HALF // 2 ** e - A * CH for e in range(NE) if 0 < HALF // 2 ** e - A * CH < CH})
            SEGS.append([(c0, c1, sum(HALF // 2 ** e > A * CH + c0 for e in range(NE))) for c0, c1 in zip(cuts, cuts[1:])])

        st3 = ExitStack()
        with st3:
            mu = sb("mu", [P, NE, AR, P], on=st3)
            psA = ps("psA3", [P, 3, CH], st3)
            psU = ps("psU3", [P, 3, 4, P], st3)
            mu_in = sem("mu_in")
            mu_ready = sem("mu_ready")
            ar_mm = sem("ar_mm")
            ar_out = sem("ar_out")
            ut_mm = sem("ut_mm")
            u_hi = sem("u_hi")
            u_lo = sem("u_lo")
            AG = 2 * NGRP
            UG = 2 * NBLK // 4

            with nc.Block() as block:
                @block.sync
                def _(sp):
                    sp.dma_start(mu[:], m_u.rearrange("i a d e -> d i a e")).then_inc(mu_in, 16)
                    sp.wait_ge(mu_in, 16)

                @block.tensor
                def _(pe):
                    pe.wait_ge(mu_ready, NE)
                    for b in range(B):
                        for t in range(AG):
                            par, A = t // NGRP, t % NGRP
                            pe.wait_ge(ar_out, b * AG + (t - 2 if t >= 3 else 0))
                            for si, (c0, c1, ne) in enumerate(SEGS[A]):
                                for a in range(AR):
                                    lo = 2 + 2 * (A * CH + c0) + par - a
                                    last = nc.tensor.matmul(psA[:, t % 3, c0:c1], mu[:, ne - 1, a],
                                                            XN[:, b, lo:lo + 2 * (c1 - c0) - 1:2],
                                                            start=(a == 0), stop=(a == AR - 1))
                            last.then_inc(ar_mm, 1)
                            for r in (2 * t, 2 * t + 1) if UG == 2 * AG else (t,):
                                pe.wait_ge(u_lo, b * UG + (r - 2 if r >= 3 else 0))
                                for j in range(4):
                                    rp, rb = (4 * r + j) // NBLK, (4 * r + j) % NBLK
                                    first = 2 + rp + 2 * P * rb
                                    last = nc.tensor.transpose(psU[:, r % 3, j], XN[:, b, first:first + 2 * P - 1:2], ident[:])
                                last.then_inc(ut_mm, 1)

                @block.scalar
                def _(act):
                    for b in range(B):
                        for r in range(UG):
                            rp, rb = 4 * r // NBLK, 4 * r % NBLK
                            act.wait_ge(ut_mm, b * UG + r + 1)
                            nc.scalar.activation(U[:, b, rp, rb:rb + 4, 0], psU[:, r % 3], ACT.Copy,
                                                 scale=U_SCALE).then_inc(u_hi, 1)

                @block.vector
                def _(dve):
                    dve.wait_ge(mu_in, 16)
                    nc.vector.tensor_scalar(mu[:, 0], mu[:, 0], gate[:, 0:1], None, ALU.mult).then_inc(mu_ready, 1)
                    for e in range(1, NE):
                        dve.wait_ge(mu_ready, e)
                        nc.vector.scalar_tensor_tensor(out=mu[:, e], in0=mu[:, e], scalar=gate[:, e:e + 1],
                                                       in1=mu[:, e - 1], op0=ALU.mult, op1=ALU.add).then_inc(mu_ready, 1)
                    for b in range(B):
                        for t in range(AG):
                            par, A = t // NGRP, t % NGRP
                            dve.wait_ge(ar_mm, b * AG + t + 1)
                            lo = 2 * A * CH + par
                            xv = X[:, b, lo:lo + 2 * CH - 1:2]
                            nc.vector.tensor_tensor(xv, psA[:, t % 3], xv, ALU.add).then_inc(ar_out, 1)
                            for r in (2 * t, 2 * t + 1) if UG == 2 * AG else (t,):
                                rp, rb = 4 * r // NBLK, 4 * r % NBLK
                                dve.wait_ge(u_hi, b * UG + r + 1)
                                nc.vector.scalar_tensor_tensor(out=U[:, b, rp, rb:rb + 4, 1], in0=psU[:, r % 3],
                                                               scalar=U_SCALE, in1=U[:, b, rp, rb:rb + 4, 0],
                                                               op0=ALU.mult, op1=ALU.subtract).then_inc(u_lo, 1)

        stN.close()

        st4 = ExitStack()
        with st4:
            S = sb("S", [P, 2, 4, SW], F16, on=st4)
            m_raw = sb("m_raw", [P, 2, 2, NE, P], on=st4)
            pq = sb("pq", [P, 2, NE, P], on=st4)
            mt = sb("mt", [P, 2, NE, 2, P], on=st4)
            mk = sb("mk", [P, NE], on=st4)
            conv_sb = sb("conv_sb", [P, 4, CH], on=st4)
            psC = ps("psC", [P, 4, CH], st4)
            psY = ps("psY", [P, 3, CH], st4)

            f_in = [sem("f_in0"), sem("f_in1")]
            m_in = [sem("m_in0"), sem("m_in1")]
            mk_ready = sem("mk_ready")
            pq_ready = sem("pq_ready")
            mt_step = sem("mt_step")
            c_mm = sem("c_mm")
            c_outA = sem("c_outA")
            c_outV = sem("c_outV")
            m_mm = sem("m_mm")
            y_added = sem("y_added")
            stored = sem("stored")
            ITEMS = B * 2 * NGRP * 2
            YS = ITEMS // 2

            def item(n):
                b, r = divmod(n, 4 * NGRP)
                par, r = divmod(r, 2 * NGRP)
                A, q = divmod(r, 2)
                return b, par, A, q

            with nc.Block() as block:
                @block.gpsimd
                def _(pool):
                    def load(s, line_at, matrix_at):
                        pool.dma_start(S[:, s], bass.AP(lines.tensor, line_at, [[1, P], [LINE, 4], [1, SW]])).then_inc(f_in[s], 16)
                        for sign, m in enumerate((m_plus, m_minus)):
                            pool.dma_start(m_raw[:, s, sign], bass.AP(m.tensor, matrix_at, [[P, P], [NK * P * P, NE], [1, P]])).then_inc(m_in[s], 16)

                    for s in range(2):
                        load(s, s * 4 * LINE, s * P * P)
                    with pool.Fori(1, NK // 2, 1) as k:
                        for s in range(2):
                            pool.wait_ge(c_mm, ((k - 1) * 2 + s + 1) * ITEMS)
                            pool.wait_ge(mt_step, 1 + ((k - 1) * 2 + s + 1) * NE)
                            load(s, (k * 2 + s) * (4 * LINE), (k * 2 + s) * (P * P))

                @block.sync
                def _(sp):
                    sp.wait_ge(y_added, 1 + NK * YS)
                    for b in range(B):
                        sp.dma_start(out_v[:, b], X[:, b]).then_inc(stored, 16)
                    sp.wait_ge(stored, 16 * B)

                @block.tensor
                def _(pe):
                    pe.sem_inc(m_mm, 1)
                    with pe.Fori(0, NK // 2, 1) as k:
                        for s in range(2):
                            base = (k * 2 + s) * ITEMS
                            ybase = (k * 2 + s) * YS

                            def conv(n):
                                b, par, A, q = item(n)
                                src = par ^ q
                                shift = 0 if (q == 1 and par == 0) else 1
                                if n % 2 == 0:
                                    pe.wait_ge(c_outA, 1 + base // 2 + max(n // 2 - 1, 0))
                                else:
                                    pe.wait_ge(c_outV, 1 + base // 2 + max(n // 2 - 1, 0))
                                last_blk = 4 * A + 3
                                for blk in range(last_blk + 1):
                                    off = max(0, blk - 4 * A) * P
                                    z = HALF - shift - (4 * A - blk) * P - off
                                    stop = z - (CH - off)
                                    for ul, fl in ((0, 0), (1, 0), (0, 1)):
                                        last = nc.tensor.matmul(
                                            psC[:, n % 4, off:CH], U[:, b, src, blk, ul],
                                            S[:, s, 2 * q + fl, z:(stop if stop >= 0 else None):-1],
                                            start=(blk == 0 and ul == 0 and fl == 0),
                                            stop=(blk == last_blk and fl == 1))
                                last.then_inc(c_mm, 1)

                            def mixdown(n):
                                b, par, A, q = item(n)
                                pe.wait_ge(c_outA if n % 2 == 0 else c_outV, 1 + base // 2 + n // 2 + 1)
                                y = n // 2
                                if q == 0:
                                    pe.wait_ge(y_added, 1 + ybase + max(y - 2, 0))
                                for si, (c0, c1, ne) in enumerate(SEGS[A]):
                                    last = nc.tensor.matmul(psY[:, y % 3, c0:c1], mt[:, s, ne - 1, q],
                                                            conv_sb[:, n % 4, c0:c1], start=(q == 0 and si == 0),
                                                            stop=(q == 1), skip_group_check=True)
                                last.then_inc(m_mm, 1)

                            pe.wait_ge(f_in[s], 16 * k + 16)
                            conv(0)
                            conv(1)
                            pe.wait_ge(mt_step, 1 + ((k * 2 + s) + 1) * NE)
                            for n in range(2, ITEMS):
                                mixdown(n - 2)
                                conv(n)
                            mixdown(ITEMS - 2)
                            mixdown(ITEMS - 1)

                @block.scalar
                def _(act):
                    act.sem_inc(c_outA, 1)
                    with act.Fori(0, NK // 2, 1) as k:
                        for s in range(2):
                            base = (k * 2 + s) * ITEMS
                            for n in range(0, ITEMS, 2):
                                act.wait_ge(c_mm, base + n + 1)
                                act.wait_ge(m_mm, 1 + base + max(n - 3, 0))
                                nc.scalar.activation(conv_sb[:, n % 4], psC[:, n % 4], ACT.Copy).then_inc(c_outA, 1)

                @block.vector
                def _(dve):
                    dve.sem_inc(c_outV, 1)
                    dve.sem_inc(y_added, 1)
                    dve.sem_inc(mt_step, 1)
                    with dve.Fori(0, NK // 2, 1) as k:
                        for s in range(2):
                            f = k * 2 + s
                            base = f * ITEMS
                            dve.wait_ge(m_in[s], 32 * k + 32)
                            dve.wait_ge(mt_step, 1 + f * NE)
                            nc.vector.tensor_copy(mk[:], mix[:, :, bass.ds(f, 1)].rearrange("p e a -> p (e a)")).then_inc(mk_ready, 1)
                            nc.vector.tensor_tensor(pq[:, 0], m_raw[:, s, 0], m_raw[:, s, 1], ALU.add).then_inc(pq_ready, 1)
                            nc.vector.tensor_tensor(pq[:, 1], m_raw[:, s, 0], m_raw[:, s, 1], ALU.subtract).then_inc(pq_ready, 1)
                            dve.wait_ge(mk_ready, f + 1)
                            dve.wait_ge(pq_ready, 2 * f + 2)
                            nc.vector.tensor_scalar(mt[:, s, 0], pq[:, :, 0], mk[:, 0:1], None, ALU.mult).then_inc(mt_step, 1)
                            for e in range(1, NE):
                                dve.wait_ge(mt_step, 1 + f * NE + e)
                                nc.vector.scalar_tensor_tensor(out=mt[:, s, e], in0=pq[:, :, e], scalar=mk[:, e:e + 1],
                                                               in1=mt[:, s, e - 1], op0=ALU.mult, op1=ALU.add).then_inc(mt_step, 1)
                            def add(y):
                                b, par, A, _ = item(2 * y)
                                dve.wait_ge(m_mm, 1 + base + 2 * y + 2)
                                lo = 2 * A * CH + par
                                xv = X[:, b, lo:lo + 2 * CH - 1:2]
                                nc.vector.tensor_tensor(xv, psY[:, y % 3], xv, ALU.add).then_inc(y_added, 1)

                            for n in range(1, ITEMS, 2):
                                dve.wait_ge(c_mm, base + n + 1)
                                dve.wait_ge(m_mm, 1 + base + max(n - 3, 0))
                                nc.vector.tensor_copy(conv_sb[:, n % 4], psC[:, n % 4]).then_inc(c_outV, 1)
                                if n >= 3:
                                    add((n - 3) // 2)
                            add(YS - 1)


_INS = ['x', 'L0_conv_w_reduce', 'L0_conv_b_reduce', 'L0_conv_w_span', 'L0_conv_b_span', 'L1_attn_w_qkv',
        'L1_attn_w_proj', 'L1_attn_b_proj', 'L1_ffn_sigma', 'L1_ffn_phi', 'L1_ffn_M_u', 'L1_ffn_M_phi_plus',
        'L1_ffn_M_phi_minus', 'L1_ffn_log_weights', 'L1_ffn_gumbel']


def kernel(**inputs):
    import numpy as np
    import concourse.bacc as bacc
    from concourse.bass_utils import run_bass_kernel_spmd

    nc = bacc.Bacc("TRN2", target_bir_lowering=False, num_devices=1)
    arrays, args = {}, []
    for name in _INS:
        a = np.ascontiguousarray(inputs[name])
        arrays[f"in_{name}"] = a
        args.append(nc.dram_tensor(f"in_{name}", a.shape, mybir.dt.from_np(a.dtype), kind="ExternalInput").ap())
    out = nc.dram_tensor("out_x", inputs["x"].shape, F32, kind="ExternalOutput").ap()
    program(nc, *args, out)
    r = run_bass_kernel_spmd(nc, [arrays], core_ids=[0])
    return r.results[0]["out_x"]
```

```python
from contextlib import ExitStack

import concourse.bass as bass
from concourse import mybir

F32 = mybir.dt.float32
F16 = mybir.dt.float16
ALU = mybir.AluOpType
ACT = mybir.ActivationFunctionType
AX = mybir.AxisListType

P = 128
B = 4
IMG = 64
T = IMG * IMG
CH = 512
NCH = T // CH
ROWS = CH // IMG

KS = 7
DIL = 2
PAD = 6
GC = 8
CG = P // GC
CR = 32
TAPS = KS * KS
PW = IMG + 2 * PAD
POOL_TAPS = 5
PARTS = POOL_TAPS + KS * (KS - POOL_TAPS)
GN_CH = 4
GN_EPS = 1e-5
LN_EPS = 1e-5

HEADS = 4
HD = P // HEADS
WIN = 64
NW = CH // WIN
NPAIR = NW // 2
NEG = -10000.0

NK = 16
NE = 4
AR = 3
HALF = T // 2
NBLK = HALF // P
NGRP = HALF // CH
PH_SCALE = 4096.0
U_SCALE = 256.0
HC = CH // 2
LINE = P + HALF
SW = HALF + 1


def program(nc, x, w_reduce, b_reduce, w_span, b_span, w_qkv, w_proj, b_proj,
            sigma, phi, m_u, m_plus, m_minus, log_weights, gumbel, out):
    x_v = x.rearrange("b c h w -> c b (h w)")
    out_v = out.rearrange("b c h w -> c b (h w)")
    lines = nc.dram_tensor("filter_lines", [NK, 2, 4, LINE], F16, kind="Internal").ap()

    top = ExitStack()
    with top:
        def sb(name, shape, dt=F32, on=top):
            return on.enter_context(nc.sbuf_tensor(name, shape, dt))

        def ps(name, shape, on):
            return on.enter_context(nc.psum_tensor(name, shape, F32))

        def sem(name):
            return top.enter_context(nc.semaphore(name))

        X = sb("X", [P, B, T])
        ident = sb("ident", [P, P])
        averager = sb("averager", [P, P])
        gn_avg = sb("gn_avg", [P, P])
        eps_col = sb("eps_col", [P, 1])
        one_row = sb("one_row", [1, P])
        wqkvT = sb("wqkvT", [P, 3, P])
        wprojT = sb("wprojT", [P, P])
        bproj = sb("bproj", [P, 1])
        mix = sb("mix", [P, NE, NK])
        gate = sb("gate", [P, NE])

        st0 = ExitStack()
        with st0:
            flip = sb("flip", [P, P], on=st0)
            wq_raw = sb("wq_raw", [P, 3, P], on=st0)
            wp_raw = sb("wp_raw", [P, P], on=st0)
            gate_in = sb("gate_in", [P, 2, NE], on=st0)
            gate_t = sb("gate_t", [P, 8, NE], on=st0)
            gate_s = sb("gate_s", [P, 8], on=st0)
            sig_in = sb("sig_in", [P, 3, NK], on=st0)
            phi_in = sb("phi_in", [P, 32, NK], on=st0)
            phi_n = sb("phi_n", [P, 32, NK], on=st0)
            phi_m = sb("phi_m", [P, 6], on=st0)
            line32 = sb("line32", [NK, 2, HALF + HC], on=st0)
            sum32 = sb("sum32", [NK, 2, HALF], on=st0)
            line_sb = sb("line_sb", [NK, 2, 4, LINE], F16, on=st0)
            psA = ps("psA", [P, 4, P], st0)
            psB = ps("psB", [P, P], st0)
            psP = ps("psP", [P, 4, CH], st0)

            weights_in = sem("weights_in")
            gate_ld = sem("gate_ld")
            phi_ld = sem("phi_ld")
            consts = sem("consts")
            ident0 = sem("ident0")
            wT_ready = sem("wT_ready")
            phi_rowmax = sem("phi_rowmax")
            phi_maxT = sem("phi_maxT")
            phi_max = sem("phi_max")
            phi_bc = sem("phi_bc")
            phi_scaled = sem("phi_scaled")
            phi_T = sem("phi_T")
            line_part = sem("line_part")
            line_sum = sem("line_sum")
            line_hi = sem("line_hi")
            line_lo = sem("line_lo")
            line_zero = sem("line_zero")
            lines_out = sem("lines_out")
            v0 = sem("v0")
            expd = sem("expd")
            sigd = sem("sigd")

            with nc.Block() as block:
                @block.sync
                def _(sp):
                    sp.dma_start(phi_in[:], phi.rearrange("(a l) k -> a l k", a=P)).then_inc(phi_ld, 16)
                    sp.dma_start(wq_raw[:], w_qkv.rearrange("(t p) c -> p t c", p=P)).then_inc(weights_in, 16)
                    sp.dma_start(wp_raw[:], w_proj).then_inc(weights_in, 16)
                    sp.dma_start(gate_in[:, 0], bass.AP(log_weights.tensor, 0, [[0, P], [1, NE]])).then_inc(gate_ld, 16)
                    sp.dma_start(gate_in[:, 1], bass.AP(gumbel.tensor, 0, [[0, P], [1, NE]])).then_inc(gate_ld, 16)
                    sp.dma_start(sig_in[:, 0], bass.AP(sigma.tensor, 0, [[0, P], [1, NK]])).then_inc(gate_ld, 16)
                    sp.dma_start(bproj[:], b_proj.rearrange("(c a) -> c a", a=1)).then_inc(weights_in, 16)
                    sp.wait_ge(line_hi, 2)
                    sp.wait_ge(line_lo, 2)
                    sp.dma_start(lines, line_sb[:]).then_inc(lines_out, 16)
                    sp.wait_ge(lines_out, 16)
                    sp.wait_ge(weights_in, 48)
                    sp.wait_ge(gate_ld, 48)

                @block.gpsimd
                def _(pool):
                    nc.gpsimd.memset(ident[:], 0.0).then_inc(ident0, 1)
                    nc.gpsimd.memset(gn_avg[:], 1.0 / GN_CH).then_inc(ident0, 1)
                    nc.gpsimd.memset(flip[:], 0.0).then_inc(ident0, 1)
                    pool.wait_ge(ident0, 3)
                    nc.gpsimd.affine_select(out=ident[:], in_=ident[:], compare_op=ALU.not_equal, fill=1.0,
                                            base=0, pattern=[[-1, P]], channel_multiplier=1).then_inc(consts, 1)
                    nc.gpsimd.affine_select(out=flip[:], in_=flip[:], compare_op=ALU.not_equal, fill=1.0,
                                            base=1 - P, pattern=[[1, P]], channel_multiplier=1).then_inc(consts, 1)
                    gv = gn_avg[:].rearrange("p (g r) -> p g r", r=GN_CH)
                    nc.gpsimd.affine_select(out=gv, in_=gv, compare_op=ALU.is_ge, fill=0.0, base=0,
                                            pattern=[[-GN_CH, P // GN_CH], [0, GN_CH]],
                                            channel_multiplier=1).then_inc(ident0, 1)
                    pool.wait_ge(ident0, 4)
                    nc.gpsimd.affine_select(out=gv, in_=gv, compare_op=ALU.is_ge, fill=0.0, base=GN_CH - 1,
                                            pattern=[[GN_CH, P // GN_CH], [0, GN_CH]],
                                            channel_multiplier=-1).then_inc(consts, 1)
                    nc.gpsimd.memset(averager[:], 1.0 / P).then_inc(consts, 1)
                    nc.gpsimd.memset(one_row[:], 1.0).then_inc(consts, 1)
                    nc.gpsimd.memset(eps_col[:], LN_EPS).then_inc(consts, 1)
                    nc.gpsimd.memset(line32[:, :, HALF:], 0.0).then_inc(consts, 1)
                    nc.gpsimd.memset(line_sb[:, :, :, HALF:], 0.0).then_inc(consts, 1)

                    pool.wait_ge(consts, 8)
                    pool.wait_ge(line_hi, 1)
                    nc.gpsimd.tensor_tensor(line_sb[:, :, 1, 0:HALF], line32[:, :, 0:HALF], line_sb[:, :, 0, 0:HALF],
                                            ALU.subtract).then_inc(line_lo, 1)

                @block.tensor
                def _(pe):
                    pe.wait_ge(consts, 8)
                    pe.wait_ge(weights_in, 48)
                    for t in range(3):
                        nc.tensor.transpose(psA[:, t], wq_raw[:, t], ident[:])
                    nc.tensor.transpose(psA[:, 3], wp_raw[:], ident[:]).then_inc(wT_ready, 1)
                    pe.wait_ge(phi_rowmax, 1)
                    nc.tensor.transpose(psB[0:1, :], phi_m[:, 0:1], ident[:]).then_inc(phi_maxT, 1)
                    pe.wait_ge(phi_max, 1)
                    nc.tensor.matmul(psB[:, 0:1], one_row[:], phi_m[0:1, 1:2], start=True, stop=True).then_inc(phi_bc, 1)
                    pe.wait_ge(phi_scaled, 1)
                    for r in range(8):
                        if r >= 4:
                            pe.wait_ge(line_part, r - 3)
                        for j in range(4):
                            slot = (1 - j // 2) * 2 + j % 2
                            last = nc.tensor.matmul(psP[0:NK, r % 4, slot * P:(slot + 1) * P], phi_n[:, 4 * r + j],
                                                    flip[:], start=True, stop=True)
                        last.then_inc(phi_T, 1)

                @block.scalar
                def _(act):
                    act.wait_ge(v0, 4)
                    nc.scalar.activation(gate_t[:, 2], gate_t[:, 1], ACT.Exp).then_inc(expd, 1)
                    act.wait_ge(gate_ld, 48)
                    nc.scalar.activation(sig_in[:, 1], sig_in[:, 0], ACT.Sqrt).then_inc(sigd, 1)
                    act.wait_ge(sigd, 1)
                    nc.scalar.activation(sig_in[:, 2], sig_in[:, 1], ACT.Sqrt).then_inc(sigd, 1)
                    act.wait_ge(consts, 8)
                    for r in range(8):
                        act.wait_ge(phi_T, r + 1)
                        for q in range(2):
                            src = psP[0:NK, r % 4, :].rearrange("p (j q a) -> p q j a", q=2, j=2)[:, q]
                            dst = line32[:, q, 0:HALF].rearrange("p (a l) -> p l a", l=16)[:, 14 - 2 * r:16 - 2 * r]
                            last = nc.scalar.activation(dst, src, ACT.Copy)
                        last.then_inc(line_part, 1)
                    act.wait_ge(line_part, 8)
                    nc.scalar.activation(line_sb[:, :, 0, 0:HALF], line32[:, :, 0:HALF], ACT.Copy).then_inc(line_hi, 1)
                    act.wait_ge(line_sum, 1)
                    nc.scalar.activation(line_sb[:, :, 2, 0:HALF], sum32[:], ACT.Copy).then_inc(line_hi, 1)

                @block.vector
                def _(dve):
                    n = [0]

                    def link(ins):
                        n[0] += 1
                        ins.then_inc(v0, 1)
                        dve.wait_ge(v0, n[0])

                    dve.wait_ge(gate_ld, 48)
                    link(nc.vector.tensor_tensor(gate_t[:, 0], gate_in[:, 0], gate_in[:, 1], ALU.add))
                    link(nc.vector.tensor_reduce(gate_s[:, 0:1], gate_t[:, 0], AX.X, ALU.max))
                    link(nc.vector.tensor_scalar(gate_t[:, 1], gate_t[:, 0], gate_s[:, 0:1], None, ALU.subtract))
                    link(nc.vector.memset(gate_s[:, 4:5], 1.0))
                    dve.wait_ge(expd, 1)
                    link(nc.vector.tensor_reduce(gate_s[:, 1:2], gate_t[:, 2], AX.X, ALU.add))
                    link(nc.vector.reciprocal(gate_s[:, 2:3], gate_s[:, 1:2]))
                    link(nc.vector.tensor_scalar(gate_t[:, 3], gate_t[:, 2], gate_s[:, 2:3], None, ALU.mult))
                    link(nc.vector.tensor_reduce(gate_s[:, 3:4], gate_t[:, 3], AX.X, ALU.max))
                    link(nc.vector.tensor_scalar(gate_t[:, 4], gate_t[:, 3], gate_s[:, 3:4], None, ALU.is_equal))
                    for i in range(NE):
                        link(nc.vector.tensor_tensor(gate_t[:, 5, i:i + 1], gate_t[:, 4, i:i + 1], gate_s[:, 4:5], ALU.mult))
                        link(nc.vector.tensor_tensor(gate_s[:, 4:5], gate_s[:, 4:5], gate_t[:, 5, i:i + 1], ALU.subtract))
                    link(nc.vector.tensor_tensor(gate_t[:, 6], gate_t[:, 5], gate_t[:, 3], ALU.subtract))
                    link(nc.vector.tensor_tensor(gate[:], gate_t[:, 6], gate_t[:, 3], ALU.add))
                    dve.wait_ge(phi_ld, 16)
                    nc.vector.tensor_reduce(phi_m[:, 0:1], phi_in[:], AX.XY, ALU.max,
                                            apply_absolute_value=True).then_inc(phi_rowmax, 1)
                    dve.wait_ge(phi_maxT, 1)
                    nc.vector.tensor_reduce(phi_m[0:1, 1:2], psB[0:1, :], AX.X, ALU.max).then_inc(phi_max, 1)
                    dve.wait_ge(phi_bc, 1)
                    link(nc.vector.tensor_scalar(phi_m[:, 2:3], psB[:, 0:1], 1e-30, None, ALU.max))
                    link(nc.vector.reciprocal(phi_m[:, 3:4], phi_m[:, 2:3]))
                    nc.vector.tensor_scalar(phi_n[:], phi_in[:], phi_m[:, 3:4], PH_SCALE, ALU.mult,
                                            ALU.mult).then_inc(phi_scaled, 1)
                    link(nc.vector.tensor_scalar(phi_m[:, 4:5], phi_m[:, 2:3], 1.0 / (PH_SCALE * U_SCALE), None, ALU.mult))
                    dve.wait_ge(sigd, 2)
                    for i in range(NE):
                        link(nc.vector.tensor_scalar(mix[:, i], sig_in[:, 2], gate[:, i:i + 1], phi_m[:, 4:5],
                                                     ALU.mult, ALU.mult))
                    dve.wait_ge(consts, 8)
                    dve.wait_ge(line_part, 8)
                    nc.vector.tensor_tensor(sum32[:], line32[:, :, 0:HALF], line32[:, :, HC:HC + HALF], ALU.add).then_inc(line_sum, 1)
                    dve.wait_ge(line_sum, 1)
                    dve.wait_ge(line_hi, 2)
                    nc.vector.tensor_tensor(line_sb[:, :, 3, 0:HALF], sum32[:], line_sb[:, :, 2, 0:HALF],
                                            ALU.subtract).then_inc(line_lo, 1)
                    dve.wait_ge(wT_ready, 1)
                    nc.vector.tensor_copy(wqkvT[:], psA[:, 0:3])
                    link(nc.vector.tensor_copy(wprojT[:], psA[:, 3]))

        st1 = ExitStack()
        with st1:
            xpad = sb("xpad", [P, PW, PW], on=st1)
            red = sb("red", [P, T], on=st1)
            tapw = sb("tapw", [P, TAPS, P], on=st1)
            wsT = sb("wsT", [CR + 1, GC * TAPS], on=st1)
            ws_raw = sb("ws_raw", [98, 4, CR], on=st1)
            wrT = sb("wrT", [P, CR], on=st1)
            wr_raw = sb("wr_raw", [CR, P], on=st1)
            bred = sb("bred", [CR, 1], on=st1)
            prod = sb("prod", [P, 2, POOL_TAPS, ROWS, IMG], on=st1)
            parts = sb("parts", [P, PARTS, ROWS, IMG], on=st1)
            conv = sb("conv", [P, CH], on=st1)
            bn = sb("bn", [P, B, NCH, 6], on=st1)
            cstat = sb("cstat", [P, B, 2], on=st1)
            dstat = sb("dstat", [P, 6, B], on=st1)
            taps_ps = ps("taps_ps", [P, KS, CH], st1)
            psR = ps("psR", [P, CH], st1)

            x_in = sem("x_in")
            cw_in = sem("cw_in")
            wr_T = sem("wr_T")
            ws_T = sem("ws_T")
            wr_ready = sem("wr_ready")
            tap_ready = sem("tap_ready")
            tap_zero = sem("tap_zero")
            gn_a = sem("gn_a")
            gn_b = sem("gn_b")
            v1 = sem("v1")
            frame = sem("frame")
            gmean = sem("gmean")
            gvar = sem("gvar")
            gstd = sem("gstd")
            gnorm = sem("gnorm")
            xpad_ready = sem("xpad_ready")
            red_mm = sem("red_mm")
            red_ready = sem("red_ready")
            kern = sem("kern")
            mul = sem("mul")
            pool_added = sem("pool_added")
            vsum = sem("vsum")

            with nc.Block() as block:
                @block.sync
                def _(sp):
                    for b in range(B):
                        sp.dma_start(X[:, b], x_v[:, b]).then_inc(x_in, 16)
                    sp.dma_start(ws_raw[:], w_span.rearrange("(t r) o -> r t o", r=98)).then_inc(cw_in, 16)
                    sp.dma_start(wr_raw[:], w_reduce).then_inc(cw_in, 16)
                    sp.dma_start(bred[:], b_reduce.rearrange("(c a) -> c a", a=1)).then_inc(cw_in, 16)
                    sp.dma_start(wsT[CR:CR + 1, :], b_span.rearrange("(a k) -> a k", a=1)).then_inc(cw_in, 16)

                @block.gpsimd
                def _(pool):
                    nc.gpsimd.memset(xpad[:], 0.0).then_inc(frame, 1)
                    nc.gpsimd.memset(red[:], 0.0).then_inc(frame, 1)
                    nc.gpsimd.memset(tapw[:], 0.0).then_inc(tap_zero, 1)
                    pool.wait_ge(frame, 2)
                    pool.wait_ge(tap_zero, 1)
                    nc.gpsimd.memset(red[CR:CR + 1, :], 1.0).then_inc(frame, 1)
                    for b in range(B):
                        with pool.Fori(0, NCH, 1) as c:
                            for i in range(1, KS):
                                pool.wait_ge(mul, KS + ((b * NCH + c) * KS + i) * KS + POOL_TAPS)
                                if i == 1:
                                    pool.wait_ge(vsum, 1 + (b * NCH + c) * 2)
                                else:
                                    pool.wait_ge(pool_added, (b * NCH + c) * (KS - 1) + i - 1)
                                sums = parts[:, 0:POOL_TAPS]
                                nc.gpsimd.tensor_tensor(sums, prod[:, 0] if i == 1 else sums, prod[:, i % 2],
                                                        ALU.add).then_inc(pool_added, 1)

                @block.tensor
                def _(pe):
                    pe.wait_ge(cw_in, 64)
                    nc.tensor.transpose(psR[:, 0:CR], wr_raw[:], ident[0:CR, 0:CR]).then_inc(wr_T, 1)
                    for t in range(4):
                        last = nc.tensor.transpose(taps_ps[0:CR, 0, t * 98:(t + 1) * 98], ws_raw[:, t], ident[0:98, 0:98])
                    last.then_inc(ws_T, 1)
                    pe.wait_ge(gn_a, 1)
                    nc.tensor.matmul(taps_ps[:, 1, 0:B], gn_avg[:], dstat[:, 0], start=True, stop=True).then_inc(gmean, 1)
                    pe.wait_ge(gn_b, 1)
                    nc.tensor.matmul(taps_ps[:, 2, 0:B], gn_avg[:], dstat[:, 2], start=True, stop=True).then_inc(gvar, 1)
                    pe.wait_ge(wr_ready, 1)
                    pe.wait_ge(tap_ready, 1)
                    pe.wait_ge(gnorm, 1)
                    for b in range(B):
                        pe.wait_ge(xpad_ready, b + 1)
                        for c in range(NCH):
                            if b or c:
                                pe.wait_ge(red_ready, b * NCH + c)
                            nc.tensor.matmul(psR[0:CR, :], wrT[:],
                                             xpad[:, PAD + c * ROWS:PAD + (c + 1) * ROWS, PAD:PAD + IMG],
                                             start=True, stop=True).then_inc(red_mm, 1)
                        pe.wait_ge(red_ready, (b + 1) * NCH)
                        with pe.Fori(0, NCH, 1) as c:
                            for i in range(KS):
                                for j in range(KS):
                                    pe.wait_ge(mul, ((b * NCH + c) * KS + i) * KS + j + 1)
                                    nc.tensor.matmul(taps_ps[:, j], tapw[:, i * KS + j], red[:, bass.ts(c, CH)],
                                                     start=True, stop=True).then_inc(kern, 1)

                @block.scalar
                def _(act):
                    act.wait_ge(gn_b, 2)
                    nc.scalar.activation(dstat[:, 3], dstat[:, 5], ACT.Sqrt, bias=eps_col[:]).then_inc(gstd, 1)
                    act.wait_ge(frame, 3)
                    act.wait_ge(gnorm, 1)
                    act.wait_ge(x_in, 16 * B)
                    for b in range(B):
                        if b:
                            act.wait_ge(mul, KS + b * NCH * TAPS)
                        nc.scalar.activation(xpad[:, PAD:PAD + IMG, PAD:PAD + IMG],
                                             X[:, b].rearrange("p (h w) -> p h w", w=IMG), ACT.Identity,
                                             bias=dstat[:, 4, b:b + 1], scale=dstat[:, 2, b:b + 1]).then_inc(xpad_ready, 1)
                        if b:
                            act.wait_ge(kern, b * NCH * TAPS)
                        for c in range(NCH):
                            act.wait_ge(red_mm, b * NCH + c + 1)
                            nc.scalar.activation(red[0:CR, c * CH:(c + 1) * CH], psR[0:CR, :], ACT.Identity,
                                                 bias=bred[:]).then_inc(red_ready, 1)

                @block.vector
                def _(dve):
                    dve.sem_inc(mul, KS)
                    dve.sem_inc(vsum, 1)
                    n = [0]

                    def link(ins):
                        n[0] += 1
                        ins.then_inc(v1, 1)
                        dve.wait_ge(v1, n[0])

                    dve.wait_ge(x_in, 16 * B)
                    for b in range(B):
                        for c in range(NCH):
                            last = nc.vector.bn_stats(bn[:, b, c], X[:, b, c * CH:(c + 1) * CH])
                    link(last)
                    for b in range(B):
                        last = nc.vector.bn_aggr(cstat[:, b], bn[:, b])
                    link(last)
                    nc.vector.tensor_copy(dstat[:, 0], cstat[:, :, 0]).then_inc(gn_a, 1)
                    dve.wait_ge(gmean, 1)
                    link(nc.vector.tensor_copy(dstat[:, 1], taps_ps[:, 1, 0:B]))
                    link(nc.vector.tensor_tensor(dstat[:, 3], dstat[:, 0], dstat[:, 1], ALU.subtract))
                    link(nc.vector.tensor_tensor(dstat[:, 4], dstat[:, 3], dstat[:, 3], ALU.mult))
                    nc.vector.tensor_tensor(dstat[:, 2], dstat[:, 4], cstat[:, :, 1], ALU.add).then_inc(gn_b, 1)
                    dve.wait_ge(gvar, 1)
                    nc.vector.tensor_copy(dstat[:, 5], taps_ps[:, 2, 0:B]).then_inc(gn_b, 1)
                    dve.wait_ge(gstd, 1)
                    link(nc.vector.reciprocal(dstat[:, 2], dstat[:, 3]))
                    nc.vector.scalar_tensor_tensor(out=dstat[:, 4], in0=dstat[:, 1], scalar=-1.0, in1=dstat[:, 2],
                                                   op0=ALU.mult, op1=ALU.mult).then_inc(gnorm, 1)
                    dve.wait_ge(wr_T, 1)
                    nc.vector.tensor_copy(wrT[:], psR[:, 0:CR]).then_inc(wr_ready, 1)
                    dve.wait_ge(ws_T, 1)
                    link(nc.vector.tensor_copy(wsT[0:CR, :], taps_ps[0:CR, 0, 0:GC * TAPS]))
                    dve.wait_ge(tap_zero, 1)
                    for k in range(TAPS):
                        src = wsT[:].rearrange("p (g k) -> p g k", k=TAPS)[:, :, k:k + 1]
                        last = nc.vector.tensor_copy(tapw[0:CR + 1, k].rearrange("p (g c) -> p g c", c=CG),
                                                     src.to_broadcast([CR + 1, GC, CG]))
                    last.then_inc(tap_ready, 1)

                    def multiply(b, c, i, j):
                        dve.wait_ge(kern, ((b * NCH + c) * KS + i) * KS + j + 1)
                        if j < POOL_TAPS:
                            dst = prod[:, i % 2, j]
                        else:
                            dst = parts[:, POOL_TAPS + i * (KS - POOL_TAPS) + j - POOL_TAPS]
                        at = (c * ROWS + i * DIL) * PW + j * DIL
                        shifted = bass.AP(xpad, at, [[PW * PW, P], [PW, ROWS], [1, IMG]])
                        nc.vector.tensor_tensor(dst, taps_ps[:, j].rearrange("p (r w) -> p r w", w=IMG), shifted,
                                                ALU.mult).then_inc(mul, 1)

                    def row(b, c, i, cols):
                        if i >= 2 and 0 in cols:
                            dve.wait_ge(pool_added, (b * NCH + c) * (KS - 1) + max(i - 2, 1))
                        for j in cols:
                            multiply(b, c, i, j)

                    def finish(b, c):
                        dve.wait_ge(pool_added, (b * NCH + c + 1) * (KS - 1))
                        dve.wait_ge(mul, KS + (b * NCH + c + 1) * TAPS)
                        nc.vector.tensor_reduce(conv[:].rearrange("p (r w) -> p r w", w=IMG),
                                                parts[:].rearrange("p j r w -> p r w j"), AX.X, ALU.add).then_inc(vsum, 1)
                        dve.wait_ge(vsum, 1 + (b * NCH + c) * 2 + 1)
                        nc.vector.tensor_tensor(X[:, b, bass.ts(c, CH)], X[:, b, bass.ts(c, CH)], conv[:],
                                                ALU.add).then_inc(vsum, 1)

                    for b in range(B):
                        dve.wait_ge(xpad_ready, b + 1)
                        with dve.Fori(0, NCH, 1) as c:
                            dve.wait_ge(vsum, 1 + (b * NCH + c) * 2)
                            for i in range(KS):
                                row(b, c, i, range(KS))
                            finish(b, c)

        SHARED = B * T
        shared = sb("shared", [P, SHARED])
        stN = ExitStack()
        XN = sb("XN", [P, B, 2 + T], on=stN)
        mean_col = sb("mean_col", [P, NCH, NCH], on=stN)
        spread = sb("spread", [NCH, NCH, P], on=stN)

        def layer_norm(name):
            st = ExitStack()
            with st:
                sq = shared[:, 0:2 * CH].rearrange("p (s c) -> p s c", s=2)
                var_sb = shared[0:NCH, 2 * CH:3 * CH]
                rstd = shared[0:NCH, 3 * CH:4 * CH]
                psM = ps(f"{name}_psM", [P, 3, CH], st)
                psV = ps(f"{name}_psV", [NCH, CH], st)
                psS = ps(f"{name}_psS", [P, 3, CH], st)
                mean_ready, centred, squared, summed = (sem(f"{name}_{s}") for s in ("mean", "centred", "squared", "summed"))
                rooted, inverted, spread_out, normed, pads = (sem(f"{name}_{s}") for s in ("rooted", "inverted", "spread", "normed", "pads"))

                with nc.Block() as block:
                    @block.gpsimd
                    def _(pool):
                        nc.gpsimd.memset(XN[:, :, 0:2], 0.0).then_inc(pads, 1)
                        nc.gpsimd.memset(mean_col[:], 0.0).then_inc(pads, 1)
                        nc.gpsimd.memset(spread[:], 0.0).then_inc(pads, 1)
                        pool.wait_ge(pads, 3)
                        nc.gpsimd.affine_select(out=mean_col[:], in_=mean_col[:], compare_op=ALU.not_equal,
                                                fill=1.0 / P, base=0, pattern=[[1, NCH], [-1, NCH]],
                                                channel_multiplier=0).then_inc(pads, 1)
                        nc.gpsimd.affine_select(out=spread[:], in_=spread[:], compare_op=ALU.not_equal, fill=1.0,
                                                base=0, pattern=[[-1, NCH], [0, P]], channel_multiplier=1).then_inc(pads, 1)

                    @block.tensor
                    def _(pe):
                        pe.sem_inc(summed, 1)
                        pe.wait_ge(pads, 5)
                        pe.sem_inc(spread_out, 1)
                        with pe.Fori(0, B, 1) as b:
                            def mean(c):
                                if c >= 3:
                                    pe.wait_ge(centred, 1 + b * NCH + c - 2)
                                else:
                                    pe.wait_ge(centred, 1 + b * NCH)
                                nc.tensor.matmul(psM[:, c % 3], averager[:], X[:, b, c * CH:(c + 1) * CH],
                                                 start=True, stop=True).then_inc(mean_ready, 1)

                            def var(c):
                                pe.wait_ge(squared, b * NCH + c + 1)
                                if c == 0:
                                    pe.wait_ge(rooted, 1 + b)
                                nc.tensor.matmul(psV[:], mean_col[:, c], sq[:, c % 2], start=(c == 0),
                                                 stop=(c == NCH - 1)).then_inc(summed, 1)

                            mean(0)
                            mean(1)
                            for c in range(NCH):
                                if c + 2 < NCH:
                                    mean(c + 2)
                                var(c)
                            pe.wait_ge(inverted, 1 + b + 1)
                            for c in range(NCH):
                                if c >= 3:
                                    pe.wait_ge(normed, 1 + b * NCH + c - 2)
                                else:
                                    pe.wait_ge(normed, 1 + b * NCH)
                                nc.tensor.matmul(psS[:, c % 3], spread[:, c], rstd, start=True,
                                                 stop=True).then_inc(spread_out, 1)

                    @block.scalar
                    def _(act):
                        act.sem_inc(rooted, 1)
                        with act.Fori(0, B, 1) as b:
                            for c in range(NCH):
                                act.wait_ge(centred, 1 + b * NCH + c + 1)
                                act.wait_ge(summed, 1 + b * NCH + max(c - 1, 0))
                                nc.scalar.activation(sq[:, c % 2], XN[:, b, 2 + c * CH:2 + (c + 1) * CH],
                                                     ACT.Square).then_inc(squared, 1)
                            act.wait_ge(summed, 1 + b * NCH + NCH)
                            act.wait_ge(inverted, 1 + b)
                            nc.scalar.activation(var_sb, psV[:], ACT.Sqrt, bias=eps_col[0:NCH]).then_inc(rooted, 1)

                    @block.vector
                    def _(dve):
                        dve.sem_inc(centred, 1)
                        dve.sem_inc(inverted, 1)
                        dve.sem_inc(normed, 1)
                        with dve.Fori(0, B, 1) as b:
                            for c in range(NCH):
                                dve.wait_ge(mean_ready, b * NCH + c + 1)
                                nc.vector.scalar_tensor_tensor(
                                    out=XN[:, b, 2 + c * CH:2 + (c + 1) * CH], in0=psM[:, c % 3], scalar=-1.0,
                                    in1=X[:, b, c * CH:(c + 1) * CH], op0=ALU.mult, op1=ALU.add).then_inc(centred, 1)
                            dve.wait_ge(rooted, 1 + b + 1)
                            dve.wait_ge(spread_out, 1 + b * NCH)
                            nc.vector.reciprocal(rstd, var_sb).then_inc(inverted, 1)
                            for c in range(NCH):
                                dve.wait_ge(spread_out, 1 + b * NCH + c + 1)
                                if c == 0:
                                    dve.wait_ge(squared, b * NCH + NCH)
                                v = XN[:, b, 2 + c * CH:2 + (c + 1) * CH]
                                nc.vector.tensor_tensor(v, psS[:, c % 3], v, ALU.mult).then_inc(normed, 1)

        layer_norm("ln1")

        st2 = ExitStack()
        with st2:
            used = [0]

            def carve(*dims):
                size = 1
                for d in dims:
                    size *= d
                a = used[0]
                used[0] += size
                assert used[0] <= SHARED
                names = "abcdef"[:len(dims)]
                spec = f"p ({' '.join(names)}) -> p {' '.join(names)}"
                return shared[:, a:a + size].rearrange(spec, **dict(zip(names, dims)))

            xs = carve(2, NW, 2, WIN)
            qs = carve(2, CH)
            ks = carve(2, CH)
            vs = carve(2, NW, P)
            pr = carve(2, NPAIR, HEADS, WIN)
            pT = carve(2, 2, NPAIR, P)
            at = carve(2, CH)
            keep_mask = carve(1, WIN)
            neg_mask = carve(1, WIN)
            red1 = sb("red1", [P, 2, 3, HEADS * NPAIR], on=st2)
            psS = ps("psS", [P, HEADS, CH], st2)
            psV = ps("psV", [P, 2, CH], st2)
            psO = ps("psO", [P, 2, CH], st2)

            chunk_in = sem("chunk_in")
            qk_mm = sem("qk_mm")
            q_out = sem("q_out")
            k_out = sem("k_out")
            v_mm = sem("v_mm")
            v_out = sem("v_out")
            v_zero = sem("v_zero")
            mask_fill = sem("mask_fill")
            s_mm = sem("s_mm")
            s_out = sem("s_out")
            masked = sem("masked")
            maxed = sem("maxed")
            shifted_ = sem("shifted_")
            exped = sem("exped")
            sumd = sem("sumd")
            recd = sem("recd")
            probs = sem("probs")
            pt_mm = sem("pt_mm")
            pt_out = sem("pt_out")
            o_mm = sem("o_mm")
            o_out = sem("o_out")
            y_mm = sem("y_mm")
            y_out = sem("y_out")

            NG2 = B * NCH // 2

            with nc.Block() as block:
                def where(i, s):
                    return (i * 2 + s) // NCH, (i * 2 + s) % NCH

                @block.gpsimd
                def _(pool):
                    nc.gpsimd.memset(keep_mask[:], 1.0).then_inc(mask_fill, 1)
                    nc.gpsimd.memset(neg_mask[:], 0.0).then_inc(mask_fill, 1)
                    pool.wait_ge(mask_fill, 2)
                    for w in range(2):
                        half = slice(w * WIN, (w + 1) * WIN)
                        for m, v in ((keep_mask, 0.0), (neg_mask, NEG)):
                            nc.gpsimd.affine_select(out=m[half], in_=m[half], compare_op=ALU.is_ge, fill=v, base=0,
                                                    pattern=[[0, 1], [-1, WIN]], channel_multiplier=1).then_inc(mask_fill, 1)
                    pool.wait_ge(mask_fill, 6)
                    nc.gpsimd.memset(vs[:], 0.0).then_inc(v_zero, 1)
                    for b in range(B):
                        with pool.Fori(0, NCH // 2, 1) as i:
                            g = (b * NCH // 2 + i) * 2
                            for s in range(2):
                                pool.wait_ge(v_mm, 1 + g)
                                src = XN[:, b, bass.ds(2 + (i * 2 + s) * CH, CH)].rearrange("p (n a t) -> p n a t", a=1, t=WIN)
                                nc.gpsimd.tensor_copy(xs[:, s], src.to_broadcast([P, NW, 2, WIN])).then_inc(chunk_in, 1)
                            for s in range(2):
                                pool.wait_ge(s_out, 1 + g + s + 1)
                                sc = pr[:, s].rearrange("p n h k -> p (n h) k")
                                nc.gpsimd.tensor_tensor(sc, sc, neg_mask.to_broadcast([P, NPAIR * HEADS, WIN]),
                                                        ALU.add).then_inc(masked, 1)

                @block.tensor
                def _(pe):
                    pe.sem_inc(v_mm, 1)
                    with pe.Fori(0, NG2, 1) as i:
                        g = i * 2

                        def scores(s):
                            pe.wait_ge(chunk_in, g + s + 1)
                            pe.wait_ge(y_out, 1 + g)
                            if s:
                                pe.wait_ge(q_out, g + 1)
                                pe.wait_ge(k_out, g + 1)
                            nc.tensor.matmul(psO[:, 0], wqkvT[:, 0], xs[:, s, :, 0], start=True, stop=True)
                            nc.tensor.matmul(psO[:, 1], wqkvT[:, 1], xs[:, s, :, 0], start=True, stop=True).then_inc(qk_mm, 1)
                            pe.wait_ge(pt_out, 1 + g)
                            if s:
                                pe.wait_ge(v_out, g + 1)
                            for w in range(NW):
                                both = xs[:, s, w].rearrange("p a t -> p (a t)")
                                last = nc.tensor.matmul(psV[:, w // 4, (w % 4) * P:(w % 4 + 1) * P], both,
                                                        wqkvT[:, 2], start=True, stop=True)
                            last.then_inc(v_mm, 1)
                            pe.wait_ge(q_out, g + s + 1)
                            pe.wait_ge(k_out, g + s + 1)
                            pe.wait_ge(s_out, 1 + g)
                            for n in range(NPAIR):
                                for w in range(2):
                                    for h in range(HEADS):
                                        tok = slice((2 * n + w) * WIN, (2 * n + w + 1) * WIN)
                                        hp = slice(h * HD, (h + 1) * HD)
                                        col = (s * NPAIR + n) * WIN
                                        last = nc.tensor.matmul(psS[w * WIN:(w + 1) * WIN, h, col:col + WIN],
                                                                qs[hp, s, tok], ks[hp, s, tok], start=True, stop=True)
                            last.then_inc(s_mm, 1)

                        def heads(s):
                            pe.wait_ge(probs, g + s + 1)
                            pe.wait_ge(v_out, g + 2)
                            pe.wait_ge(pt_out, 1 + g + s)
                            for a in range(2):
                                for n in range(NPAIR):
                                    last = nc.tensor.transpose(psV[:, a, n * P:(n + 1) * P],
                                                               pr[:, s, n, 2 * a:2 * a + 2].rearrange("p h k -> p (h k)"), ident[:])
                            last.then_inc(pt_mm, 1)
                            pe.wait_ge(pt_out, 1 + g + s + 1)
                            for n in range(NPAIR):
                                for w in range(2):
                                    for a in range(2):
                                        hp = slice(a * 2 * HD, (a + 1) * 2 * HD)
                                        tok = slice((2 * n + w) * WIN, (2 * n + w + 1) * WIN)
                                        last = nc.tensor.matmul(psO[hp, 1, tok], vs[:, s, 2 * n + w, hp],
                                                                pT[:, s, a, n, w * WIN:(w + 1) * WIN],
                                                                start=True, stop=True)
                            last.then_inc(o_mm, 1)

                        def project(s):
                            pe.wait_ge(o_out, g + s + 1)
                            pe.wait_ge(y_out, 1 + g + s)
                            nc.tensor.matmul(psO[:, 0], wprojT[:], at[:, s], start=True, stop=True).then_inc(y_mm, 1)

                        scores(0)
                        scores(1)
                        heads(0)
                        project(0)
                        heads(1)
                        project(1)

                @block.scalar
                def _(act):
                    act.sem_inc(pt_out, 1)
                    act.wait_ge(v_zero, 1)
                    with act.Fori(0, NG2, 1) as i:
                        g = i * 2
                        for s in range(2):
                            act.wait_ge(qk_mm, g + s + 1)
                            nc.scalar.activation(qs[:, s], psO[:, 0], ACT.Copy, scale=HD ** -0.5).then_inc(q_out, 1)
                            act.wait_ge(v_mm, 1 + g + s + 1)
                            for j in range(2):
                                half = slice(j * WIN, (j + 1) * WIN)
                                dst = vs[half, s].rearrange("p w (a j c) -> p (w a) j c", a=2, j=2)[:, :, j]
                                src = psV[half].rearrange("p b (w a j c) -> p (b w a) j c", a=2, j=2, c=HD)[:, :, j]
                                last = nc.scalar.activation(dst, src, ACT.Copy)
                            last.then_inc(v_out, 1)
                        for s in range(2):
                            act.wait_ge(shifted_, g + s + 1)
                            nc.scalar.activation(pr[:, s], pr[:, s], ACT.Exp).then_inc(exped, 1)
                        for s in range(2):
                            act.wait_ge(pt_mm, g + s + 1)
                            nc.scalar.activation(pT[:, s].rearrange("p a n q -> p a (n q)"), psV[:], ACT.Copy).then_inc(pt_out, 1)
                            act.wait_ge(o_mm, g + s + 1)
                            nc.scalar.activation(at[:, s], psO[:, 1], ACT.Copy).then_inc(o_out, 1)

                @block.vector
                def _(dve):
                    dve.sem_inc(y_out, 1)
                    dve.sem_inc(s_out, 1)
                    dve.wait_ge(mask_fill, 6)
                    for b in range(B):
                        with dve.Fori(0, NCH // 2, 1) as i:
                            g = (b * NCH // 2 + i) * 2
                            rows = [pr[:, s].rearrange("p n h k -> p (n h) k") for s in range(2)]

                            def spread_row(v):
                                return v.rearrange("p (m a) -> p m a", a=1).to_broadcast([P, HEADS * NPAIR, WIN])

                            def keys_out(s):
                                dve.wait_ge(qk_mm, g + s + 1)
                                nc.vector.tensor_copy(ks[:, s], psO[:, 1]).then_inc(k_out, 1)

                            def mask(s):
                                dve.wait_ge(s_mm, g + s + 1)
                                src = psS[:, :, s * NPAIR * WIN:(s + 1) * NPAIR * WIN].rearrange("p h (n k) -> p h n k", k=WIN)
                                keep = keep_mask.rearrange("p (a b) k -> p a b k", a=1).to_broadcast([P, HEADS, NPAIR, WIN])
                                nc.vector.tensor_tensor(pr[:, s].rearrange("p n h k -> p h n k"), src, keep,
                                                        ALU.mult).then_inc(s_out, 1)

                            def shift(s):
                                dve.wait_ge(masked, g + s + 1)
                                nc.vector.tensor_reduce(red1[:, s, 0], rows[s], AX.X, ALU.max).then_inc(maxed, 1)
                                dve.wait_ge(maxed, g + s + 1)
                                nc.vector.tensor_tensor(rows[s], rows[s], spread_row(red1[:, s, 0]),
                                                        ALU.subtract).then_inc(shifted_, 1)

                            def normalise(s):
                                dve.wait_ge(exped, g + s + 1)
                                nc.vector.tensor_reduce(red1[:, s, 1], rows[s], AX.X, ALU.add).then_inc(sumd, 1)
                                dve.wait_ge(sumd, g + s + 1)
                                nc.vector.reciprocal(red1[:, s, 2], red1[:, s, 1]).then_inc(recd, 1)
                                dve.wait_ge(recd, g + s + 1)
                                nc.vector.tensor_tensor(rows[s], rows[s], spread_row(red1[:, s, 2]),
                                                        ALU.mult).then_inc(probs, 1)

                            keys_out(0)
                            mask(0)
                            keys_out(1)
                            shift(0)
                            mask(1)
                            normalise(0)
                            shift(1)
                            normalise(1)
                            for s in range(2):
                                dve.wait_ge(y_mm, g + s + 1)
                                xv = X[:, b, bass.ts(i * 2 + s, CH)]
                                nc.vector.scalar_tensor_tensor(out=xv, in0=psO[:, 0], scalar=bproj[:], in1=xv,
                                                               op0=ALU.add, op1=ALU.add).then_inc(y_out, 1)

        layer_norm("ln2")

        U = shared[:].bitcast(F16).rearrange("p (b q n h c) -> p b q n h c", b=B, q=2, n=NBLK, h=2)
        SEGS = []
        for A in range(NGRP):
            cuts = sorted({0, CH} | {HALF // 2 ** e - A * CH for e in range(NE) if 0 < HALF // 2 ** e - A * CH < CH})
            SEGS.append([(c0, c1, sum(HALF // 2 ** e > A * CH + c0 for e in range(NE))) for c0, c1 in zip(cuts, cuts[1:])])

        st3 = ExitStack()
        with st3:
            mu = sb("mu", [P, NE, AR, P], on=st3)
            psA = ps("psA3", [P, 3, CH], st3)
            psU = ps("psU3", [P, 3, 4, P], st3)
            mu_in = sem("mu_in")
            mu_ready = sem("mu_ready")
            ar_mm = sem("ar_mm")
            ar_out = sem("ar_out")
            ut_mm = sem("ut_mm")
            u_hi = sem("u_hi")
            u_lo = sem("u_lo")
            AG = 2 * NGRP
            UG = 2 * NBLK // 4

            with nc.Block() as block:
                @block.sync
                def _(sp):
                    sp.dma_start(mu[:], m_u.rearrange("i a d e -> d i a e")).then_inc(mu_in, 16)
                    sp.wait_ge(mu_in, 16)

                @block.tensor
                def _(pe):
                    pe.wait_ge(mu_ready, NE)
                    for b in range(B):
                        for t in range(AG):
                            par, A = t // NGRP, t % NGRP
                            pe.wait_ge(ar_out, b * AG + (t - 2 if t >= 3 else 0))
                            for si, (c0, c1, ne) in enumerate(SEGS[A]):
                                for a in range(AR):
                                    lo = 2 + 2 * (A * CH + c0) + par - a
                                    last = nc.tensor.matmul(psA[:, t % 3, c0:c1], mu[:, ne - 1, a],
                                                            XN[:, b, lo:lo + 2 * (c1 - c0) - 1:2],
                                                            start=(a == 0), stop=(a == AR - 1))
                            last.then_inc(ar_mm, 1)
                            for r in (2 * t, 2 * t + 1) if UG == 2 * AG else (t,):
                                pe.wait_ge(u_lo, b * UG + (r - 2 if r >= 3 else 0))
                                for j in range(4):
                                    rp, rb = (4 * r + j) // NBLK, (4 * r + j) % NBLK
                                    first = 2 + rp + 2 * P * rb
                                    last = nc.tensor.transpose(psU[:, r % 3, j], XN[:, b, first:first + 2 * P - 1:2], ident[:])
                                last.then_inc(ut_mm, 1)

                @block.scalar
                def _(act):
                    for b in range(B):
                        for r in range(UG):
                            rp, rb = 4 * r // NBLK, 4 * r % NBLK
                            act.wait_ge(ut_mm, b * UG + r + 1)
                            nc.scalar.activation(U[:, b, rp, rb:rb + 4, 0], psU[:, r % 3], ACT.Copy,
                                                 scale=U_SCALE).then_inc(u_hi, 1)

                @block.vector
                def _(dve):
                    dve.wait_ge(mu_in, 16)
                    nc.vector.tensor_scalar(mu[:, 0], mu[:, 0], gate[:, 0:1], None, ALU.mult).then_inc(mu_ready, 1)
                    for e in range(1, NE):
                        dve.wait_ge(mu_ready, e)
                        nc.vector.scalar_tensor_tensor(out=mu[:, e], in0=mu[:, e], scalar=gate[:, e:e + 1],
                                                       in1=mu[:, e - 1], op0=ALU.mult, op1=ALU.add).then_inc(mu_ready, 1)
                    for b in range(B):
                        for t in range(AG):
                            par, A = t // NGRP, t % NGRP
                            dve.wait_ge(ar_mm, b * AG + t + 1)
                            lo = 2 * A * CH + par
                            xv = X[:, b, lo:lo + 2 * CH - 1:2]
                            nc.vector.tensor_tensor(xv, psA[:, t % 3], xv, ALU.add).then_inc(ar_out, 1)
                            for r in (2 * t, 2 * t + 1) if UG == 2 * AG else (t,):
                                rp, rb = 4 * r // NBLK, 4 * r % NBLK
                                dve.wait_ge(u_hi, b * UG + r + 1)
                                nc.vector.scalar_tensor_tensor(out=U[:, b, rp, rb:rb + 4, 1], in0=psU[:, r % 3],
                                                               scalar=U_SCALE, in1=U[:, b, rp, rb:rb + 4, 0],
                                                               op0=ALU.mult, op1=ALU.subtract).then_inc(u_lo, 1)

        stN.close()

        st4 = ExitStack()
        with st4:
            S = sb("S", [P, 2, 4, SW], F16, on=st4)
            V = sb("V", [P, B, 2, NGRP - 1, 2, 2, P], F16, on=st4)
            m_raw = sb("m_raw", [P, 2, NE, P], on=st4)
            mt = sb("mt", [P, 2, NE, P], on=st4)
            mk = sb("mk", [P, NE], on=st4)
            conv_sb = sb("conv_sb", [P, NGRP, CH], on=st4)
            w_sb = sb("w_sb", [P, 2, HC], on=st4)
            psC = ps("psC", [P, NGRP, CH], st4)
            psW = ps("psW", [P, 2, CH], st4)
            psY = ps("psY", [P, 2, CH], st4)

            f_in = [sem("f_in0"), sem("f_in1")]
            m_in = sem("m_in")
            v_step = sem("v_step")
            v_step_pool = sem("v_step_pool")
            v_ready = sem("v_ready")
            v_ready_pool = sem("v_ready_pool")
            mk_ready = sem("mk_ready")
            msum_ready = sem("msum_ready")
            mt_step = sem("mt_step")
            c_mm = sem("c_mm")
            w_mm = sem("w_mm")
            w_out = sem("w_out")
            c_out_act = sem("c_out_act")
            c_out_dve = sem("c_out_dve")
            m_mm = sem("m_mm")
            y_added = sem("y_added")
            stored = sem("stored")
            ITEMS = B * 2 * NGRP
            FIRSTS = ITEMS // NGRP
            LATER = ITEMS - FIRSTS
            V_TMP = (NGRP - 1) * HC
            ITEM = [(n // (2 * NGRP), n // NGRP % 2, n % NGRP) for n in range(ITEMS)]

            def later(n):
                return n // NGRP * (NGRP - 1) + max(n % NGRP - 1, 0)

            def v_pieces(eng, ops, batches, tmp, step, ready):
                t = tmp.rearrange("p (g i c) -> p g i c", g=NGRP - 1, i=2)
                n = 0
                for b in batches:
                    for par in range(2):
                        u = U[:, b, par, 0:NBLK - 4].rearrange("p (g a i) h c -> p a h g i c", a=2, i=2)
                        v = V[:, b, par].rearrange("p g i h c -> p h g i c")
                        ops.tensor_tensor(t, u[:, 0, 0], u[:, 1, 0], ALU.subtract).then_inc(step, 1)
                        eng.wait_ge(step, n + 1)
                        ops.tensor_tensor(t, t, u[:, 0, 1], ALU.add).then_inc(step, 1)
                        eng.wait_ge(step, n + 2)
                        ops.tensor_tensor(t, t, u[:, 1, 1], ALU.subtract).then_inc(step, 1)
                        eng.wait_ge(step, n + 3)
                        ops.tensor_copy(v[:, 0], t).then_inc(step, 1)
                        eng.wait_ge(step, n + 4)
                        ops.tensor_tensor(v[:, 1], t, v[:, 0], ALU.subtract).then_inc(step, 1)
                        n += 5
                        eng.wait_ge(step, n)
                eng.sem_inc(ready, 1)

            with nc.Block() as block:
                @block.gpsimd
                def _(pool):
                    def load_lines(q, at):
                        pool.dma_start(S[:, q], bass.AP(lines.tensor, at, [[1, P], [LINE, 4], [1, SW]])).then_inc(f_in[q], 16)

                    def load_matrices(at):
                        for sign, m in enumerate((m_plus, m_minus)):
                            pool.dma_start(m_raw[:, sign], bass.AP(m.tensor, at, [[P, P], [NK * P * P, NE], [1, P]])).then_inc(m_in, 16)

                    load_lines(0, 0)
                    load_matrices(0)
                    load_lines(1, 4 * LINE)
                    v_pieces(pool, nc.gpsimd, (2, 3), mt[:].rearrange("p q e c -> p (q e c)")[:, 0:V_TMP], v_step_pool, v_ready_pool)
                    with pool.Fori(1, NK, 1) as k:
                        pool.wait_ge(c_mm, (2 * k - 1) * ITEMS)
                        load_lines(0, (2 * k) * (4 * LINE))
                        pool.wait_ge(msum_ready, 2 * k)
                        load_matrices(k * (P * P))
                        pool.wait_ge(c_mm, 2 * k * ITEMS)
                        load_lines(1, (2 * k + 1) * (4 * LINE))

                @block.sync
                def _(sp):
                    sp.wait_ge(y_added, 2 + 2 * NK * ITEMS)
                    for b in range(B):
                        sp.dma_start(out_v[:, b], X[:, b]).then_inc(stored, 16)
                    sp.wait_ge(stored, 16 * B)

                @block.tensor
                def _(pe):
                    pe.sem_inc(m_mm, NGRP)

                    def phase(k, q):
                        f = 2 * k + q

                        def triple(out, blocks, which, y, width, first, final):
                            z = HALF - y
                            stop = z - width
                            for ul, fl in ((0, 0), (1, 0), (0, 1)):
                                last = nc.tensor.matmul(out, blocks[:, ul],
                                                        S[:, q, which + fl, z:(stop if stop >= 0 else None):-1],
                                                        start=(first and ul == 0 and fl == 0), stop=(final and fl == 1),
                                                        skip_group_check=True)
                            return last

                        def conv(n):
                            b, par, A = ITEM[n]
                            src = par ^ q
                            shift = 0 if (q == 1 and par == 0) else 1
                            if A:
                                pe.wait_ge(w_out, f * LATER + later(n) + 1)
                                for a in range(A):
                                    for i in range(2):
                                        last = triple(psW[:, later(n) % 2, 0:HC], V[:, b, src, a, i], 0,
                                                      shift + (A - a) * CH - i * P, HC,
                                                      a == 0 and i == 0, a == A - 1 and i == 1)
                                last.then_inc(w_mm, 1)
                            if A:
                                pe.wait_ge(c_out_dve, f * LATER + n // NGRP * (NGRP - 1) + A)
                            else:
                                pe.wait_ge(c_out_act, 1 + f * FIRSTS + n // NGRP)
                            for i in range(4):
                                last = triple(psC[:, A, i * P:], U[:, b, src, 4 * A + i], 0, shift, CH - i * P, i == 0, i == 3)
                            for a in range(A):
                                for i in range(2):
                                    triple(psC[:, A, 0:HC], U[:, b, src, 4 * a + 2 + i], 2,
                                           shift + (A - a) * CH - i * P, HC, False, False)
                                    last = triple(psC[:, A, HC:], U[:, b, src, 4 * a + i], 2,
                                                  shift + (A - a) * CH + HC - i * P, HC, False, True)
                            last.then_inc(c_mm, 1)

                        def mixdown(n):
                            b, par, A = ITEM[n]
                            if A:
                                pe.wait_ge(c_out_dve, NGRP - 1 + f * LATER + later(n) + 1)
                            else:
                                pe.wait_ge(c_out_act, 1 + f * FIRSTS + n // NGRP + 1)
                            pe.wait_ge(y_added, f * ITEMS + n + 1)
                            for si, (c0, c1, ne) in enumerate(SEGS[A]):
                                last = nc.tensor.matmul(psY[:, n % 2, c0:c1], mt[:, q, ne - 1],
                                                        conv_sb[:, A, c0:c1], start=(si == 0),
                                                        stop=True, skip_group_check=True)
                            last.then_inc(m_mm, 1)

                        pe.wait_ge(f_in[q], 16 * k + 16)
                        conv(0)
                        conv(1)
                        pe.wait_ge(mt_step, 1 + f * NE + NE)
                        for n in range(2, ITEMS):
                            mixdown(n - 2)
                            conv(n)
                        mixdown(ITEMS - 2)
                        mixdown(ITEMS - 1)

                    pe.wait_ge(v_ready, 1)
                    pe.wait_ge(v_ready_pool, 1)
                    with pe.Fori(0, NK, 1) as k:
                        phase(k, 0)
                        phase(k, 1)

                @block.scalar
                def _(act):
                    act.sem_inc(c_out_act, 1)
                    act.sem_inc(w_out, 2)
                    with act.Fori(0, NK, 1) as k:
                        for q in range(2):
                            f = 2 * k + q
                            for n in range(ITEMS):
                                if n % NGRP == 0:
                                    act.wait_ge(c_mm, f * ITEMS + n + 1)
                                    act.wait_ge(m_mm, f * ITEMS + n + 1)
                                    nc.scalar.activation(conv_sb[:, 0], psC[:, 0], ACT.Copy).then_inc(c_out_act, 1)
                                else:
                                    act.wait_ge(w_mm, f * LATER + later(n) + 1)
                                    act.wait_ge(c_out_dve, NGRP - 1 + f * LATER + max(later(n) - 1, 0))
                                    nc.scalar.activation(w_sb[:, later(n) % 2], psW[:, later(n) % 2, 0:HC],
                                                         ACT.Copy).then_inc(w_out, 1)

                @block.vector
                def _(dve):
                    v_pieces(dve, nc.vector, (0, 1), conv_sb[:].rearrange("p a c -> p (a c)")[:, 0:V_TMP], v_step, v_ready)
                    dve.wait_ge(v_ready_pool, 1)
                    dve.sem_inc(c_out_dve, NGRP - 1)
                    dve.sem_inc(y_added, 2)
                    dve.sem_inc(mt_step, 1)
                    with dve.Fori(0, NK, 1) as k:
                        for q in range(2):
                            f = 2 * k + q

                            def mix_matrices():
                                dve.wait_ge(m_in, 32 * k + 32)
                                dve.wait_ge(mt_step, 1 + f * NE)
                                nc.vector.tensor_scalar(mk[:], mix[:, :, bass.ds(k, 1)].rearrange("p e a -> p (e a)"), 1.0, None,
                                                        ALU.mult).then_inc(mk_ready, 1)
                                nc.vector.tensor_tensor(mt[:, q], m_raw[:, 0], m_raw[:, 1],
                                                        ALU.subtract if q else ALU.add).then_inc(msum_ready, 1)
                                dve.wait_ge(mk_ready, f + 1)
                                dve.wait_ge(msum_ready, f + 1)
                                nc.vector.tensor_scalar(mt[:, q, 0], mt[:, q, 0], mk[:, 0:1], None, ALU.mult).then_inc(mt_step, 1)
                                for e in range(1, NE):
                                    dve.wait_ge(mt_step, 1 + f * NE + e)
                                    nc.vector.scalar_tensor_tensor(out=mt[:, q, e], in0=mt[:, q, e], scalar=mk[:, e:e + 1],
                                                                   in1=mt[:, q, e - 1], op0=ALU.mult, op1=ALU.add).then_inc(mt_step, 1)

                            def combine(n):
                                A = n % NGRP
                                dve.wait_ge(c_mm, f * ITEMS + n + 1)
                                dve.wait_ge(w_out, 2 + f * LATER + later(n) + 1)
                                dve.wait_ge(m_mm, f * ITEMS + n + 1)
                                w = w_sb[:, later(n) % 2]
                                nc.vector.tensor_tensor(conv_sb[:, A, 0:HC], psC[:, A, 0:HC], w, ALU.add)
                                nc.vector.tensor_tensor(conv_sb[:, A, HC:], psC[:, A, HC:], w,
                                                        ALU.subtract).then_inc(c_out_dve, 1)

                            def add(n):
                                b, par, A = ITEM[n]
                                dve.wait_ge(m_mm, NGRP + f * ITEMS + n + 1)
                                lo = 2 * A * CH + par
                                xv = X[:, b, lo:lo + 2 * CH - 1:2]
                                nc.vector.tensor_tensor(xv, psY[:, n % 2], xv, ALU.add).then_inc(y_added, 1)

                            mix_matrices()
                            for n in range(ITEMS):
                                if n % NGRP:
                                    combine(n)
                                if n >= 2:
                                    add(n - 2)
                            add(ITEMS - 2)
                            add(ITEMS - 1)


_INS = ['x', 'L0_conv_w_reduce', 'L0_conv_b_reduce', 'L0_conv_w_span', 'L0_conv_b_span', 'L1_attn_w_qkv',
        'L1_attn_w_proj', 'L1_attn_b_proj', 'L1_ffn_sigma', 'L1_ffn_phi', 'L1_ffn_M_u', 'L1_ffn_M_phi_plus',
        'L1_ffn_M_phi_minus', 'L1_ffn_log_weights', 'L1_ffn_gumbel']


def kernel(**inputs):
    import numpy as np
    import concourse.bacc as bacc
    from concourse.bass_utils import run_bass_kernel_spmd

    nc = bacc.Bacc("TRN2", target_bir_lowering=False, num_devices=1)
    arrays, args = {}, []
    for name in _INS:
        a = np.ascontiguousarray(inputs[name])
        arrays[f"in_{name}"] = a
        args.append(nc.dram_tensor(f"in_{name}", a.shape, mybir.dt.from_np(a.dtype), kind="ExternalInput").ap())
    out = nc.dram_tensor("out_x", inputs["x"].shape, F32, kind="ExternalOutput").ap()
    program(nc, *args, out)
    r = run_bass_kernel_spmd(nc, [arrays], core_ids=[0])
    return r.results[0]["out_x"]
```

```python
from contextlib import ExitStack

import concourse.bass as bass
from concourse import mybir

F32 = mybir.dt.float32
F16 = mybir.dt.float16
ALU = mybir.AluOpType
ACT = mybir.ActivationFunctionType
AX = mybir.AxisListType

P = 128
B = 4
IMG = 64
T = IMG * IMG
CH = 512
NCH = T // CH
ROWS = CH // IMG

KS = 7
DIL = 2
PAD = 6
GC = 8
CG = P // GC
CR = 32
TAPS = KS * KS
PW = IMG + 2 * PAD
POOL_TAPS = 4
PE_TAPS = KS - POOL_TAPS
PROD_ROWS = 4
KROWS = 3 * CR + 2
RED_SCALE = 256.0
SPAN_SCALE = 4096.0
GN_CH = 4
GN_EPS = 1e-5
LN_EPS = 1e-5

HEADS = 4
HD = P // HEADS
WIN = 64
NW = CH // WIN
NPAIR = NW // 2
NEG = -10000.0

NK = 16
NE = 4
AR = 3
HALF = T // 2
NBLK = HALF // P
NGRP = HALF // CH
PH_SCALE = 4096.0
U_SCALE = 256.0
HC = CH // 2
LINE = P + HALF
F_FROM = HALF - 2 * CH - HC
G_FROM = F_FROM - HC
F_W = HALF + 1 - F_FROM
G_W = HALF + P - CH + 1 - G_FROM
H_W = HALF + P - 2 * CH + 1


def program(nc, x, w_reduce, b_reduce, w_span, b_span, w_qkv, w_proj, b_proj,
            sigma, phi, m_u, m_plus, m_minus, log_weights, gumbel, out):
    x_v = x.rearrange("b c h w -> c b (h w)")
    out_v = out.rearrange("b c h w -> c b (h w)")
    lines = nc.dram_tensor("filter_lines", [NK, 2, 8, LINE], F16, kind="Internal").ap()

    top = ExitStack()
    with top:
        def sb(name, shape, dt=F32, on=top):
            return on.enter_context(nc.sbuf_tensor(name, shape, dt))

        def ps(name, shape, on):
            return on.enter_context(nc.psum_tensor(name, shape, F32))

        def sem(name):
            return top.enter_context(nc.semaphore(name))

        X = sb("X", [P, B, T])
        weights = sb("weights", [P, 8, P])
        ident = weights[:, 0]
        averager = weights[:, 1]
        gn_avg = weights[:, 2]
        eps_col = sb("eps_col", [P, 1])
        one_row = weights[0:1, 7]
        wqkvT = weights[:, 3:6]
        wprojT = weights[:, 6]
        bproj = sb("bproj", [P, 1])
        mix = sb("mix", [P, NE, NK])
        gate = sb("gate", [P, NE])

        st0 = ExitStack()
        with st0:
            flip = sb("flip", [P, P], on=st0)
            wq_raw = sb("wq_raw", [P, 3, P], on=st0)
            wp_raw = sb("wp_raw", [P, P], on=st0)
            gate_in = sb("gate_in", [P, 2, NE], on=st0)
            gate_t = sb("gate_t", [P, 8, NE], on=st0)
            gate_s = sb("gate_s", [P, 8], on=st0)
            sig_in = sb("sig_in", [P, 3, NK], on=st0)
            phi_in = sb("phi_in", [P, 32, NK], on=st0)
            phi_n = sb("phi_n", [P, 32, NK], on=st0)
            phi_m = sb("phi_m", [P, 6], on=st0)
            line32 = sb("line32", [NK, 2, HALF + HC + CH], on=st0)
            scratch = X[0:NK].rearrange("p b t -> p (b t)").rearrange("p (q z) -> p q z", q=2)
            g32 = scratch[:, :, 0:HALF]
            h32 = scratch[:, :, HALF:2 * HALF + HC]
            k32 = scratch[:, :, 2 * HALF + HC:3 * HALF + HC]
            line_sb = sb("line_sb", [NK, 2, 8, LINE], F16, on=st0)
            psA = ps("psA", [P, 4, P], st0)
            psB = ps("psB", [P, P], st0)
            psP = ps("psP", [P, 4, CH], st0)

            weights_in = sem("weights_in")
            gate_ld = sem("gate_ld")
            phi_ld = sem("phi_ld")
            consts = sem("consts")
            ident0 = sem("ident0")
            wT_ready = sem("wT_ready")
            phi_rowmax = sem("phi_rowmax")
            phi_maxT = sem("phi_maxT")
            phi_max = sem("phi_max")
            phi_bc = sem("phi_bc")
            phi_scaled = sem("phi_scaled")
            phi_T = sem("phi_T")
            line_part = sem("line_part")
            line_sum = sem("line_sum")
            line_hi = sem("line_hi")
            line_lo = sem("line_lo")
            line_lo_pool = sem("line_lo_pool")
            lines_out = sem("lines_out")
            v0 = sem("v0")
            expd = sem("expd")
            sigd = sem("sigd")

            with nc.Block() as block:
                @block.sync
                def _(sp):
                    sp.dma_start(phi_in[:], phi.rearrange("(a l) k -> a l k", a=P)).then_inc(phi_ld, 16)
                    sp.dma_start(wq_raw[:], w_qkv.rearrange("(t p) c -> p t c", p=P)).then_inc(weights_in, 16)
                    sp.dma_start(wp_raw[:], w_proj).then_inc(weights_in, 16)
                    sp.dma_start(gate_in[:, 0], bass.AP(log_weights.tensor, 0, [[0, P], [1, NE]])).then_inc(gate_ld, 16)
                    sp.dma_start(gate_in[:, 1], bass.AP(gumbel.tensor, 0, [[0, P], [1, NE]])).then_inc(gate_ld, 16)
                    sp.dma_start(sig_in[:, 0], bass.AP(sigma.tensor, 0, [[0, P], [1, NK]])).then_inc(gate_ld, 16)
                    sp.dma_start(bproj[:], b_proj.rearrange("(c a) -> c a", a=1)).then_inc(weights_in, 16)
                    sp.wait_ge(line_hi, 4)
                    sp.wait_ge(line_lo, 2)
                    sp.wait_ge(line_lo_pool, 2)
                    sp.dma_start(lines, line_sb[:]).then_inc(lines_out, 16)
                    sp.wait_ge(lines_out, 16)
                    sp.wait_ge(weights_in, 48)
                    sp.wait_ge(gate_ld, 48)

                @block.gpsimd
                def _(pool):
                    nc.gpsimd.memset(ident[:], 0.0).then_inc(ident0, 1)
                    nc.gpsimd.memset(gn_avg[:], 1.0 / GN_CH).then_inc(ident0, 1)
                    nc.gpsimd.memset(flip[:], 0.0).then_inc(ident0, 1)
                    pool.wait_ge(ident0, 3)
                    nc.gpsimd.affine_select(out=ident[:], in_=ident[:], compare_op=ALU.not_equal, fill=1.0,
                                            base=0, pattern=[[-1, P]], channel_multiplier=1).then_inc(consts, 1)
                    nc.gpsimd.affine_select(out=flip[:], in_=flip[:], compare_op=ALU.not_equal, fill=1.0,
                                            base=1 - P, pattern=[[1, P]], channel_multiplier=1).then_inc(consts, 1)
                    gv = gn_avg[:].rearrange("p (g r) -> p g r", r=GN_CH)
                    nc.gpsimd.affine_select(out=gv, in_=gv, compare_op=ALU.is_ge, fill=0.0, base=0,
                                            pattern=[[-GN_CH, P // GN_CH], [0, GN_CH]],
                                            channel_multiplier=1).then_inc(ident0, 1)
                    pool.wait_ge(ident0, 4)
                    nc.gpsimd.affine_select(out=gv, in_=gv, compare_op=ALU.is_ge, fill=0.0, base=GN_CH - 1,
                                            pattern=[[GN_CH, P // GN_CH], [0, GN_CH]],
                                            channel_multiplier=-1).then_inc(consts, 1)
                    nc.gpsimd.memset(averager[:], 1.0 / P).then_inc(consts, 1)
                    nc.gpsimd.memset(one_row[:], 1.0).then_inc(consts, 1)
                    nc.gpsimd.memset(eps_col[:], LN_EPS).then_inc(consts, 1)
                    nc.gpsimd.memset(line32[:, :, HALF:], 0.0).then_inc(consts, 1)
                    nc.gpsimd.memset(line_sb[:, :, :, HALF:], 0.0).then_inc(consts, 1)

                    pool.wait_ge(consts, 8)
                    pool.wait_ge(line_hi, 1)
                    nc.gpsimd.tensor_tensor(line_sb[:, :, 1, 0:HALF], line32[:, :, 0:HALF], line_sb[:, :, 0, 0:HALF],
                                            ALU.subtract).then_inc(line_lo_pool, 1)
                    pool.wait_ge(line_sum, 2)
                    pool.wait_ge(line_hi, 3)
                    pool.wait_ge(line_lo_pool, 1)
                    nc.gpsimd.tensor_tensor(line_sb[:, :, 5, 0:HALF], h32[:, :, 0:HALF], line_sb[:, :, 4, 0:HALF],
                                            ALU.subtract).then_inc(line_lo_pool, 1)

                @block.tensor
                def _(pe):
                    pe.wait_ge(consts, 8)
                    pe.wait_ge(weights_in, 48)
                    for t in range(3):
                        nc.tensor.transpose(psA[:, t], wq_raw[:, t], ident[:])
                    nc.tensor.transpose(psA[:, 3], wp_raw[:], ident[:]).then_inc(wT_ready, 1)
                    pe.wait_ge(phi_rowmax, 1)
                    nc.tensor.transpose(psB[0:1, :], phi_m[:, 0:1], ident[:]).then_inc(phi_maxT, 1)
                    pe.wait_ge(phi_max, 1)
                    nc.tensor.matmul(psB[:, 0:1], one_row[:], phi_m[0:1, 1:2], start=True, stop=True).then_inc(phi_bc, 1)
                    pe.wait_ge(phi_scaled, 1)
                    for r in range(8):
                        if r >= 4:
                            pe.wait_ge(line_part, r - 3)
                        for j in range(4):
                            slot = (1 - j // 2) * 2 + j % 2
                            last = nc.tensor.matmul(psP[0:NK, r % 4, slot * P:(slot + 1) * P], phi_n[:, 4 * r + j],
                                                    flip[:], start=True, stop=True)
                        last.then_inc(phi_T, 1)

                @block.scalar
                def _(act):
                    act.wait_ge(v0, 4)
                    nc.scalar.activation(gate_t[:, 2], gate_t[:, 1], ACT.Exp).then_inc(expd, 1)
                    act.wait_ge(gate_ld, 48)
                    nc.scalar.activation(sig_in[:, 1], sig_in[:, 0], ACT.Sqrt).then_inc(sigd, 1)
                    act.wait_ge(sigd, 1)
                    nc.scalar.activation(sig_in[:, 2], sig_in[:, 1], ACT.Sqrt).then_inc(sigd, 1)
                    act.wait_ge(consts, 8)
                    for r in range(8):
                        act.wait_ge(phi_T, r + 1)
                        for q in range(2):
                            src = psP[0:NK, r % 4, :].rearrange("p (j q a) -> p q j a", q=2, j=2)[:, q]
                            dst = line32[:, q, 0:HALF].rearrange("p (a l) -> p l a", l=16)[:, 14 - 2 * r:16 - 2 * r]
                            last = nc.scalar.activation(dst, src, ACT.Copy)
                        last.then_inc(line_part, 1)
                    act.wait_ge(line_part, 8)
                    nc.scalar.activation(line_sb[:, :, 0, 0:HALF], line32[:, :, 0:HALF], ACT.Copy).then_inc(line_hi, 1)
                    for n, src in enumerate((g32, h32[:, :, 0:HALF], k32)):
                        act.wait_ge(line_sum, n + 1)
                        nc.scalar.activation(line_sb[:, :, 2 * n + 2, 0:HALF], src, ACT.Copy).then_inc(line_hi, 1)

                @block.vector
                def _(dve):
                    n = [0]

                    def link(ins):
                        n[0] += 1
                        ins.then_inc(v0, 1)
                        dve.wait_ge(v0, n[0])

                    dve.wait_ge(gate_ld, 48)
                    link(nc.vector.tensor_tensor(gate_t[:, 0], gate_in[:, 0], gate_in[:, 1], ALU.add))
                    link(nc.vector.tensor_reduce(gate_s[:, 0:1], gate_t[:, 0], AX.X, ALU.max))
                    link(nc.vector.tensor_scalar(gate_t[:, 1], gate_t[:, 0], gate_s[:, 0:1], None, ALU.subtract))
                    link(nc.vector.memset(gate_s[:, 4:5], 1.0))
                    dve.wait_ge(expd, 1)
                    link(nc.vector.tensor_reduce(gate_s[:, 1:2], gate_t[:, 2], AX.X, ALU.add))
                    link(nc.vector.reciprocal(gate_s[:, 2:3], gate_s[:, 1:2]))
                    link(nc.vector.tensor_scalar(gate_t[:, 3], gate_t[:, 2], gate_s[:, 2:3], None, ALU.mult))
                    link(nc.vector.tensor_reduce(gate_s[:, 3:4], gate_t[:, 3], AX.X, ALU.max))
                    link(nc.vector.tensor_scalar(gate_t[:, 4], gate_t[:, 3], gate_s[:, 3:4], None, ALU.is_equal))
                    for i in range(NE):
                        link(nc.vector.tensor_tensor(gate_t[:, 5, i:i + 1], gate_t[:, 4, i:i + 1], gate_s[:, 4:5], ALU.mult))
                        link(nc.vector.tensor_tensor(gate_s[:, 4:5], gate_s[:, 4:5], gate_t[:, 5, i:i + 1], ALU.subtract))
                    link(nc.vector.tensor_tensor(gate_t[:, 6], gate_t[:, 5], gate_t[:, 3], ALU.subtract))
                    link(nc.vector.tensor_tensor(gate[:], gate_t[:, 6], gate_t[:, 3], ALU.add))
                    dve.wait_ge(phi_ld, 16)
                    nc.vector.tensor_reduce(phi_m[:, 0:1], phi_in[:], AX.XY, ALU.max,
                                            apply_absolute_value=True).then_inc(phi_rowmax, 1)
                    dve.wait_ge(phi_maxT, 1)
                    nc.vector.tensor_reduce(phi_m[0:1, 1:2], psB[0:1, :], AX.X, ALU.max).then_inc(phi_max, 1)
                    dve.wait_ge(phi_bc, 1)
                    link(nc.vector.tensor_scalar(phi_m[:, 2:3], psB[:, 0:1], 1e-30, None, ALU.max))
                    link(nc.vector.reciprocal(phi_m[:, 3:4], phi_m[:, 2:3]))
                    nc.vector.tensor_scalar(phi_n[:], phi_in[:], phi_m[:, 3:4], PH_SCALE, ALU.mult,
                                            ALU.mult).then_inc(phi_scaled, 1)
                    link(nc.vector.tensor_scalar(phi_m[:, 4:5], phi_m[:, 2:3], 1.0 / (PH_SCALE * U_SCALE), None, ALU.mult))
                    dve.wait_ge(sigd, 2)
                    for i in range(NE):
                        link(nc.vector.tensor_scalar(mix[:, i], sig_in[:, 2], gate[:, i:i + 1], phi_m[:, 4:5],
                                                     ALU.mult, ALU.mult))
                    dve.wait_ge(consts, 8)
                    dve.wait_ge(line_part, 8)
                    nc.vector.tensor_tensor(g32, line32[:, :, 0:HALF], line32[:, :, HC:HC + HALF], ALU.add).then_inc(line_sum, 1)
                    nc.vector.tensor_tensor(h32, line32[:, :, 0:HALF + HC], line32[:, :, CH:CH + HALF + HC],
                                            ALU.add).then_inc(line_sum, 1)
                    dve.wait_ge(line_sum, 2)
                    nc.vector.tensor_tensor(k32, h32[:, :, 0:HALF], h32[:, :, HC:HC + HALF], ALU.add).then_inc(line_sum, 1)
                    dve.wait_ge(line_hi, 2)
                    nc.vector.tensor_tensor(line_sb[:, :, 3, 0:HALF], g32, line_sb[:, :, 2, 0:HALF],
                                            ALU.subtract).then_inc(line_lo, 1)
                    dve.wait_ge(line_sum, 3)
                    dve.wait_ge(line_hi, 4)
                    nc.vector.tensor_tensor(line_sb[:, :, 7, 0:HALF], k32, line_sb[:, :, 6, 0:HALF],
                                            ALU.subtract).then_inc(line_lo, 1)
                    dve.wait_ge(wT_ready, 1)
                    nc.vector.tensor_copy(wqkvT[:], psA[:, 0:3])
                    link(nc.vector.tensor_copy(wprojT[:], psA[:, 3]))

        st1 = ExitStack()
        with st1:
            xpad = sb("xpad", [P, PW, PW], on=st1)
            red = sb("red", [KROWS, T], F16, on=st1)
            tapw = sb("tapw", [KROWS, TAPS, P], F16, on=st1)
            ws_raw = sb("ws_raw", [98, 4, 3, CR], on=st1)
            ws32 = sb("ws32", [KROWS, GC * TAPS], on=st1)
            ws_hi = sb("ws_hi", [KROWS, GC * TAPS], F16, on=st1)
            ws16 = sb("ws16", [KROWS, GC * TAPS], F16, on=st1)
            low_row = sb("low_row", [P, 1], on=st1)
            span_m = sb("span_m", [P, 4], on=st1)
            wr_raw = sb("wr_raw", [3 * CR, P], on=st1)
            wr_n = sb("wr_n", [3 * CR, P], on=st1)
            wrT = sb("wrT", [P, 3 * CR], on=st1)
            bred = sb("bred", [3 * CR, 2], on=st1)
            bred_n = sb("bred_n", [3 * CR, 1], on=st1)
            rnorm = sb("rnorm", [3 * CR, 4], on=st1)
            prod = sb("prod", [P, PROD_ROWS, POOL_TAPS, ROWS, IMG], on=st1)
            sums = sb("sums", [P, POOL_TAPS, ROWS, IMG], on=st1)
            direct = sb("direct", [P, KS, PE_TAPS, ROWS, IMG], on=st1)
            bn = sb("bn", [P, B, NCH, 6], on=st1)
            cstat = sb("cstat", [P, B, 2], on=st1)
            dstat = sb("dstat", [P, 6, B], on=st1)
            taps_ps = ps("taps_ps", [P, KS, CH], st1)
            psI = ps("psI", [P, CH], st1)

            x_in = sem("x_in")
            cw_in = sem("cw_in")
            wr_scaled = sem("wr_scaled")
            wr_T = sem("wr_T")
            ws_T = sem("ws_T")
            wr_ready = sem("wr_ready")
            span_rowmax = sem("span_rowmax")
            span_maxT = sem("span_maxT")
            span_max = sem("span_max")
            span_bc = sem("span_bc")
            tap_ready = sem("tap_ready")
            low_rows = sem("low_rows")
            gn_a = sem("gn_a")
            gn_b = sem("gn_b")
            v1 = sem("v1")
            frame = sem("frame")
            gmean = sem("gmean")
            gvar = sem("gvar")
            gstd = sem("gstd")
            gnorm = sem("gnorm")
            xpad_ready = sem("xpad_ready")
            red_mm = sem("red_mm")
            red_hi = sem("red_hi")
            red_ready = sem("red_ready")
            kern = sem("kern")
            mul = sem("mul")
            pool_added = sem("pool_added")
            summed = sem("summed")
            x_added = sem("x_added")

            ADDS = KS - 1
            SUMMED = KS * PE_TAPS + POOL_TAPS
            EARLY = PE_TAPS * 5
            LATE = SUMMED - EARLY
            ADD_AT = 2 * PE_TAPS + 8

            with nc.Block() as block:
                @block.sync
                def _(sp):
                    for b in range(B):
                        sp.dma_start(X[:, b], x_v[:, b]).then_inc(x_in, 16)
                    for n in range(3):
                        sp.dma_start(wr_raw[n * CR:(n + 1) * CR], w_reduce).then_inc(cw_in, 16)
                        sp.dma_start(bred[n * CR:(n + 1) * CR, 0:1], b_reduce.rearrange("(c a) -> c a", a=1)).then_inc(cw_in, 16)
                        sp.dma_start(ws_raw[:, :, n], w_span.rearrange("(t r) o -> r t o", r=98)).then_inc(cw_in, 16)
                    sp.dma_start(ws32[3 * CR:KROWS, :], bass.AP(b_span.tensor, 0, [[0, 2], [1, GC * TAPS]])).then_inc(cw_in, 16)

                @block.gpsimd
                def _(pool):
                    nc.gpsimd.memset(xpad[:], 0.0).then_inc(frame, 1)
                    pool.wait_ge(frame, 1)
                    nc.gpsimd.memset(red[3 * CR:KROWS, :], RED_SCALE).then_inc(frame, 1)
                    pool.wait_ge(frame, 2)
                    nc.gpsimd.memset(low_row[:], 0.0).then_inc(low_rows, 1)
                    pool.wait_ge(low_rows, 1)
                    nc.gpsimd.memset(low_row[CR:2 * CR], -1.0).then_inc(low_rows, 1)
                    pool.wait_ge(low_rows, 2)
                    nc.gpsimd.affine_select(out=low_row[:], in_=low_row[:], compare_op=ALU.not_equal, fill=-1.0,
                                            base=1 - KROWS, pattern=[[0, 1]], channel_multiplier=1).then_inc(low_rows, 1)
                    pool.sem_inc(pool_added, ADDS)
                    for b in range(B):
                        with pool.Fori(0, NCH, 1) as c:
                            g = b * NCH + c
                            for i in range(1, KS):
                                pool.wait_ge(mul, KS + (g * KS + i) * KS + POOL_TAPS)
                                if i == 1:
                                    pool.wait_ge(summed, (g + 1) * SUMMED)
                                else:
                                    pool.wait_ge(pool_added, (g + 1) * ADDS + i - 1)
                                nc.gpsimd.tensor_tensor(sums[:], prod[:, 0] if i == 1 else sums[:], prod[:, i % PROD_ROWS],
                                                        ALU.add).then_inc(pool_added, 1)

                @block.tensor
                def _(pe):
                    pe.sem_inc(summed, SUMMED)
                    pe.wait_ge(cw_in, 160)
                    for t in range(4):
                        last = nc.tensor.transpose(taps_ps[0:3 * CR, 0, t * 98:(t + 1) * 98],
                                                   ws_raw[:, t].rearrange("r n o -> r (n o)"), ident[0:98, 0:98])
                    last.then_inc(ws_T, 1)
                    pe.wait_ge(wr_scaled, 1)
                    nc.tensor.transpose(psI[:, 0:3 * CR], wr_n[:], ident[0:3 * CR, 0:3 * CR]).then_inc(wr_T, 1)
                    pe.wait_ge(span_rowmax, 1)
                    nc.tensor.transpose(taps_ps[0:1, 3, 0:KROWS], span_m[0:KROWS, 0:1], ident[0:KROWS, 0:KROWS]).then_inc(span_maxT, 1)
                    pe.wait_ge(span_max, 1)
                    nc.tensor.matmul(taps_ps[:, 4, 0:1], one_row[:], span_m[0:1, 1:2], start=True, stop=True).then_inc(span_bc, 1)
                    pe.wait_ge(gn_a, 1)
                    nc.tensor.matmul(taps_ps[:, 1, 0:B], gn_avg[:], dstat[:, 0], start=True, stop=True).then_inc(gmean, 1)
                    pe.wait_ge(gn_b, 1)
                    nc.tensor.matmul(taps_ps[:, 2, 0:B], gn_avg[:], dstat[:, 2], start=True, stop=True).then_inc(gvar, 1)
                    pe.wait_ge(wr_ready, 1)
                    pe.wait_ge(tap_ready, 1)
                    pe.wait_ge(gnorm, 1)

                    def sum_up(g, m):
                        if m < KS * PE_TAPS:
                            i, j = m // PE_TAPS, m % PE_TAPS
                            operand = direct[:, i, j]
                            pe.wait_ge(mul, KS + (g * KS + i) * KS + POOL_TAPS + j + 1)
                        else:
                            operand = sums[:, m - KS * PE_TAPS]
                            pe.wait_ge(pool_added, ADDS + (g + 1) * ADDS)
                        if m == 0:
                            pe.wait_ge(x_added, g + 1)
                        nc.tensor.matmul(psI[:], ident[:], operand.rearrange("p r w -> p (r w)"), start=(m == 0),
                                         stop=(m == SUMMED - 1), skip_group_check=True).then_inc(summed, 1)

                    def chunk(b, c, after_another):
                        g = b * NCH + c
                        for t in range(TAPS):
                            pe.wait_ge(mul, g * TAPS + t + 1)
                            nc.tensor.matmul(taps_ps[:, t % KS], tapw[:, t], red[:, bass.ts(c, CH)],
                                             start=True, stop=True, skip_group_check=True).then_inc(kern, 1)
                            n = t // 2 if t % 2 else (SUMMED - 1 if t == TAPS - 1 else None)
                            if n is None:
                                continue
                            if n >= LATE:
                                sum_up(g, n - LATE)
                            elif after_another:
                                sum_up(g - 1, EARLY + n)

                    for b in range(B):
                        pe.wait_ge(xpad_ready, b + 1)
                        for c in range(NCH):
                            if c >= KS:
                                pe.wait_ge(red_ready, b * NCH + c - KS + 1)
                            nc.tensor.matmul(taps_ps[0:3 * CR, c % KS], wrT[:],
                                             xpad[:, PAD + c * ROWS:PAD + (c + 1) * ROWS, PAD:PAD + IMG],
                                             start=True, stop=True, skip_group_check=True).then_inc(red_mm, 1)
                        pe.wait_ge(red_ready, (b + 1) * NCH)
                        chunk(b, 0, b > 0)
                        with pe.Fori(1, NCH, 1) as c:
                            chunk(b, c, True)
                    for n in range(LATE):
                        sum_up(B * NCH - 1, EARLY + n)

                @block.scalar
                def _(act):
                    act.wait_ge(gn_b, 2)
                    nc.scalar.activation(dstat[:, 3], dstat[:, 5], ACT.Sqrt, bias=eps_col[:]).then_inc(gstd, 1)
                    act.wait_ge(frame, 2)
                    act.wait_ge(gnorm, 1)
                    act.wait_ge(x_in, 16 * B)
                    act.wait_ge(wr_scaled, 1)
                    for b in range(B):
                        if b:
                            act.wait_ge(mul, KS + b * NCH * TAPS)
                        nc.scalar.activation(xpad[:, PAD:PAD + IMG, PAD:PAD + IMG],
                                             X[:, b].rearrange("p (h w) -> p h w", w=IMG), ACT.Identity,
                                             bias=dstat[:, 4, b:b + 1], scale=dstat[:, 2, b:b + 1]).then_inc(xpad_ready, 1)
                        for c in range(NCH):
                            act.wait_ge(red_mm, b * NCH + c + 1)
                            nc.scalar.activation(red[0:3 * CR, c * CH:(c + 1) * CH], taps_ps[0:3 * CR, c % KS], ACT.Identity,
                                                 bias=bred_n[:]).then_inc(red_hi, 1)

                @block.vector
                def _(dve):
                    dve.sem_inc(mul, KS)
                    dve.sem_inc(x_added, 1)
                    n = [0]

                    def link(ins):
                        n[0] += 1
                        ins.then_inc(v1, 1)
                        dve.wait_ge(v1, n[0])

                    dve.wait_ge(cw_in, 160)
                    link(nc.vector.tensor_reduce(rnorm[:, 0:1], wr_raw[:], AX.X, ALU.add, apply_absolute_value=True))
                    link(nc.vector.tensor_scalar(bred[:, 1:2], bred[:, 0:1], -1.0, None, ALU.mult))
                    link(nc.vector.tensor_tensor(rnorm[:, 1:2], bred[:, 0:1], bred[:, 1:2], ALU.max))
                    link(nc.vector.tensor_tensor(rnorm[:, 2:3], rnorm[:, 0:1], rnorm[:, 1:2], ALU.add))
                    link(nc.vector.tensor_scalar(rnorm[:, 2:3], rnorm[:, 2:3], 1e-30, None, ALU.max))
                    link(nc.vector.reciprocal(rnorm[:, 3:4], rnorm[:, 2:3]))
                    nc.vector.tensor_scalar(wr_n[:], wr_raw[:], rnorm[:, 3:4], RED_SCALE, ALU.mult, ALU.mult)
                    nc.vector.tensor_scalar(bred_n[:], bred[:, 0:1], rnorm[:, 3:4], RED_SCALE, ALU.mult,
                                            ALU.mult).then_inc(wr_scaled, 1)
                    dve.wait_ge(ws_T, 1)
                    link(nc.vector.tensor_scalar(ws32[0:3 * CR, :], taps_ps[0:3 * CR, 0, 0:GC * TAPS], rnorm[:, 2:3], None,
                                                 ALU.mult))
                    nc.vector.tensor_reduce(span_m[0:KROWS, 0:1], ws32[:], AX.X, ALU.max,
                                            apply_absolute_value=True).then_inc(span_rowmax, 1)
                    dve.wait_ge(wr_T, 1)
                    nc.vector.tensor_copy(wrT[:], psI[:, 0:3 * CR]).then_inc(wr_ready, 1)
                    dve.wait_ge(span_maxT, 1)
                    nc.vector.tensor_reduce(span_m[0:1, 1:2], taps_ps[0:1, 3, 0:KROWS], AX.X, ALU.max).then_inc(span_max, 1)
                    dve.wait_ge(span_bc, 1)
                    link(nc.vector.tensor_scalar(span_m[:, 2:3], taps_ps[:, 4, 0:1], 1e-30, None, ALU.max))
                    link(nc.vector.reciprocal(span_m[:, 3:4], span_m[:, 2:3]))
                    link(nc.vector.tensor_scalar(ws32[:], ws32[:], span_m[0:KROWS, 3:4], SPAN_SCALE, ALU.mult, ALU.mult))
                    link(nc.vector.tensor_scalar(span_m[:, 2:3], span_m[:, 2:3], 1.0 / (RED_SCALE * SPAN_SCALE), None,
                                                 ALU.mult))
                    link(nc.vector.tensor_copy(ws_hi[:], ws32[:]))
                    dve.wait_ge(low_rows, 3)
                    link(nc.vector.scalar_tensor_tensor(out=ws16[:], in0=ws_hi[:], scalar=low_row[0:KROWS], in1=ws32[:],
                                                        op0=ALU.mult, op1=ALU.add))
                    for k in range(TAPS):
                        src = ws16[:].rearrange("p (g k) -> p g k", k=TAPS)[:, :, k:k + 1]
                        last = nc.vector.tensor_copy(tapw[:, k].rearrange("p (g c) -> p g c", c=CG),
                                                     src.to_broadcast([KROWS, GC, CG]))
                    last.then_inc(tap_ready, 1)

                    dve.wait_ge(x_in, 16 * B)
                    for b in range(B):
                        for c in range(NCH):
                            last = nc.vector.bn_stats(bn[:, b, c], X[:, b, c * CH:(c + 1) * CH])
                    link(last)
                    for b in range(B):
                        last = nc.vector.bn_aggr(cstat[:, b], bn[:, b])
                    link(last)
                    nc.vector.tensor_copy(dstat[:, 0], cstat[:, :, 0]).then_inc(gn_a, 1)
                    dve.wait_ge(gmean, 1)
                    link(nc.vector.tensor_copy(dstat[:, 1], taps_ps[:, 1, 0:B]))
                    link(nc.vector.tensor_tensor(dstat[:, 3], dstat[:, 0], dstat[:, 1], ALU.subtract))
                    link(nc.vector.tensor_tensor(dstat[:, 4], dstat[:, 3], dstat[:, 3], ALU.mult))
                    nc.vector.tensor_tensor(dstat[:, 2], dstat[:, 4], cstat[:, :, 1], ALU.add).then_inc(gn_b, 1)
                    dve.wait_ge(gvar, 1)
                    nc.vector.tensor_copy(dstat[:, 5], taps_ps[:, 2, 0:B]).then_inc(gn_b, 1)
                    dve.wait_ge(gstd, 1)
                    link(nc.vector.reciprocal(dstat[:, 2], dstat[:, 3]))
                    nc.vector.scalar_tensor_tensor(out=dstat[:, 4], in0=dstat[:, 1], scalar=-1.0, in1=dstat[:, 2],
                                                   op0=ALU.mult, op1=ALU.mult).then_inc(gnorm, 1)

                    def add_involution(g, b, c):
                        dve.wait_ge(summed, (g + 2) * SUMMED)
                        xv = X[:, b, bass.ts(c, CH)]
                        nc.vector.scalar_tensor_tensor(out=xv, in0=psI[:], scalar=span_m[:, 2:3], in1=xv, op0=ALU.mult,
                                                       op1=ALU.add).then_inc(x_added, 1)

                    def chunk(b, c, before):
                        g = b * NCH + c
                        for i in range(KS):
                            if i != 3:
                                dve.wait_ge(pool_added, g * ADDS + i + PROD_ROWS if i < 3 else
                                            (g + 1) * ADDS + max(i - PROD_ROWS, 1))
                            for j in range(KS):
                                t = i * KS + j
                                if t == ADD_AT and before:
                                    add_involution(*before)
                                if j == POOL_TAPS:
                                    dve.wait_ge(summed, g * SUMMED + (i + 1) * PE_TAPS)
                                dve.wait_ge(kern, g * TAPS + t + 1)
                                dst = prod[:, i % PROD_ROWS, j] if j < POOL_TAPS else direct[:, i, j - POOL_TAPS]
                                at = (c * ROWS + i * DIL) * PW + j * DIL
                                shifted = bass.AP(xpad, at, [[PW * PW, P], [PW, ROWS], [1, IMG]])
                                nc.vector.tensor_tensor(dst, taps_ps[:, j].rearrange("p (r w) -> p r w", w=IMG), shifted,
                                                        ALU.mult).then_inc(mul, 1)

                    for b in range(B):
                        for c in range(NCH):
                            dve.wait_ge(red_hi, b * NCH + c + 1)
                            low = red[2 * CR:3 * CR, c * CH:(c + 1) * CH]
                            nc.vector.scalar_tensor_tensor(out=low, in0=taps_ps[2 * CR:3 * CR, c % KS],
                                                           scalar=bred_n[2 * CR:3 * CR], in1=low, op0=ALU.add,
                                                           op1=ALU.subtract).then_inc(red_ready, 1)
                        dve.wait_ge(xpad_ready, b + 1)
                        chunk(b, 0, (b * NCH - 1, b - 1, NCH - 1) if b else None)
                        with dve.Fori(1, NCH, 1) as c:
                            chunk(b, c, (b * NCH + c - 1, b, c - 1))
                    add_involution(B * NCH - 1, B - 1, NCH - 1)

        SHARED = B * T
        shared = sb("shared", [P, SHARED])
        stN = ExitStack()
        XN = sb("XN", [P, B, 2 + T], on=stN)
        mean_col = sb("mean_col", [P, NCH, NCH], on=stN)
        spread = sb("spread", [NCH, NCH, P], on=stN)

        def layer_norm(name):
            st = ExitStack()
            with st:
                sq = shared[:, 0:2 * CH].rearrange("p (s c) -> p s c", s=2)
                var_sb = shared[0:NCH, 2 * CH:3 * CH]
                rstd = shared[0:NCH, 3 * CH:4 * CH]
                psM = ps(f"{name}_psM", [P, 3, CH], st)
                psV = ps(f"{name}_psV", [NCH, CH], st)
                psS = ps(f"{name}_psS", [P, 3, CH], st)
                mean_ready, centred, squared, summed = (sem(f"{name}_{s}") for s in ("mean", "centred", "squared", "summed"))
                rooted, inverted, spread_out, normed, pads = (sem(f"{name}_{s}") for s in ("rooted", "inverted", "spread", "normed", "pads"))

                with nc.Block() as block:
                    @block.gpsimd
                    def _(pool):
                        nc.gpsimd.memset(XN[:, :, 0:2], 0.0).then_inc(pads, 1)
                        nc.gpsimd.memset(mean_col[:], 0.0).then_inc(pads, 1)
                        nc.gpsimd.memset(spread[:], 0.0).then_inc(pads, 1)
                        pool.wait_ge(pads, 3)
                        nc.gpsimd.affine_select(out=mean_col[:], in_=mean_col[:], compare_op=ALU.not_equal,
                                                fill=1.0 / P, base=0, pattern=[[1, NCH], [-1, NCH]],
                                                channel_multiplier=0).then_inc(pads, 1)
                        nc.gpsimd.affine_select(out=spread[:], in_=spread[:], compare_op=ALU.not_equal, fill=1.0,
                                                base=0, pattern=[[-1, NCH], [0, P]], channel_multiplier=1).then_inc(pads, 1)

                    @block.tensor
                    def _(pe):
                        pe.sem_inc(summed, 1)
                        pe.wait_ge(pads, 5)
                        pe.sem_inc(spread_out, 1)
                        with pe.Fori(0, B, 1) as b:
                            def mean(c):
                                if c >= 3:
                                    pe.wait_ge(centred, 1 + b * NCH + c - 2)
                                else:
                                    pe.wait_ge(centred, 1 + b * NCH)
                                nc.tensor.matmul(psM[:, c % 3], averager[:], X[:, b, c * CH:(c + 1) * CH],
                                                 start=True, stop=True).then_inc(mean_ready, 1)

                            def var(c):
                                pe.wait_ge(squared, b * NCH + c + 1)
                                if c == 0:
                                    pe.wait_ge(rooted, 1 + b)
                                nc.tensor.matmul(psV[:], mean_col[:, c], sq[:, c % 2], start=(c == 0),
                                                 stop=(c == NCH - 1)).then_inc(summed, 1)

                            mean(0)
                            mean(1)
                            for c in range(NCH):
                                if c + 2 < NCH:
                                    mean(c + 2)
                                var(c)
                            pe.wait_ge(inverted, 1 + b + 1)
                            for c in range(NCH):
                                if c >= 3:
                                    pe.wait_ge(normed, 1 + b * NCH + c - 2)
                                else:
                                    pe.wait_ge(normed, 1 + b * NCH)
                                nc.tensor.matmul(psS[:, c % 3], spread[:, c], rstd, start=True,
                                                 stop=True).then_inc(spread_out, 1)

                    @block.scalar
                    def _(act):
                        act.sem_inc(rooted, 1)
                        with act.Fori(0, B, 1) as b:
                            for c in range(NCH):
                                act.wait_ge(centred, 1 + b * NCH + c + 1)
                                act.wait_ge(summed, 1 + b * NCH + max(c - 1, 0))
                                nc.scalar.activation(sq[:, c % 2], XN[:, b, 2 + c * CH:2 + (c + 1) * CH],
                                                     ACT.Square).then_inc(squared, 1)
                            act.wait_ge(summed, 1 + b * NCH + NCH)
                            act.wait_ge(inverted, 1 + b)
                            nc.scalar.activation(var_sb, psV[:], ACT.Sqrt, bias=eps_col[0:NCH]).then_inc(rooted, 1)

                    @block.vector
                    def _(dve):
                        dve.sem_inc(centred, 1)
                        dve.sem_inc(inverted, 1)
                        dve.sem_inc(normed, 1)
                        with dve.Fori(0, B, 1) as b:
                            for c in range(NCH):
                                dve.wait_ge(mean_ready, b * NCH + c + 1)
                                nc.vector.scalar_tensor_tensor(
                                    out=XN[:, b, 2 + c * CH:2 + (c + 1) * CH], in0=psM[:, c % 3], scalar=-1.0,
                                    in1=X[:, b, c * CH:(c + 1) * CH], op0=ALU.mult, op1=ALU.add).then_inc(centred, 1)
                            dve.wait_ge(rooted, 1 + b + 1)
                            dve.wait_ge(spread_out, 1 + b * NCH)
                            nc.vector.reciprocal(rstd, var_sb).then_inc(inverted, 1)
                            for c in range(NCH):
                                dve.wait_ge(spread_out, 1 + b * NCH + c + 1)
                                if c == 0:
                                    dve.wait_ge(squared, b * NCH + NCH)
                                v = XN[:, b, 2 + c * CH:2 + (c + 1) * CH]
                                nc.vector.tensor_tensor(v, psS[:, c % 3], v, ALU.mult).then_inc(normed, 1)

        layer_norm("ln1")

        st2 = ExitStack()
        with st2:
            used = [0]

            def carve(*dims):
                size = 1
                for d in dims:
                    size *= d
                a = used[0]
                used[0] += size
                assert used[0] <= SHARED
                names = "abcdef"[:len(dims)]
                spec = f"p ({' '.join(names)}) -> p {' '.join(names)}"
                return shared[:, a:a + size].rearrange(spec, **dict(zip(names, dims)))

            xs = carve(2, NW, 2, WIN)
            qs = carve(2, CH)
            ks = carve(2, CH)
            vs = carve(2, NW, P)
            pr = carve(2, NPAIR, HEADS, WIN)
            pT = carve(2, 2, NPAIR, P)
            at = carve(2, CH)
            keep_mask = carve(1, WIN)
            neg_mask = carve(1, WIN)
            red1 = sb("red1", [P, 2, 3, HEADS * NPAIR], on=st2)
            psS = ps("psS", [P, HEADS, CH], st2)
            psV = ps("psV", [P, 2, CH], st2)
            psO = ps("psO", [P, 2, CH], st2)

            chunk_in = sem("chunk_in")
            qk_mm = sem("qk_mm")
            q_out = sem("q_out")
            k_out = sem("k_out")
            v_mm = sem("v_mm")
            v_out = sem("v_out")
            v_zero = sem("v_zero")
            mask_fill = sem("mask_fill")
            s_mm = sem("s_mm")
            s_out = sem("s_out")
            masked = sem("masked")
            maxed = sem("maxed")
            shifted_ = sem("shifted_")
            exped = sem("exped")
            sumd = sem("sumd")
            recd = sem("recd")
            probs = sem("probs")
            pt_mm = sem("pt_mm")
            pt_out = sem("pt_out")
            o_mm = sem("o_mm")
            o_out = sem("o_out")
            y_mm = sem("y_mm")
            y_out = sem("y_out")

            ALL = B * NCH

            with nc.Block() as block:
                @block.gpsimd
                def _(pool):
                    nc.gpsimd.memset(keep_mask[:], 1.0).then_inc(mask_fill, 1)
                    nc.gpsimd.memset(neg_mask[:], 0.0).then_inc(mask_fill, 1)
                    pool.wait_ge(mask_fill, 2)
                    for w in range(2):
                        half = slice(w * WIN, (w + 1) * WIN)
                        for m, v in ((keep_mask, 0.0), (neg_mask, NEG)):
                            nc.gpsimd.affine_select(out=m[half], in_=m[half], compare_op=ALU.is_ge, fill=v, base=0,
                                                    pattern=[[0, 1], [-1, WIN]], channel_multiplier=1).then_inc(mask_fill, 1)
                    pool.wait_ge(mask_fill, 6)
                    nc.gpsimd.memset(vs[:], 0.0).then_inc(v_zero, 1)

                    def windows(c, s, b, at):
                        pool.wait_ge(v_mm, c + 1)
                        src = XN[:, b, bass.ds(2 + at * CH, CH)].rearrange("p (n a t) -> p n a t", a=1, t=WIN)
                        nc.gpsimd.tensor_copy(xs[:, s], src.to_broadcast([P, NW, 2, WIN])).then_inc(chunk_in, 1)

                    def mask_off(c, s):
                        pool.wait_ge(s_out, 2 + c + 1)
                        sc = pr[:, s].rearrange("p n h k -> p (n h) k")
                        nc.gpsimd.tensor_tensor(sc, sc, neg_mask.to_broadcast([P, NPAIR * HEADS, WIN]),
                                                ALU.add).then_inc(masked, 1)

                    def step(b, i, after_another):
                        c = (b * NCH // 2 + i) * 2
                        windows(c, 0, b, i * 2)
                        if after_another:
                            mask_off(c - 1, 1)
                        windows(c + 1, 1, b, i * 2 + 1)
                        mask_off(c, 0)

                    for b in range(B):
                        step(b, 0, b > 0)
                        with pool.Fori(1, NCH // 2, 1) as i:
                            step(b, i, True)
                    mask_off(ALL - 1, 1)

                @block.tensor
                def _(pe):
                    pe.sem_inc(v_mm, 2)

                    def queries_keys(c, s):
                        pe.wait_ge(chunk_in, c + 1)
                        pe.wait_ge(y_out, c + 1)
                        pe.wait_ge(o_out, c + 1)
                        nc.tensor.matmul(psO[:, 0], wqkvT[:, 0], xs[:, s, :, 0], start=True, stop=True)
                        nc.tensor.matmul(psO[:, 1], wqkvT[:, 1], xs[:, s, :, 0], start=True, stop=True).then_inc(qk_mm, 1)

                    def scores(c, s):
                        pe.wait_ge(q_out, c + 1)
                        pe.wait_ge(k_out, c + 1)
                        pe.wait_ge(s_out, c + 1)
                        for n in range(NPAIR):
                            for w in range(2):
                                for h in range(HEADS):
                                    tok = slice((2 * n + w) * WIN, (2 * n + w + 1) * WIN)
                                    hp = slice(h * HD, (h + 1) * HD)
                                    col = (s * NPAIR + n) * WIN
                                    last = nc.tensor.matmul(psS[w * WIN:(w + 1) * WIN, h, col:col + WIN],
                                                            qs[hp, s, tok], ks[hp, s, tok], start=True, stop=True)
                        last.then_inc(s_mm, 1)

                    def values(c, s):
                        pe.wait_ge(pt_out, 2 + c)
                        for w in range(NW):
                            both = xs[:, s, w].rearrange("p a t -> p (a t)")
                            last = nc.tensor.matmul(psV[:, w // 4, (w % 4) * P:(w % 4 + 1) * P], both,
                                                    wqkvT[:, 2], start=True, stop=True)
                        last.then_inc(v_mm, 1)

                    def heads(c, s):
                        pe.wait_ge(probs, c + 1)
                        pe.wait_ge(v_out, c + 1)
                        for a in range(2):
                            for n in range(NPAIR):
                                last = nc.tensor.transpose(psV[:, a, n * P:(n + 1) * P],
                                                           pr[:, s, n, 2 * a:2 * a + 2].rearrange("p h k -> p (h k)"), ident[:])
                        last.then_inc(pt_mm, 1)
                        pe.wait_ge(pt_out, 2 + c + 1)
                        for n in range(NPAIR):
                            for w in range(2):
                                for a in range(2):
                                    hp = slice(a * 2 * HD, (a + 1) * 2 * HD)
                                    tok = slice((2 * n + w) * WIN, (2 * n + w + 1) * WIN)
                                    last = nc.tensor.matmul(psO[hp, 1, tok], vs[:, s, 2 * n + w, hp],
                                                            pT[:, s, a, n, w * WIN:(w + 1) * WIN],
                                                            start=True, stop=True)
                        last.then_inc(o_mm, 1)

                    def project(c, s, queried):
                        pe.wait_ge(o_out, 2 + c + 1)
                        pe.wait_ge(q_out, queried)
                        nc.tensor.matmul(psO[:, 0], wprojT[:], at[:, s], start=True, stop=True).then_inc(y_mm, 1)

                    def step(c, after_another, before_another):
                        scores(c, 0)
                        if after_another:
                            heads(c - 1, 1)
                        values(c, 0)
                        queries_keys(c + 1, 1)
                        if after_another:
                            project(c - 1, 1, c + 2)
                        scores(c + 1, 1)
                        heads(c, 0)
                        values(c + 1, 1)
                        if before_another:
                            queries_keys(c + 2, 0)
                        project(c, 0, c + 3 if before_another else c + 2)

                    queries_keys(0, 0)
                    step(0, False, True)
                    with pe.Fori(1, ALL // 2 - 1, 1) as i:
                        step(2 * i, True, True)
                    step(ALL - 2, True, False)
                    heads(ALL - 1, 1)
                    project(ALL - 1, 1, ALL)

                @block.scalar
                def _(act):
                    act.sem_inc(pt_out, 2)
                    act.sem_inc(o_out, 2)
                    act.wait_ge(v_zero, 1)

                    def queries_out(c, s):
                        act.wait_ge(qk_mm, c + 1)
                        nc.scalar.activation(qs[:, s], psO[:, 0], ACT.Copy, scale=HD ** -0.5).then_inc(q_out, 1)

                    def values_out(c, s):
                        act.wait_ge(v_mm, 2 + c + 1)
                        for j in range(2):
                            half = slice(j * WIN, (j + 1) * WIN)
                            dst = vs[half, s].rearrange("p w (a j c) -> p (w a) j c", a=2, j=2)[:, :, j]
                            src = psV[half].rearrange("p b (w a j c) -> p (b w a) j c", a=2, j=2, c=HD)[:, :, j]
                            last = nc.scalar.activation(dst, src, ACT.Copy)
                        last.then_inc(v_out, 1)

                    def exponentials(c, s):
                        act.wait_ge(shifted_, c + 1)
                        nc.scalar.activation(pr[:, s], pr[:, s], ACT.Exp).then_inc(exped, 1)

                    def heads_out(c, s):
                        act.wait_ge(pt_mm, c + 1)
                        nc.scalar.activation(pT[:, s].rearrange("p a n q -> p a (n q)"), psV[:], ACT.Copy).then_inc(pt_out, 1)
                        act.wait_ge(o_mm, c + 1)
                        nc.scalar.activation(at[:, s], psO[:, 1], ACT.Copy).then_inc(o_out, 1)

                    def step(c, after_another, before_another):
                        if after_another:
                            exponentials(c - 1, 1)
                            heads_out(c - 1, 1)
                        values_out(c, 0)
                        queries_out(c + 1, 1)
                        exponentials(c, 0)
                        heads_out(c, 0)
                        values_out(c + 1, 1)
                        if before_another:
                            queries_out(c + 2, 0)

                    queries_out(0, 0)
                    step(0, False, True)
                    with act.Fori(1, ALL // 2 - 1, 1) as i:
                        step(2 * i, True, True)
                    step(ALL - 2, True, False)
                    exponentials(ALL - 1, 1)
                    heads_out(ALL - 1, 1)

                @block.vector
                def _(dve):
                    dve.sem_inc(y_out, 3)
                    dve.sem_inc(s_out, 2)
                    dve.wait_ge(mask_fill, 6)
                    rows = [pr[:, s].rearrange("p n h k -> p (n h) k") for s in range(2)]

                    def spread_row(v):
                        return v.rearrange("p (m a) -> p m a", a=1).to_broadcast([P, HEADS * NPAIR, WIN])

                    def keys_out(c, s):
                        dve.wait_ge(qk_mm, c + 1)
                        nc.vector.tensor_copy(ks[:, s], psO[:, 1]).then_inc(k_out, 1)

                    def mask(c, s):
                        dve.wait_ge(s_mm, c + 1)
                        src = psS[:, :, s * NPAIR * WIN:(s + 1) * NPAIR * WIN].rearrange("p h (n k) -> p h n k", k=WIN)
                        keep = keep_mask.rearrange("p (a b) k -> p a b k", a=1).to_broadcast([P, HEADS, NPAIR, WIN])
                        nc.vector.tensor_tensor(pr[:, s].rearrange("p n h k -> p h n k"), src, keep,
                                                ALU.mult).then_inc(s_out, 1)

                    def find_maxima(c, s):
                        dve.wait_ge(masked, c + 1)
                        nc.vector.tensor_reduce(red1[:, s, 0], rows[s], AX.X, ALU.max).then_inc(maxed, 1)

                    def shift(c, s):
                        dve.wait_ge(maxed, c + 1)
                        nc.vector.tensor_tensor(rows[s], rows[s], spread_row(red1[:, s, 0]),
                                                ALU.subtract).then_inc(shifted_, 1)

                    def normalise(c, s):
                        dve.wait_ge(exped, c + 1)
                        nc.vector.tensor_reduce(red1[:, s, 1], rows[s], AX.X, ALU.add).then_inc(sumd, 1)
                        dve.wait_ge(sumd, c + 1)
                        nc.vector.reciprocal(red1[:, s, 2], red1[:, s, 1]).then_inc(recd, 1)
                        dve.wait_ge(recd, c + 1)
                        nc.vector.tensor_tensor(rows[s], rows[s], spread_row(red1[:, s, 2]),
                                                ALU.mult).then_inc(probs, 1)

                    def add_projection(c, b, at_chunk):
                        dve.wait_ge(y_mm, c + 1)
                        xv = X[:, b, bass.ts(at_chunk, CH)]
                        nc.vector.scalar_tensor_tensor(out=xv, in0=psO[:, 0], scalar=bproj[:], in1=xv,
                                                       op0=ALU.add, op1=ALU.add).then_inc(y_out, 1)

                    def step(b, i, before):
                        c = (b * NCH // 2 + i) * 2
                        keys_out(c, 0)
                        if before:
                            add_projection(c - 2, *before)
                            normalise(c - 1, 1)
                        mask(c, 0)
                        find_maxima(c, 0)
                        shift(c, 0)
                        keys_out(c + 1, 1)
                        if before:
                            add_projection(c - 1, before[0], before[1] + 1)
                        normalise(c, 0)
                        mask(c + 1, 1)
                        find_maxima(c + 1, 1)
                        shift(c + 1, 1)

                    for b in range(B):
                        step(b, 0, (b - 1, NCH - 2) if b else None)
                        with dve.Fori(1, NCH // 2, 1) as i:
                            step(b, i, (b, i * 2 - 2))
                    add_projection(ALL - 2, B - 1, NCH - 2)
                    normalise(ALL - 1, 1)
                    add_projection(ALL - 1, B - 1, NCH - 1)

        layer_norm("ln2")

        U = shared[:].bitcast(F16).rearrange("p (b q n h c) -> p b q n h c", b=B, q=2, n=NBLK, h=2)
        SEGS = []
        for A in range(NGRP):
            cuts = sorted({0, CH} | {HALF // 2 ** e - A * CH for e in range(NE) if 0 < HALF // 2 ** e - A * CH < CH})
            SEGS.append([(c0, c1, sum(HALF // 2 ** e > A * CH + c0 for e in range(NE))) for c0, c1 in zip(cuts, cuts[1:])])

        st3 = ExitStack()
        with st3:
            mu = sb("mu", [P, NE, AR, P], on=st3)
            psA = ps("psA3", [P, 3, CH], st3)
            psU = ps("psU3", [P, 3, 4, P], st3)
            mu_in = sem("mu_in")
            mu_ready = sem("mu_ready")
            ar_mm = sem("ar_mm")
            ar_out = sem("ar_out")
            ut_mm = sem("ut_mm")
            u_hi = sem("u_hi")
            u_lo = sem("u_lo")
            AG = 2 * NGRP
            UG = 2 * NBLK // 4

            with nc.Block() as block:
                @block.sync
                def _(sp):
                    sp.dma_start(mu[:], m_u.rearrange("i a d e -> d i a e")).then_inc(mu_in, 16)
                    sp.wait_ge(mu_in, 16)

                @block.tensor
                def _(pe):
                    pe.wait_ge(mu_ready, NE)
                    for b in range(B):
                        for t in range(AG):
                            par, A = t // NGRP, t % NGRP
                            pe.wait_ge(ar_out, b * AG + (t - 2 if t >= 3 else 0))
                            for si, (c0, c1, ne) in enumerate(SEGS[A]):
                                for a in range(AR):
                                    lo = 2 + 2 * (A * CH + c0) + par - a
                                    last = nc.tensor.matmul(psA[:, t % 3, c0:c1], mu[:, ne - 1, a],
                                                            XN[:, b, lo:lo + 2 * (c1 - c0) - 1:2],
                                                            start=(a == 0), stop=(a == AR - 1))
                            last.then_inc(ar_mm, 1)
                            for r in (2 * t, 2 * t + 1) if UG == 2 * AG else (t,):
                                pe.wait_ge(u_lo, b * UG + (r - 2 if r >= 3 else 0))
                                for j in range(4):
                                    rp, rb = (4 * r + j) // NBLK, (4 * r + j) % NBLK
                                    first = 2 + rp + 2 * P * rb
                                    last = nc.tensor.transpose(psU[:, r % 3, j], XN[:, b, first:first + 2 * P - 1:2], ident[:])
                                last.then_inc(ut_mm, 1)

                @block.scalar
                def _(act):
                    for b in range(B):
                        for r in range(UG):
                            rp, rb = 4 * r // NBLK, 4 * r % NBLK
                            act.wait_ge(ut_mm, b * UG + r + 1)
                            nc.scalar.activation(U[:, b, rp, rb:rb + 4, 0], psU[:, r % 3], ACT.Copy,
                                                 scale=U_SCALE).then_inc(u_hi, 1)

                @block.vector
                def _(dve):
                    dve.wait_ge(mu_in, 16)
                    nc.vector.tensor_scalar(mu[:, 0], mu[:, 0], gate[:, 0:1], None, ALU.mult).then_inc(mu_ready, 1)
                    for e in range(1, NE):
                        dve.wait_ge(mu_ready, e)
                        nc.vector.scalar_tensor_tensor(out=mu[:, e], in0=mu[:, e], scalar=gate[:, e:e + 1],
                                                       in1=mu[:, e - 1], op0=ALU.mult, op1=ALU.add).then_inc(mu_ready, 1)
                    for b in range(B):
                        for t in range(AG):
                            par, A = t // NGRP, t % NGRP
                            dve.wait_ge(ar_mm, b * AG + t + 1)
                            lo = 2 * A * CH + par
                            xv = X[:, b, lo:lo + 2 * CH - 1:2]
                            nc.vector.tensor_tensor(xv, psA[:, t % 3], xv, ALU.add).then_inc(ar_out, 1)
                            for r in (2 * t, 2 * t + 1) if UG == 2 * AG else (t,):
                                rp, rb = 4 * r // NBLK, 4 * r % NBLK
                                dve.wait_ge(u_hi, b * UG + r + 1)
                                nc.vector.scalar_tensor_tensor(out=U[:, b, rp, rb:rb + 4, 1], in0=psU[:, r % 3],
                                                               scalar=U_SCALE, in1=U[:, b, rp, rb:rb + 4, 0],
                                                               op0=ALU.mult, op1=ALU.subtract).then_inc(u_lo, 1)

        stN.close()

        st4 = ExitStack()
        with st4:
            SF = sb("SF", [P, 2, 2, F_W], F16, on=st4)
            SG = sb("SG", [P, 2, 2, G_W], F16, on=st4)
            SH = sb("SH", [P, 2, 4, H_W], F16, on=st4)
            HB = HC // P
            V = sb("V", [P, 2, 2, 6 * HB, 2, P], F16, on=st4)
            VD_AT = 3 * HB
            D_AT = 4 * HB
            m_raw = sb("m_raw", [P, 2, NE, P], on=st4)
            mt = sb("mt", [P, 2, NE, P], on=st4)
            mk = sb("mk", [P, NE], on=st4)
            conv_sb = sb("conv_sb", [P, 2, CH], on=st4)
            w_sb = weights[:, 0:4].rearrange("p (s a) c -> p s (a c)", s=2)
            d_sb = weights[:, 4:8].rearrange("p a c -> p (a c)")
            psC = ps("psC", [P, 4, CH], st4)
            psW = ps("psW", [P, 2, CH], st4)
            psY = ps("psY", [P, 2, CH], st4)

            f_in = [sem("f_in0"), sem("f_in1")]
            m_in = sem("m_in")
            v_step = sem("v_step")
            v_step_pool = sem("v_step_pool")
            v_ready = sem("v_ready")
            v_ready_pool = sem("v_ready_pool")
            mk_ready = sem("mk_ready")
            msum_ready = sem("msum_ready")
            mt_step = sem("mt_step")
            c_mm = sem("c_mm")
            w_mm = sem("w_mm")
            w_out = sem("w_out")
            c_out_act = sem("c_out_act")
            c_out_dve = sem("c_out_dve")
            d_used = sem("d_used")
            m_mm = sem("m_mm")
            y_added = sem("y_added")
            stored = sem("stored")
            PASSES = B // 2
            GROUPS = 4
            KINDS = 5
            CHUNK = (0, 1, None, 2, 3)
            BANK = (0, 1, 2, 3, 1)
            UNITS = GROUPS * KINDS
            WS = GROUPS * (KINDS - 1)
            MIX = GROUPS * NGRP
            AHEAD = 3
            UNIT = [(n // (2 * KINDS), n // KINDS % 2, n % KINDS) for n in range(UNITS)]
            MIXED = [n for n in range(UNITS) if CHUNK[n % KINDS] is not None]
            V_TMP = (NGRP - 1) * HC

            def w_no(n):
                return n // KINDS * (KINDS - 1) + max(n % KINDS - 1, 0)

            def differences(eng, ops, p, par, tmp, step, ready):
                n = p * STEPS
                for slot in range(2):
                    u = U[:, 2 * p + slot, par]
                    v = V[:, slot, par].rearrange("p n h c -> p h n c")
                    pairs = u[:, 0:NBLK - 4].rearrange("p (g a i) h c -> p a h g i c", a=2, i=HB)
                    chunks = u[:, 0:8].rearrange("p (a n) h c -> p a h n c", a=2)
                    half = tmp[:, 0:V_TMP].rearrange("p (g i c) -> p g i c", g=NGRP - 1, i=HB)
                    whole = tmp[:, 0:CH].rearrange("p (n c) -> p n c", c=P)
                    both = tmp[:, CH:CH + HC].rearrange("p (n c) -> p n c", c=P)
                    v_half = v[:, :, 0:VD_AT].rearrange("p h (g i) c -> p h g i c", i=HB)
                    for out, in0, in1, op in (
                            (half, pairs[:, 0, 0], pairs[:, 1, 0], ALU.subtract),
                            (half, half, pairs[:, 0, 1], ALU.add),
                            (half, half, pairs[:, 1, 1], ALU.subtract),
                            (v_half[:, 0], half, None, None),
                            (v_half[:, 1], half, v_half[:, 0], ALU.subtract),
                            (whole, chunks[:, 0, 0], chunks[:, 1, 0], ALU.subtract),
                            (whole, whole, chunks[:, 0, 1], ALU.add),
                            (whole, whole, chunks[:, 1, 1], ALU.subtract),
                            (v[:, 0, D_AT:], whole, None, None),
                            (v[:, 1, D_AT:], whole, v[:, 0, D_AT:], ALU.subtract),
                            (both, whole[:, 0:HB], whole[:, HB:], ALU.subtract),
                            (v[:, 0, VD_AT:D_AT], both, None, None),
                            (v[:, 1, VD_AT:D_AT], both, v[:, 0, VD_AT:D_AT], ALU.subtract)):
                        if in1 is None:
                            last = ops.tensor_copy(out, in0)
                        else:
                            last = ops.tensor_tensor(out, in0, in1, op)
                        n += 1
                        last.then_inc(step, 1)
                        eng.wait_ge(step, n)
                    eng.sem_inc(ready, 1)

            STEPS = 2 * 13

            with nc.Block() as block:
                @block.gpsimd
                def _(pool):
                    def load_lines(q, k):
                        at = (2 * k + q) * (8 * LINE)
                        pool.dma_start(SF[:, q], bass.AP(lines.tensor, at + F_FROM, [[1, P], [LINE, 2], [1, F_W]])).then_inc(f_in[q], 16)
                        pool.dma_start(SG[:, q], bass.AP(lines.tensor, at + 2 * LINE + G_FROM, [[1, P], [LINE, 2], [1, G_W]])).then_inc(f_in[q], 16)
                        pool.dma_start(SH[:, q], bass.AP(lines.tensor, at + 4 * LINE, [[1, P], [LINE, 4], [1, H_W]])).then_inc(f_in[q], 16)

                    def load_matrices(k):
                        for sign, m in enumerate((m_plus, m_minus)):
                            pool.dma_start(m_raw[:, sign], bass.AP(m.tensor, k * (P * P), [[P, P], [NK * P * P, NE], [1, P]])).then_inc(m_in, 16)

                    def reload(done, k):
                        pool.wait_ge(c_mm, (2 * done - 1) * UNITS)
                        load_lines(0, k)
                        pool.wait_ge(msum_ready, 2 * done)
                        load_matrices(k)
                        pool.wait_ge(c_mm, 2 * done * UNITS)
                        load_lines(1, k)

                    load_lines(0, 0)
                    load_matrices(0)
                    load_lines(1, 0)
                    for p in range(PASSES):
                        if p:
                            reload(p * NK, 0)
                            pool.wait_ge(y_added, 2 + 2 * p * NK * MIX)
                        differences(pool, nc.gpsimd, p, 1, mt[:].rearrange("p q e c -> p (q e c)"),
                                    v_step_pool, v_ready_pool)
                        with pool.Fori(1, NK, 1) as k:
                            reload(p * NK + k, k)

                @block.sync
                def _(sp):
                    for p in range(PASSES):
                        sp.wait_ge(y_added, 2 + 2 * (p + 1) * NK * MIX)
                        for b in (2 * p, 2 * p + 1):
                            sp.dma_start(out_v[:, b], X[:, b]).then_inc(stored, 16)
                    sp.wait_ge(stored, 16 * B)

                @block.tensor
                def _(pe):
                    pe.sem_inc(m_mm, 2)

                    def phase(p, k, q):
                        f = 2 * (p * NK + k) + q

                        def triple(out, blocks, line, y, width, first, final):
                            skewed, high, z_from = line
                            z = HALF - y - z_from
                            stop = z - width
                            for ul, fl in ((0, 0), (1, 0), (0, 1)):
                                last = nc.tensor.matmul(out, blocks[:, ul],
                                                        skewed[:, q, high + fl, z:(stop if stop >= 0 else None):-1],
                                                        start=(first and ul == 0 and fl == 0), stop=(final and fl == 1),
                                                        skip_group_check=True)
                            return last

                        f_line, g_line = (SF, 0, F_FROM), (SG, 0, G_FROM)
                        h_line, k_line = (SH, 0, 0), (SH, 2, 0)

                        def conv(n):
                            slot, par, kind = UNIT[n]
                            A = CHUNK[kind]
                            bank = psC[:, BANK[kind]]
                            src = par ^ q
                            shift = 0 if (q == 1 and par == 0) else 1
                            u = U[:, 2 * p + slot, src]
                            v = V[:, slot, src]
                            shares = [(u[:, 4 * a:4 * a + 4], v[:, HB * a:HB * (a + 1)], ln, d) for a, ln, d in (
                                (), ((0, (f_line, g_line), 1),), (), ((1, (h_line, k_line), 2),),
                                ((2, (f_line, g_line), 1), (0, (h_line, k_line), 3)))[kind]]
                            if A is None:
                                shares = [(v[:, D_AT:], v[:, VD_AT:D_AT], (f_line, g_line), 2)]
                            if shares:
                                pe.wait_ge(w_out, f * WS + w_no(n) + 1)
                                for x, (_, v_blocks, ln, d) in enumerate(shares):
                                    for i in range(HB):
                                        last = triple(psW[:, w_no(n) % 2, 0:HC], v_blocks[:, i], ln[0],
                                                      shift + d * CH - i * P, HC, x == 0 and i == 0,
                                                      x == len(shares) - 1 and i == HB - 1)
                                last.then_inc(w_mm, 1)
                            if kind == 0:
                                pe.wait_ge(c_out_act, 1 + f * GROUPS + n // KINDS)
                            else:
                                pe.wait_ge(c_out_dve, AHEAD + f * WS + n // KINDS * (KINDS - 1) + (0, 0, -2, -1, 1)[kind])
                            if A is not None:
                                for i in range(4):
                                    last = triple(bank[:, i * P:], u[:, 4 * A + i], f_line, shift, CH - i * P, i == 0, i == 3)
                            for x, (blocks, _, ln, d) in enumerate(shares):
                                for i in range(HB):
                                    triple(bank[:, 0:HC], blocks[:, HB + i], ln[1],
                                           shift + d * CH - i * P, HC, A is None and i == 0, False)
                                    last = triple(bank[:, HC:], blocks[:, i], ln[1],
                                                  shift + d * CH + HC - i * P, HC, False, True)
                            last.then_inc(c_mm, 1)

                        def mixdown(m):
                            n = MIXED[m]
                            A = CHUNK[UNIT[n][2]]
                            if A:
                                pe.wait_ge(c_out_dve, AHEAD + f * WS + w_no(n) + 1)
                            else:
                                pe.wait_ge(c_out_act, 1 + f * GROUPS + n // KINDS + 1)
                            pe.wait_ge(y_added, f * MIX + m + 1)
                            for si, (c0, c1, ne) in enumerate(SEGS[A]):
                                last = nc.tensor.matmul(psY[:, m % 2, c0:c1], mt[:, q, ne - 1],
                                                        conv_sb[:, m % 2, c0:c1], start=(si == 0),
                                                        stop=True, skip_group_check=True)
                            last.then_inc(m_mm, 1)

                        pe.wait_ge(f_in[q], 48 * (p * NK + k) + 48)
                        pe.wait_ge(v_ready, 2 * p + 1)
                        pe.wait_ge(v_ready_pool, 2 * p + 1)
                        conv(0)
                        conv(1)
                        pe.wait_ge(mt_step, 1 + f * NE + NE)
                        for n in range(2, UNITS):
                            if n - 2 in MIXED:
                                mixdown(MIXED.index(n - 2))
                            if n == UNITS // 2:
                                pe.wait_ge(v_ready, 2 * p + 2)
                                pe.wait_ge(v_ready_pool, 2 * p + 2)
                            conv(n)
                        mixdown(MIX - 2)
                        mixdown(MIX - 1)

                    for p in range(PASSES):
                        with pe.Fori(0, NK, 1) as k:
                            phase(p, k, 0)
                            phase(p, k, 1)

                @block.scalar
                def _(act):
                    act.sem_inc(c_out_act, 1)
                    act.sem_inc(w_out, 2)
                    for p in range(PASSES):
                        act.wait_ge(v_ready, 2 * p + 2)
                        with act.Fori(0, NK, 1) as k:
                            for q in range(2):
                                f = 2 * (p * NK + k) + q
                                for n in range(UNITS):
                                    if n % KINDS == 0:
                                        m = MIXED.index(n)
                                        act.wait_ge(c_mm, f * UNITS + n + 1)
                                        act.wait_ge(m_mm, f * MIX + m + 1)
                                        nc.scalar.activation(conv_sb[:, m % 2], psC[:, BANK[0]], ACT.Copy).then_inc(c_out_act, 1)
                                    else:
                                        act.wait_ge(w_mm, f * WS + w_no(n) + 1)
                                        act.wait_ge(c_out_dve, AHEAD + f * WS + max(w_no(n) - 1, 0))
                                        nc.scalar.activation(w_sb[:, w_no(n) % 2], psW[:, w_no(n) % 2, 0:HC],
                                                             ACT.Copy).then_inc(w_out, 1)

                @block.vector
                def _(dve):
                    dve.sem_inc(c_out_dve, AHEAD)
                    dve.sem_inc(y_added, 2)
                    dve.sem_inc(mt_step, 1)

                    def phase(p, k, q):
                        f = 2 * (p * NK + k) + q

                        def mix_matrices():
                            dve.wait_ge(m_in, 32 * (p * NK + k) + 32)
                            dve.wait_ge(mt_step, 1 + f * NE)
                            nc.vector.tensor_scalar(mk[:], mix[:, :, bass.ds(k, 1)].rearrange("p e a -> p (e a)"), 1.0, None,
                                                    ALU.mult).then_inc(mk_ready, 1)
                            nc.vector.tensor_tensor(mt[:, q], m_raw[:, 0], m_raw[:, 1],
                                                    ALU.subtract if q else ALU.add).then_inc(msum_ready, 1)
                            dve.wait_ge(mk_ready, f + 1)
                            dve.wait_ge(msum_ready, f + 1)
                            nc.vector.tensor_scalar(mt[:, q, 0], mt[:, q, 0], mk[:, 0:1], None, ALU.mult).then_inc(mt_step, 1)
                            for e in range(1, NE):
                                dve.wait_ge(mt_step, 1 + f * NE + e)
                                nc.vector.scalar_tensor_tensor(out=mt[:, q, e], in0=mt[:, q, e], scalar=mk[:, e:e + 1],
                                                               in1=mt[:, q, e - 1], op0=ALU.mult, op1=ALU.add).then_inc(mt_step, 1)

                        def combine(n):
                            kind = n % KINDS
                            dve.wait_ge(c_mm, f * UNITS + n + 1)
                            dve.wait_ge(w_out, 2 + f * WS + w_no(n) + 1)
                            dve.wait_ge(c_out_dve, AHEAD + f * WS + w_no(n))
                            w = w_sb[:, w_no(n) % 2]
                            bank = psC[:, BANK[kind]]
                            if CHUNK[kind] is None:
                                dst = d_sb
                            else:
                                m = MIXED.index(n)
                                dst = conv_sb[:, m % 2]
                                dve.wait_ge(m_mm, f * MIX + m + 1)
                            if kind >= 3:
                                nc.vector.tensor_tensor(dst, bank, d_sb, ALU.add if kind == 3 else ALU.subtract).then_inc(d_used, 1)
                                dve.wait_ge(d_used, 2 * (f * GROUPS + n // KINDS) + kind - 2)
                                bank = dst
                            nc.vector.tensor_tensor(dst[:, 0:HC], bank[:, 0:HC], w, ALU.add)
                            nc.vector.tensor_tensor(dst[:, HC:], bank[:, HC:], w, ALU.subtract).then_inc(c_out_dve, 1)

                        def add(m):
                            slot, par, kind = UNIT[MIXED[m]]
                            dve.wait_ge(m_mm, 2 + f * MIX + m + 1)
                            lo = 2 * CHUNK[kind] * CH + par
                            xv = X[:, 2 * p + slot, lo:lo + 2 * CH - 1:2]
                            nc.vector.tensor_tensor(xv, psY[:, m % 2], xv, ALU.add).then_inc(y_added, 1)

                        mix_matrices()
                        for n in range(UNITS):
                            if n % KINDS:
                                combine(n)
                            if n - 2 in MIXED:
                                add(MIXED.index(n - 2))
                        add(MIX - 2)
                        add(MIX - 1)

                    for p in range(PASSES):
                        if p:
                            dve.wait_ge(y_added, 2 + 2 * p * NK * MIX)
                        differences(dve, nc.vector, p, 0, conv_sb[:].rearrange("p a c -> p (a c)"), v_step, v_ready)
                        dve.wait_ge(v_ready_pool, 2 * p + 2)
                        with dve.Fori(0, NK, 1) as k:
                            phase(p, k, 0)
                            phase(p, k, 1)



_INS = ['x', 'L0_conv_w_reduce', 'L0_conv_b_reduce', 'L0_conv_w_span', 'L0_conv_b_span', 'L1_attn_w_qkv',
        'L1_attn_w_proj', 'L1_attn_b_proj', 'L1_ffn_sigma', 'L1_ffn_phi', 'L1_ffn_M_u', 'L1_ffn_M_phi_plus',
        'L1_ffn_M_phi_minus', 'L1_ffn_log_weights', 'L1_ffn_gumbel']


def kernel(**inputs):
    import numpy as np
    import concourse.bacc as bacc
    from concourse.bass_utils import run_bass_kernel_spmd

    nc = bacc.Bacc("TRN2", target_bir_lowering=False, num_devices=1)
    arrays, args = {}, []
    for name in _INS:
        a = np.ascontiguousarray(inputs[name])
        arrays[f"in_{name}"] = a
        args.append(nc.dram_tensor(f"in_{name}", a.shape, mybir.dt.from_np(a.dtype), kind="ExternalInput").ap())
    out = nc.dram_tensor("out_x", inputs["x"].shape, F32, kind="ExternalOutput").ap()
    program(nc, *args, out)
    r = run_bass_kernel_spmd(nc, [arrays], core_ids=[0])
    return r.results[0]["out_x"]
```
